# Optimizing a Trainium2 kernel written in Bass

```python
import numpy as np
import jax
import jax.numpy as jnp

def _softmax(x, axis=-1):
    return jax.nn.softmax(x, axis=axis)

def _gelu(x):
    return jax.nn.gelu(x, approximate=True)

def _silu(x):
    return jax.nn.silu(x)

def _sigmoid(x):
    return jax.nn.sigmoid(x)

def _layernorm(x, axis=-1, eps=1e-05):
    m = jnp.mean(x, axis=axis, keepdims=True)
    v = jnp.var(x, axis=axis, keepdims=True)
    return (x - m) / jnp.sqrt(v + eps)

def _scatter_add(tgt, idx, src, axis=0):
    return tgt.at[idx].add(src)

def _segment_sum(src, seg, n):
    return jax.ops.segment_sum(src, seg, n)
kernel_name = 'mk_macaron_d2_jaxref_r8_985ae6'

def setup_inputs(seed: int=0):
    np.random.seed(seed)
    _w = jnp.asarray

    def _L0_attn_setup():
        import jax, jax.numpy as jnp
        import numpy as np
        HEADS = 16
        key = jax.random.key(seed)
        ks = jax.random.split(key, 5)
        B, T, D = (2, 256, 256)
        s = 0.02
        return {'x': jax.random.normal(ks[0], (B, T, D), dtype=jnp.float32), 'Wq': jax.random.normal(ks[1], (D, D), dtype=jnp.float32) * s, 'Wk': jax.random.normal(ks[2], (D, D), dtype=jnp.float32) * s, 'Wv': jax.random.normal(ks[3], (D, D), dtype=jnp.float32) * s, 'Wo': jax.random.normal(ks[4], (D, D), dtype=jnp.float32) * s}
    _L0_attn_in = _L0_attn_setup()

    def _L0_ffn_setup():
        import jax, jax.numpy as jnp
        import numpy as np
        N_EXPERTS = 8
        TOP_K = 2
        C = 256
        H = 128
        HS = 256
        B, T = (1, 64)
        SCALE = 0.02
        key = jax.random.key(seed)
        ks = jax.random.split(key, 10)
        x = jax.random.normal(ks[0], (B, T, C), dtype=jnp.float32)
        gate_w = jax.random.normal(ks[1], (N_EXPERTS, C), dtype=jnp.float32) * SCALE
        w_gate = jax.random.normal(ks[2], (N_EXPERTS, H, C), dtype=jnp.float32) * SCALE
        w_up = jax.random.normal(ks[3], (N_EXPERTS, H, C), dtype=jnp.float32) * SCALE
        w_down = jax.random.normal(ks[4], (N_EXPERTS, C, H), dtype=jnp.float32) * SCALE
        sh_gate = jax.random.normal(ks[5], (HS, C), dtype=jnp.float32) * SCALE
        sh_up = jax.random.normal(ks[6], (HS, C), dtype=jnp.float32) * SCALE
        sh_down = jax.random.normal(ks[7], (C, HS), dtype=jnp.float32) * SCALE
        se_gate_w = jax.random.normal(ks[8], (1, C), dtype=jnp.float32) * SCALE
        return {'x': x, 'gate_w': gate_w, 'w_gate': w_gate, 'w_up': w_up, 'w_down': w_down, 'sh_gate': sh_gate, 'sh_up': sh_up, 'sh_down': sh_down, 'se_gate_w': se_gate_w}
    _L0_ffn_in = _L0_ffn_setup()

    def _L1_attn_setup():
        import jax, jax.numpy as jnp
        import numpy as np
        D_INNER = 256
        DT_RANK = 64
        D_STATE = 16
        BATCH = 2
        SEQLEN = 256
        key = jax.random.key(seed)
        k0, k1, k2, k3 = jax.random.split(key, 4)
        x = jax.random.normal(k0, (BATCH, SEQLEN, D_INNER), dtype=jnp.float32)
        x_proj_w = jax.random.normal(k1, (DT_RANK + 2 * D_STATE, D_INNER), dtype=jnp.float32) / np.float32(np.sqrt(D_INNER))
        dt_proj_w = jax.random.normal(k2, (D_INNER, DT_RANK), dtype=jnp.float32) / np.float32(np.sqrt(DT_RANK))
        dt_proj_b = jax.random.normal(k3, (D_INNER,), dtype=jnp.float32) * 0.01
        A_log = jnp.log(jnp.broadcast_to(jnp.arange(1, D_STATE + 1, dtype=jnp.float32), (D_INNER, D_STATE)))
        D = jnp.ones((D_INNER,), dtype=jnp.float32)
        return {'x': x, 'x_proj_w': x_proj_w, 'dt_proj_w': dt_proj_w, 'dt_proj_b': dt_proj_b, 'A_log': A_log, 'D': D}
    _L1_attn_in = _L1_attn_setup()

    def _L1_ffn_setup():
        import jax, jax.numpy as jnp
        import numpy as np
        COST_LAMBDA = 1e-07
        HID = [128, 256, 384, 512, 128, 256, 384, 512]
        TOP_K = 2

        def _gelu(v):
            return jax.nn.gelu(v, approximate=False)

        def _forward(x, down_w, down_b, up_w, up_b, router_w, router_b, shared_w1, shared_b1, shared_w2, shared_b2, core_w, core_b, expert_params):
            E = len(expert_params)
            h = x @ down_w + down_b
            cost = jnp.array([w1.shape[0] * w1.shape[1] + w2.shape[0] * w2.shape[1] for w1, _, w2, _ in expert_params], jnp.float32)
            logits = x @ router_w + router_b - COST_LAMBDA * cost
            probs = jax.nn.softmax(logits, axis=-1)
            topv, topi = jax.lax.top_k(probs, TOP_K)
            gate = jax.nn.softmax(topv, axis=-1)
            out = jnp.zeros_like(h)
            for k in range(TOP_K):
                mask = jax.nn.one_hot(topi[..., k], E, dtype=h.dtype)
                acc = jnp.zeros_like(h)
                for e, (w1, b1, w2, b2) in enumerate(expert_params):
                    hm = h * mask[..., e:e + 1]
                    acc = acc + (_gelu(_gelu(hm) @ w1 + b1) @ w2 + b2)
                out = out + acc * gate[..., k:k + 1]
            out = out + 0.1 * (_gelu(_gelu(h) @ shared_w1 + shared_b1) @ shared_w2 + shared_b2)
            out = out @ up_w + up_b
            out = out + (_gelu(x) @ core_w + core_b)
            return out
        key = jax.random.key(seed)
        ks = iter(jax.random.split(key, 80))

        def W(shape):
            return jax.random.normal(next(ks), shape, jnp.float32) * 0.02
        B, T, D, L = (4, 256, 256, 128)
        inp = {'x': jax.random.normal(next(ks), (B, T, D), jnp.float32)}
        inp['down_w'] = W((D, L))
        inp['down_b'] = jnp.zeros((L,), jnp.float32)
        inp['up_w'] = W((L, D))
        inp['up_b'] = jnp.zeros((D,), jnp.float32)
        inp['router_w'] = W((D, len(HID)))
        inp['router_b'] = jnp.zeros((len(HID),), jnp.float32)
        inp['shared_w1'] = W((L, L))
        inp['shared_b1'] = jnp.zeros((L,), jnp.float32)
        inp['shared_w2'] = W((L, L))
        inp['shared_b2'] = jnp.zeros((L,), jnp.float32)
        inp['core_w'] = W((D, D))
        inp['core_b'] = jnp.zeros((D,), jnp.float32)
        for e, h in enumerate(HID):
            inp[f'e{e}_w1'] = W((L, h))
            inp[f'e{e}_b1'] = jnp.zeros((h,), jnp.float32)
            inp[f'e{e}_w2'] = W((h, L))
            inp[f'e{e}_b2'] = jnp.zeros((L,), jnp.float32)
        return inp
    _L1_ffn_in = _L1_ffn_setup()
    _d = {'L0_attn_x': _L0_attn_in['x'], 'L0_attn_Wq': _L0_attn_in['Wq'], 'L0_attn_Wk': _L0_attn_in['Wk'], 'L0_attn_Wv': _L0_attn_in['Wv'], 'L0_attn_Wo': _L0_attn_in['Wo'], 'L0_ffn_gate_w': _L0_ffn_in['gate_w'], 'L0_ffn_w_gate': _L0_ffn_in['w_gate'], 'L0_ffn_w_up': _L0_ffn_in['w_up'], 'L0_ffn_w_down': _L0_ffn_in['w_down'], 'L0_ffn_sh_gate': _L0_ffn_in['sh_gate'], 'L0_ffn_sh_up': _L0_ffn_in['sh_up'], 'L0_ffn_sh_down': _L0_ffn_in['sh_down'], 'L0_ffn_se_gate_w': _L0_ffn_in['se_gate_w'], 'L1_attn_x_proj_w': _L1_attn_in['x_proj_w'], 'L1_attn_dt_proj_w': _L1_attn_in['dt_proj_w'], 'L1_attn_dt_proj_b': _L1_attn_in['dt_proj_b'], 'L1_attn_A_log': _L1_attn_in['A_log'], 'L1_attn_D': _L1_attn_in['D'], 'L1_ffn_down_w': _L1_ffn_in['down_w'], 'L1_ffn_down_b': _L1_ffn_in['down_b'], 'L1_ffn_up_w': _L1_ffn_in['up_w'], 'L1_ffn_up_b': _L1_ffn_in['up_b'], 'L1_ffn_router_w': _L1_ffn_in['router_w'], 'L1_ffn_router_b': _L1_ffn_in['router_b'], 'L1_ffn_shared_w1': _L1_ffn_in['shared_w1'], 'L1_ffn_shared_b1': _L1_ffn_in['shared_b1'], 'L1_ffn_shared_w2': _L1_ffn_in['shared_w2'], 'L1_ffn_shared_b2': _L1_ffn_in['shared_b2'], 'L1_ffn_core_w': _L1_ffn_in['core_w'], 'L1_ffn_core_b': _L1_ffn_in['core_b'], 'L1_ffn_e0_w1': _L1_ffn_in['e0_w1'], 'L1_ffn_e0_b1': _L1_ffn_in['e0_b1'], 'L1_ffn_e0_w2': _L1_ffn_in['e0_w2'], 'L1_ffn_e0_b2': _L1_ffn_in['e0_b2'], 'L1_ffn_e1_w1': _L1_ffn_in['e1_w1'], 'L1_ffn_e1_b1': _L1_ffn_in['e1_b1'], 'L1_ffn_e1_w2': _L1_ffn_in['e1_w2'], 'L1_ffn_e1_b2': _L1_ffn_in['e1_b2'], 'L1_ffn_e2_w1': _L1_ffn_in['e2_w1'], 'L1_ffn_e2_b1': _L1_ffn_in['e2_b1'], 'L1_ffn_e2_w2': _L1_ffn_in['e2_w2'], 'L1_ffn_e2_b2': _L1_ffn_in['e2_b2'], 'L1_ffn_e3_w1': _L1_ffn_in['e3_w1'], 'L1_ffn_e3_b1': _L1_ffn_in['e3_b1'], 'L1_ffn_e3_w2': _L1_ffn_in['e3_w2'], 'L1_ffn_e3_b2': _L1_ffn_in['e3_b2'], 'L1_ffn_e4_w1': _L1_ffn_in['e4_w1'], 'L1_ffn_e4_b1': _L1_ffn_in['e4_b1'], 'L1_ffn_e4_w2': _L1_ffn_in['e4_w2'], 'L1_ffn_e4_b2': _L1_ffn_in['e4_b2'], 'L1_ffn_e5_w1': _L1_ffn_in['e5_w1'], 'L1_ffn_e5_b1': _L1_ffn_in['e5_b1'], 'L1_ffn_e5_w2': _L1_ffn_in['e5_w2'], 'L1_ffn_e5_b2': _L1_ffn_in['e5_b2'], 'L1_ffn_e6_w1': _L1_ffn_in['e6_w1'], 'L1_ffn_e6_b1': _L1_ffn_in['e6_b1'], 'L1_ffn_e6_w2': _L1_ffn_in['e6_w2'], 'L1_ffn_e6_b2': _L1_ffn_in['e6_b2'], 'L1_ffn_e7_w1': _L1_ffn_in['e7_w1'], 'L1_ffn_e7_b1': _L1_ffn_in['e7_b1'], 'L1_ffn_e7_w2': _L1_ffn_in['e7_w2'], 'L1_ffn_e7_b2': _L1_ffn_in['e7_b2']}
    _x0 = _d['L0_attn_x']
    _d['L0_attn_x'] = jax.random.normal(jax.random.fold_in(jax.random.key(seed), 1), (4, 1024, 256), dtype=_x0.dtype)
    del _x0
    return _d

def reference(L0_attn_x, L0_attn_Wq, L0_attn_Wk, L0_attn_Wv, L0_attn_Wo, L0_ffn_gate_w, L0_ffn_w_gate, L0_ffn_w_up, L0_ffn_w_down, L0_ffn_sh_gate, L0_ffn_sh_up, L0_ffn_sh_down, L0_ffn_se_gate_w, L1_attn_x_proj_w, L1_attn_dt_proj_w, L1_attn_dt_proj_b, L1_attn_A_log, L1_attn_D, L1_ffn_down_w, L1_ffn_down_b, L1_ffn_up_w, L1_ffn_up_b, L1_ffn_router_w, L1_ffn_router_b, L1_ffn_shared_w1, L1_ffn_shared_b1, L1_ffn_shared_w2, L1_ffn_shared_b2, L1_ffn_core_w, L1_ffn_core_b, L1_ffn_e0_w1, L1_ffn_e0_b1, L1_ffn_e0_w2, L1_ffn_e0_b2, L1_ffn_e1_w1, L1_ffn_e1_b1, L1_ffn_e1_w2, L1_ffn_e1_b2, L1_ffn_e2_w1, L1_ffn_e2_b1, L1_ffn_e2_w2, L1_ffn_e2_b2, L1_ffn_e3_w1, L1_ffn_e3_b1, L1_ffn_e3_w2, L1_ffn_e3_b2, L1_ffn_e4_w1, L1_ffn_e4_b1, L1_ffn_e4_w2, L1_ffn_e4_b2, L1_ffn_e5_w1, L1_ffn_e5_b1, L1_ffn_e5_w2, L1_ffn_e5_b2, L1_ffn_e6_w1, L1_ffn_e6_b1, L1_ffn_e6_w2, L1_ffn_e6_b2, L1_ffn_e7_w1, L1_ffn_e7_b1, L1_ffn_e7_w2, L1_ffn_e7_b2):

    def _L0_attn_ref(x, Wq, Wk, Wv, Wo):
        import jax, jax.numpy as jnp
        import numpy as np
        HEADS = 16
        B, T, _ = x.shape
        H = HEADS
        Dh = Wq.shape[1] // H
        q = (x @ Wq).reshape(B, T, H, Dh)
        k = (x @ Wk).reshape(B, T, H, Dh)
        v = (x @ Wv).reshape(B, T, H, Dh)
        scores = jnp.einsum('bthd,bshd->bhts', q, k)
        mask = jnp.tril(jnp.ones((T, T), dtype=scores.dtype))
        scores = scores * mask
        attn = jax.nn.softmax(scores / T ** 0.5, axis=-1)
        out = jnp.einsum('bhts,bshd->bthd', attn, v).reshape(B, T, H * Dh)
        return out @ Wo

    def _L0_ffn_ref(x, gate_w, w_gate, w_up, w_down, sh_gate, sh_up, sh_down, se_gate_w):
        import jax, jax.numpy as jnp
        import numpy as np
        N_EXPERTS = 8
        TOP_K = 2
        C = 256
        H = 128
        HS = 256
        B, T = (1, 64)
        SCALE = 0.02
        Bb, Tt, Cc = x.shape
        xf = x.reshape(-1, Cc)
        scores = xf @ gate_w.T
        ew, ei = jax.lax.top_k(scores, TOP_K)
        ew = jax.nn.softmax(ew, axis=-1)
        x1 = jax.nn.silu(jnp.einsum('td,ehd->teh', xf, w_gate))
        x3 = jnp.einsum('td,ehd->teh', xf, w_up)
        expert_out = jnp.einsum('teh,edh->ted', x1 * x3, w_down)
        onehot = jax.nn.one_hot(ei, N_EXPERTS, dtype=ew.dtype)
        comb = jnp.einsum('ta,tae->te', ew, onehot)
        routed = jnp.einsum('te,ted->td', comb, expert_out)
        shared = jax.nn.silu(xf @ sh_gate.T) * (xf @ sh_up.T) @ sh_down.T
        sgate = jax.nn.sigmoid(xf @ se_gate_w.T)
        return (routed + sgate * shared).reshape(Bb, Tt, Cc)

    def _L1_attn_ref(x, x_proj_w, dt_proj_w, dt_proj_b, A_log, D):
        import jax, jax.numpy as jnp
        import numpy as np
        D_INNER = 256
        DT_RANK = 64
        D_STATE = 16
        BATCH = 2
        SEQLEN = 256
        A = -jnp.exp(A_log)
        x_dbl = jnp.einsum('bld,kd->blk', x, x_proj_w)
        delta, Bmat, Cmat = jnp.split(x_dbl, [DT_RANK, DT_RANK + D_STATE], axis=-1)
        delta = jax.nn.softplus(jnp.einsum('blr,dr->bld', delta, dt_proj_w) + dt_proj_b)
        deltaA = jnp.exp(jnp.einsum('bld,dn->bldn', delta, A))
        deltaB_u = jnp.einsum('bld,bln->bldn', delta * x, Bmat)

        def step(h, inp):
            dA_t, dBu_t, c_t = inp
            h = dA_t * h + dBu_t
            y_t = jnp.einsum('bdn,bn->bd', h, c_t)
            return (h, y_t)
        h0 = jnp.zeros((x.shape[0], D_INNER, D_STATE), dtype=x.dtype)
        xs = (jnp.swapaxes(deltaA, 0, 1), jnp.swapaxes(deltaB_u, 0, 1), jnp.swapaxes(Cmat, 0, 1))
        _, ys = jax.lax.scan(step, h0, xs)
        y = jnp.swapaxes(ys, 0, 1)
        return y + x * D

    def _L1_ffn_ref(x, down_w, down_b, up_w, up_b, router_w, router_b, shared_w1, shared_b1, shared_w2, shared_b2, core_w, core_b, e0_w1, e0_b1, e0_w2, e0_b2, e1_w1, e1_b1, e1_w2, e1_b2, e2_w1, e2_b1, e2_w2, e2_b2, e3_w1, e3_b1, e3_w2, e3_b2, e4_w1, e4_b1, e4_w2, e4_b2, e5_w1, e5_b1, e5_w2, e5_b2, e6_w1, e6_b1, e6_w2, e6_b2, e7_w1, e7_b1, e7_w2, e7_b2):
        import jax, jax.numpy as jnp
        import numpy as np
        COST_LAMBDA = 1e-07
        HID = [128, 256, 384, 512, 128, 256, 384, 512]
        TOP_K = 2

        def _gelu(v):
            return jax.nn.gelu(v, approximate=False)

        def _forward(x, down_w, down_b, up_w, up_b, router_w, router_b, shared_w1, shared_b1, shared_w2, shared_b2, core_w, core_b, expert_params):
            E = len(expert_params)
            h = x @ down_w + down_b
            cost = jnp.array([w1.shape[0] * w1.shape[1] + w2.shape[0] * w2.shape[1] for w1, _, w2, _ in expert_params], jnp.float32)
            logits = x @ router_w + router_b - COST_LAMBDA * cost
            probs = jax.nn.softmax(logits, axis=-1)
            topv, topi = jax.lax.top_k(probs, TOP_K)
            gate = jax.nn.softmax(topv, axis=-1)
            out = jnp.zeros_like(h)
            for k in range(TOP_K):
                mask = jax.nn.one_hot(topi[..., k], E, dtype=h.dtype)
                acc = jnp.zeros_like(h)
                for e, (w1, b1, w2, b2) in enumerate(expert_params):
                    hm = h * mask[..., e:e + 1]
                    acc = acc + (_gelu(_gelu(hm) @ w1 + b1) @ w2 + b2)
                out = out + acc * gate[..., k:k + 1]
            out = out + 0.1 * (_gelu(_gelu(h) @ shared_w1 + shared_b1) @ shared_w2 + shared_b2)
            out = out @ up_w + up_b
            out = out + (_gelu(x) @ core_w + core_b)
            return out
        ep = [(e0_w1, e0_b1, e0_w2, e0_b2), (e1_w1, e1_b1, e1_w2, e1_b2), (e2_w1, e2_b1, e2_w2, e2_b2), (e3_w1, e3_b1, e3_w2, e3_b2), (e4_w1, e4_b1, e4_w2, e4_b2), (e5_w1, e5_b1, e5_w2, e5_b2), (e6_w1, e6_b1, e6_w2, e6_b2), (e7_w1, e7_b1, e7_w2, e7_b2)]
        return _forward(x, down_w, down_b, up_w, up_b, router_w, router_b, shared_w1, shared_b1, shared_w2, shared_b2, core_w, core_b, ep)
    x = L0_attn_x
    x = x + 0.5 * _L0_ffn_ref(_layernorm(x, axis=-1), L0_ffn_gate_w, L0_ffn_w_gate, L0_ffn_w_up, L0_ffn_w_down, L0_ffn_sh_gate, L0_ffn_sh_up, L0_ffn_sh_down, L0_ffn_se_gate_w)
    x = x + _L0_attn_ref(_layernorm(x, axis=-1), L0_attn_Wq, L0_attn_Wk, L0_attn_Wv, L0_attn_Wo)
    x = x + 0.5 * _L0_ffn_ref(_layernorm(x, axis=-1), L0_ffn_gate_w, L0_ffn_w_gate, L0_ffn_w_up, L0_ffn_w_down, L0_ffn_sh_gate, L0_ffn_sh_up, L0_ffn_sh_down, L0_ffn_se_gate_w)
    x = x + 0.5 * _L1_ffn_ref(_layernorm(x, axis=-1), L1_ffn_down_w, L1_ffn_down_b, L1_ffn_up_w, L1_ffn_up_b, L1_ffn_router_w, L1_ffn_router_b, L1_ffn_shared_w1, L1_ffn_shared_b1, L1_ffn_shared_w2, L1_ffn_shared_b2, L1_ffn_core_w, L1_ffn_core_b, L1_ffn_e0_w1, L1_ffn_e0_b1, L1_ffn_e0_w2, L1_ffn_e0_b2, L1_ffn_e1_w1, L1_ffn_e1_b1, L1_ffn_e1_w2, L1_ffn_e1_b2, L1_ffn_e2_w1, L1_ffn_e2_b1, L1_ffn_e2_w2, L1_ffn_e2_b2, L1_ffn_e3_w1, L1_ffn_e3_b1, L1_ffn_e3_w2, L1_ffn_e3_b2, L1_ffn_e4_w1, L1_ffn_e4_b1, L1_ffn_e4_w2, L1_ffn_e4_b2, L1_ffn_e5_w1, L1_ffn_e5_b1, L1_ffn_e5_w2, L1_ffn_e5_b2, L1_ffn_e6_w1, L1_ffn_e6_b1, L1_ffn_e6_w2, L1_ffn_e6_b2, L1_ffn_e7_w1, L1_ffn_e7_b1, L1_ffn_e7_w2, L1_ffn_e7_b2)
    x = x + _L1_attn_ref(_layernorm(x, axis=-1), L1_attn_x_proj_w, L1_attn_dt_proj_w, L1_attn_dt_proj_b, L1_attn_A_log, L1_attn_D)
    x = x + 0.5 * _L1_ffn_ref(_layernorm(x, axis=-1), L1_ffn_down_w, L1_ffn_down_b, L1_ffn_up_w, L1_ffn_up_b, L1_ffn_router_w, L1_ffn_router_b, L1_ffn_shared_w1, L1_ffn_shared_b1, L1_ffn_shared_w2, L1_ffn_shared_b2, L1_ffn_core_w, L1_ffn_core_b, L1_ffn_e0_w1, L1_ffn_e0_b1, L1_ffn_e0_w2, L1_ffn_e0_b2, L1_ffn_e1_w1, L1_ffn_e1_b1, L1_ffn_e1_w2, L1_ffn_e1_b2, L1_ffn_e2_w1, L1_ffn_e2_b1, L1_ffn_e2_w2, L1_ffn_e2_b2, L1_ffn_e3_w1, L1_ffn_e3_b1, L1_ffn_e3_w2, L1_ffn_e3_b2, L1_ffn_e4_w1, L1_ffn_e4_b1, L1_ffn_e4_w2, L1_ffn_e4_b2, L1_ffn_e5_w1, L1_ffn_e5_b1, L1_ffn_e5_w2, L1_ffn_e5_b2, L1_ffn_e6_w1, L1_ffn_e6_b1, L1_ffn_e6_w2, L1_ffn_e6_b2, L1_ffn_e7_w1, L1_ffn_e7_b1, L1_ffn_e7_w2, L1_ffn_e7_b2)
    return x

_drawn_inputs = setup_inputs


def setup_inputs(seed=0):
    import zlib

    import numpy as np

    out = dict(_drawn_inputs(seed))
    spreads = {'L1_attn_D': (1.0, 0.2),
     'L1_ffn_down_b': (0.0, 0.8),
     'L1_ffn_up_b': (0.0, 0.1),
     'L1_ffn_router_b': (0.0, 0.8),
     'L1_ffn_shared_b1': (0.0, 2.0),
     'L1_ffn_shared_b2': (0.0, 2.0),
     'L1_ffn_core_b': (0.0, 0.1),
     'L1_ffn_e0_b1': (0.0, 0.8),
     'L1_ffn_e0_b2': (0.0, 0.385),
     'L1_ffn_e1_b1': (0.0, 0.8),
     'L1_ffn_e1_b2': (0.0, 0.373),
     'L1_ffn_e2_b1': (0.0, 0.8),
     'L1_ffn_e2_b2': (0.0, 0.427),
     'L1_ffn_e3_b1': (0.0, 0.8),
     'L1_ffn_e3_b2': (0.0, 0.396),
     'L1_ffn_e4_b1': (0.0, 0.8),
     'L1_ffn_e4_b2': (0.0, 0.415),
     'L1_ffn_e5_b1': (0.0, 0.8),
     'L1_ffn_e5_b2': (0.0, 0.408),
     'L1_ffn_e6_b1': (0.0, 0.8),
     'L1_ffn_e6_b2': (0.0, 0.33),
     'L1_ffn_e7_b1': (0.0, 0.8),
     'L1_ffn_e7_b2': (0.0, 0.367)}
    factors = {'L0_attn_Wq': 8.0,
     'L0_attn_Wk': 8.0,
     'L0_attn_Wv': 8.0,
     'L0_attn_Wo': 8.0,
     'L0_ffn_gate_w': 4.382,
     'L0_ffn_w_gate': 3.867,
     'L0_ffn_w_up': 3.778,
     'L0_ffn_w_down': 3.8,
     'L0_ffn_sh_gate': 3.804,
     'L0_ffn_sh_up': 3.808,
     'L0_ffn_sh_down': 3.798,
     'L0_ffn_se_gate_w': 8.0,
     'L1_attn_dt_proj_b': 8.0,
     'L1_ffn_down_w': 8.0,
     'L1_ffn_router_w': 8.0,
     'L1_ffn_shared_w1': 8.0,
     'L1_ffn_shared_w2': 8.0,
     'L1_ffn_e0_w1': 8.0,
     'L1_ffn_e0_w2': 8.0,
     'L1_ffn_e1_w1': 8.0,
     'L1_ffn_e1_w2': 8.0,
     'L1_ffn_e2_w1': 8.0,
     'L1_ffn_e2_w2': 8.0,
     'L1_ffn_e3_w1': 8.0,
     'L1_ffn_e3_w2': 8.0,
     'L1_ffn_e4_w1': 8.0,
     'L1_ffn_e4_w2': 8.0,
     'L1_ffn_e5_w1': 8.0,
     'L1_ffn_e5_w2': 8.0,
     'L1_ffn_e6_w1': 8.0,
     'L1_ffn_e6_w2': 8.0,
     'L1_ffn_e7_w1': 8.0,
     'L1_ffn_e7_w2': 8.0}
    for name, (base, spread) in spreads.items():
        noise = np.random.default_rng([zlib.crc32(name.encode()), seed]).standard_normal(out[name].shape)
        drawn = base * np.exp(spread * noise) if base else spread * noise
        out[name] = jnp.asarray(drawn.astype(out[name].dtype))
    for name, factor in factors.items():
        out[name] = (out[name] * factor).astype(out[name].dtype)
    return out
```

```python
from contextlib import ExitStack

import numpy as np

import concourse.bass as bass
from concourse import mybir

ALU = mybir.AluOpType
ACT = mybir.ActivationFunctionType
AX = mybir.AxisListType
F32 = mybir.dt.float32
BF16 = mybir.dt.bfloat16
U32 = mybir.dt.uint32

P = 128
B, T, D = 4, 1024, 256
KD = D // P
TOKENS = B * T
TILES = TOKENS // P
CH = 512
CT = CH // P
CHUNKS = TOKENS // CH
EPS = 1e-5
E0 = 8
UNITS0 = E0 + 2
G0 = E0 + 1
E1 = 8
HID1 = [128, 256, 384, 512, 128, 256, 384, 512]
TILE_EXPERT = [e for e in range(E1) for _ in range(HID1[e] // P)]
HT1 = len(TILE_EXPERT)
HEADS, DH = 16, 16
GH = 4
HG = HEADS // GH
BT = T // P
STATES = 16
RANK = 64


def three_parts(dve, sem, base, whole, part1, rest, part2, rest2, part3):
    dve.tensor_copy(part1, whole).then_inc(sem, 1)
    dve.wait_ge(sem, base + 1)
    dve.tensor_tensor(rest, whole, part1, ALU.subtract).then_inc(sem, 1)
    dve.wait_ge(sem, base + 2)
    dve.tensor_copy(part2, rest).then_inc(sem, 1)
    dve.wait_ge(sem, base + 3)
    dve.tensor_tensor(rest2, rest, part2, ALU.subtract).then_inc(sem, 1)
    dve.wait_ge(sem, base + 4)
    return dve.tensor_copy(part3, rest2)


def ffn_moe(nc, tag, x, w, const):
    with ExitStack() as ctx:
        ctx.enter_context(nc.cleanup_on_exit())

        def sb(name, shape, dt=F32):
            return ctx.enter_context(nc.sbuf_tensor(f"{tag}_{name}", shape, dt))

        def psum(name, shape, dt=F32):
            return ctx.enter_context(nc.psum_tensor(f"{tag}_{name}", shape, dt))

        def sem(name):
            return nc.alloc_semaphore(f"{tag}_{name}")

        xn = sb("xn", [P, CT, D])
        xnT = sb("xnT", [P, 2, KD, CH])
        stats = sb("stats", [P, CT, 6])
        mean_var = sb("mean_var", [P, CT, 2])
        var_eps = sb("var_eps", [P, CT])
        rstd = sb("rstd", [P, CT])
        scores = sb("scores", [P, CT, G0])
        top = sb("top", [P, CT, 8])
        top_at = sb("top_at", [P, CT, 8], U32)
        at = sb("at", [P, CT, 2])
        diff = sb("diff", [P, CT, 2])
        tanh = sb("tanh", [P, CT, 2])
        weight = sb("weight", [P, CT, 2])
        hit = sb("hit", [P, 2, CT, E0])
        gates = sb("gates", [P, CT, G0])
        rest = sb("rest", [P, CT, G0])
        rest2 = sb("rest2", [P, CT, G0])
        gparts = sb("gparts", [P, CT, 3 * G0], BF16)
        gT = sb("gT", [3 * G0, 2, CH], BF16)
        silu = sb("silu", [P, 2, CH])
        prod = sb("prod", [P, 2, CH])
        hid = sb("hid", [P, 2, CH])

        x1 = psum("x1", [P, 2, CH])
        x3 = psum("x3", [P, 2, CH])
        gate_bc = psum("gate_bc", [P, CH])
        acc = psum("acc", [P, CT, D])
        misc = psum("misc", [P, CH])
        misc_bf = misc[0:3 * G0, 0:CH // 2].bitcast(BF16)

        chain = sem("dve_steps")
        s_var = sem("var_ready")
        s_rstd = sem("rstd_ready")
        s_xn = sem("xn_ready")
        s_T = sem("half_transposed")
        s_Tc = sem("half_kept")
        s_R = sem("scores_ready")
        s_Rc = sem("scores_kept")
        s_diff = sem("diff_ready")
        s_tanh = sem("tanh_ready")
        s_gp = sem("gate_parts_ready")
        s_GT = sem("gates_transposed")
        s_gT = sem("gates_kept")
        s_x1 = sem("x1_ready")
        s_x3 = sem("x3_and_gate_ready")
        s_silu = sem("silu_done")
        s_prod = sem("product_done")
        s_hid = sem("hidden_ready")
        s_down = sem("down_done")
        s_acc = sem("chunk_added")

        NORM, CHOOSE, WEIGH = 3, 7, 7
        STEPS = NORM + CHOOSE + WEIGH

        def tile_of(c, t):
            return bass.ds(c * CT + t, 1) if not isinstance(c, int) else slice(c * CT + t, c * CT + t + 1)

        block = ctx.enter_context(nc.Block())

        @block.vector
        def _(dve):
            def norm_stats(c):
                for t in range(CT):
                    last = dve.bn_stats(stats[:, t, :], x[:, tile_of(c, t), :].rearrange("p a d -> p (a d)"))
                last.then_inc(chain, 1)
                dve.wait_ge(chain, c * STEPS + 1)
                dve.sem_inc(chain, 1)
                for t in range(CT):
                    last = dve.bn_aggr(mean_var[:, t, :], stats[:, t, :])
                last.then_inc(chain, 1)
                dve.wait_ge(chain, c * STEPS + 3)
                dve.tensor_scalar(var_eps[:, :], mean_var[:, :, 1], EPS, None, ALU.add).then_inc(s_var, 1)

            def norm_apply(c):
                dve.wait_ge(s_rstd, c + 1)
                dve.wait_ge(s_T, c * KD)
                for t in range(CT):
                    last = dve.tensor_scalar(xn[:, t, :], x[:, tile_of(c, t), :].rearrange("p a d -> p (a d)"),
                                             mean_var[:, t, 0:1], rstd[:, t:t + 1], ALU.subtract, ALU.mult)
                last.then_inc(s_xn, 1)

            def choose(c):
                base = c * STEPS + NORM
                dve.wait_ge(s_R, c + 1)
                dve.tensor_copy(scores[:, :, :], misc[:, 0:CT * G0].rearrange("p (t g) -> p t g", t=CT)).then_inc(s_Rc, 1)
                dve.wait_ge(s_Rc, c + 1)
                dve.sem_inc(chain, 1)
                for t in range(CT):
                    last = dve.max(top[:, t, :], scores[:, t, 0:E0])
                last.then_inc(chain, 1)
                dve.wait_ge(chain, base + 2)
                dve.sem_inc(chain, 1)
                for t in range(CT):
                    last = dve.max_index(top_at[:, t, :], top[:, t, :], scores[:, t, 0:E0])
                last.then_inc(chain, 1)
                dve.tensor_tensor(diff[:, :, 0:1], top[:, :, 0:1], top[:, :, 1:2], ALU.subtract)
                dve.tensor_copy(diff[:, :, 1:2], scores[:, :, E0:E0 + 1]).then_inc(s_diff, 1)
                dve.wait_ge(chain, base + 4)
                dve.tensor_copy(at[:, :, :], top_at[:, :, 0:2]).then_inc(chain, 1)
                dve.wait_ge(chain, base + 5)
                for k in range(2):
                    dve.tensor_tensor(hit[:, k, :, :], const["iota"][:, :].rearrange("p (a e) -> p a e", a=1).broadcast_to([P, CT, E0]),
                                      at[:, :, k:k + 1].broadcast_to([P, CT, E0]), ALU.is_equal).then_inc(chain, 1)

            def weigh(c):
                base = c * STEPS + NORM + CHOOSE
                dve.wait_ge(s_tanh, c + 1)
                dve.tensor_scalar(weight[:, :, 0:1], tanh[:, :, 0:1], 0.25, 0.25, ALU.mult, ALU.add)
                dve.tensor_scalar(weight[:, :, 1:2], tanh[:, :, 0:1], -0.25, 0.25, ALU.mult, ALU.add)
                dve.tensor_scalar(gates[:, :, E0:G0], tanh[:, :, 1:2], 0.25, 0.25, ALU.mult, ALU.add).then_inc(chain, 1)
                dve.wait_ge(chain, base + 1)
                for k in range(2):
                    last = dve.tensor_tensor(hit[:, k, :, :], hit[:, k, :, :],
                                             weight[:, :, k:k + 1].broadcast_to([P, CT, E0]), ALU.mult)
                last.then_inc(chain, 1)
                dve.wait_ge(chain, base + 2)
                dve.tensor_tensor(gates[:, :, 0:E0], hit[:, 0, :, :], hit[:, 1, :, :], ALU.add).then_inc(chain, 1)
                dve.wait_ge(chain, base + 3)
                dve.wait_ge(s_GT, c)
                three_parts(dve, chain, base + 3, gates[:, :, :], gparts[:, :, 0:G0], rest[:, :, :],
                            gparts[:, :, G0:2 * G0], rest2[:, :, :], gparts[:, :, 2 * G0:3 * G0]).then_inc(s_gp, 1)

            def hidden(c, u):
                n = c * UNITS0 + u
                b = u % 2
                dve.wait_ge(s_silu, n + 3)
                dve.wait_ge(s_x3, n + 1)
                dve.tensor_tensor(prod[:, b, :], silu[:, b, :], x3[:, b, :], ALU.mult).then_inc(s_prod, 1)
                dve.wait_ge(s_prod, n + 3)
                dve.wait_ge(s_down, n + 1)
                dve.tensor_tensor(hid[:, b, :], prod[:, b, :], gate_bc[:, :], ALU.mult).then_inc(s_hid, 1)

            def add(c):
                dve.wait_ge(s_down, c * UNITS0 + UNITS0 + 2)
                for t in range(0, CT, 2):
                    where = x[:, bass.ds(c * CT + t, 2) if not isinstance(c, int) else slice(c * CT + t, c * CT + t + 2), :]
                    last = dve.tensor_tensor(where, acc[:, t:t + 2, :], where, ALU.add)
                last.then_inc(s_acc, 1)

            def chunk(c, last=False):
                for u in range(1, UNITS0):
                    hidden(c, u)
                    if not last:
                        if u == 1:
                            norm_stats(c + 1)
                        if u == 2:
                            norm_apply(c + 1)
                        if u == 5:
                            choose(c + 1)
                        if u == 6:
                            weigh(c + 1)
                if not last:
                    hidden(c + 1, 0)
                add(c)

            dve.sem_inc(s_prod, 2)
            dve.sem_inc(s_hid, 1)
            dve.sem_inc(s_acc, 1)
            norm_stats(0)
            norm_apply(0)
            choose(0)
            weigh(0)
            hidden(0, 0)
            with dve.Fori(0, CHUNKS - 2, 2) as c:
                chunk(c)
                chunk(c + 1)
            chunk(CHUNKS - 2)
            chunk(CHUNKS - 1, last=True)

        @block.gpsimd
        def _(pool):
            with pool.Fori(0, CHUNKS) as c:
                pool.wait_ge(s_var, c + 1)
                pool.tensor_tensor(rstd[:, :], var_eps[:, :], const["minus_half"][:, 0:CT], ALU.pow).then_inc(s_rstd, 1)

        @block.scalar
        def _(act):
            def keep_half(c, par, k):
                act.wait_ge(s_T, c * KD + k + 1)
                act.activation(xnT[:, par, k, :], misc[:, :], ACT.Copy).then_inc(s_Tc, 1)

            def tanhs(c):
                act.wait_ge(s_diff, c + 1)
                act.activation(tanh[:, :, :], diff[:, :, :], ACT.Tanh, scale=0.5).then_inc(s_tanh, 1)

            def keep_gates(c, par):
                act.wait_ge(s_GT, c + 1)
                act.activation(gT[:, par, :], misc_bf, ACT.Copy).then_inc(s_gT, 1)

            def unit(c, u):
                n = c * UNITS0 + u
                act.wait_ge(s_x1, n + 1)
                act.wait_ge(s_prod, n + 1)
                act.activation(silu[:, u % 2, :], x1[:, u % 2, :], ACT.Silu).then_inc(s_silu, 1)

            def chunk(c, par, last=False):
                for u in range(1, UNITS0):
                    unit(c, u)
                    if not last:
                        if u == 3:
                            keep_half(c + 1, 1 - par, 0)
                        if u == 4:
                            keep_half(c + 1, 1 - par, 1)
                        if u == 6:
                            tanhs(c + 1)
                        if u == 8:
                            keep_gates(c + 1, 1 - par)
                if not last:
                    unit(c + 1, 0)

            act.sem_inc(s_silu, 2)
            for k in range(KD):
                keep_half(0, 0, k)
            tanhs(0)
            keep_gates(0, 0)
            unit(0, 0)
            with act.Fori(0, CHUNKS - 2, 2) as c:
                chunk(c, 0)
                chunk(c + 1, 1)
            chunk(CHUNKS - 2, 0)
            chunk(CHUNKS - 1, 1, last=True)

        @block.tensor
        def _(pe):
            def turn_half(c, k):
                if k == 0:
                    pe.wait_ge(s_xn, c + 1)
                    pe.wait_ge(s_gT, c)
                else:
                    pe.wait_ge(s_Tc, c * KD + k)
                for t in range(CT):
                    last = pe.transpose(misc[:, t * P:(t + 1) * P], xn[:, t, k * P:(k + 1) * P], const["ident"][:, :])
                last.then_inc(s_T, 1)

            def route(c, par):
                pe.wait_ge(s_Tc, c * KD + KD)
                for t in range(CT):
                    for k in range(KD):
                        last = pe.matmul(misc[:, t * G0:(t + 1) * G0], xnT[:, par, k, t * P:(t + 1) * P],
                                         w["router"][:, k, :], start=(k == 0), stop=(k == KD - 1))
                last.then_inc(s_R, 1)

            def turn_gates(c):
                pe.wait_ge(s_gp, c + 1)
                for t in range(CT):
                    last = pe.transpose(misc_bf[:, t * P:(t + 1) * P], gparts[:, t, :], const["ident_bf"][:, :])
                last.then_inc(s_GT, 1)

            def up(c, par, u):
                n = c * UNITS0 + u
                b = u % 2
                pe.wait_ge(s_silu, n + 1)
                for k in range(KD):
                    last = pe.matmul(x1[:, b, :], w["gate"][:, u, k, :], xnT[:, par, k, :], start=(k == 0), stop=(k == KD - 1))
                last.then_inc(s_x1, 1)
                pe.wait_ge(s_prod, n + 1)
                for k in range(KD):
                    pe.matmul(x3[:, b, :], w["up"][:, u, k, :], xnT[:, par, k, :], start=(k == 0), stop=(k == KD - 1))
                pe.wait_ge(s_hid, n + 1)
                if u == 0:
                    pe.wait_ge(s_gT, c + 1)
                pe.matmul(gate_bc[:, :], const["pick_gate"][:, min(u, E0), :], gT[:, par, :],
                          start=True, stop=True).then_inc(s_x3, 1)

            def down(c, u):
                n = c * UNITS0 + u
                pe.wait_ge(s_hid, n + 2)
                if u == 0:
                    pe.wait_ge(s_acc, c + 1)
                for t in range(CT):
                    last = pe.matmul(acc[:, t, :], hid[:, u % 2, t * P:(t + 1) * P], w["down"][:, u, :],
                                     start=(u == 0 and t % 2 == 0), stop=(u == UNITS0 - 1), skip_group_check=True)
                last.then_inc(s_down, 1)

            def chunk(c, par, last=False):
                for u in range(1, UNITS0):
                    up(c, par, u)
                    down(c, u - 1)
                    if not last:
                        if u == 2:
                            turn_half(c + 1, 0)
                        if u == 3:
                            turn_half(c + 1, 1)
                        if u == 4:
                            route(c + 1, 1 - par)
                        if u == 7:
                            turn_gates(c + 1)
                if not last:
                    up(c + 1, 1 - par, 0)
                down(c, UNITS0 - 1)

            pe.sem_inc(s_down, 2)
            turn_half(0, 0)
            turn_half(0, 1)
            route(0, 0)
            turn_gates(0)
            up(0, 0, 0)
            with pe.Fori(0, CHUNKS - 2, 2) as c:
                chunk(c, 0)
                chunk(c + 1, 1)
            chunk(CHUNKS - 2, 0)
            chunk(CHUNKS - 1, 1, last=True)


def ffn_gelu(nc, tag, x, w, const):
    with ExitStack() as ctx:
        ctx.enter_context(nc.cleanup_on_exit())

        def sb(name, shape, dt=F32):
            return ctx.enter_context(nc.sbuf_tensor(f"{tag}_{name}", shape, dt))

        def psum(name, shape, dt=F32):
            return ctx.enter_context(nc.psum_tensor(f"{tag}_{name}", shape, dt))

        def sem(name):
            return nc.alloc_semaphore(f"{tag}_{name}")

        xn = sb("xn", [P, CT, D])
        xnT = sb("xnT", [P, KD, CH])
        core = sb("core", [P, 2, KD, CH])
        gelu_h = sb("gelu_h", [P, 2, CH])
        stats = sb("stats", [P, CT, 6])
        mean_var = sb("mean_var", [P, CT, 2])
        var_eps = sb("var_eps", [P, CT])
        rstd = sb("rstd", [P, CT])
        biased = sb("biased", [P, CT, E1])
        logits = sb("logits", [P, CT, E1])
        shifted = sb("shifted", [P, CT, E1])
        expd = sb("expd", [P, CT, E1])
        total = sb("total", [P, CT])
        inverse = sb("inverse", [P, CT])
        probs = sb("probs", [P, CT, E1])
        top = sb("top", [P, CT, 8])
        top_p = sb("top_p", [P, CT, 8])
        top_at = sb("top_at", [P, CT, 8], U32)
        at = sb("at", [P, CT, 2])
        diff = sb("diff", [P, CT, 1])
        tanh = sb("tanh", [P, CT, 1])
        weight = sb("weight", [P, CT, 2])
        hit = sb("hit", [P, 2, CT, E1])
        gates = sb("gates", [P, CT, E1])
        rest = sb("rest", [P, CT, E1])
        rest2 = sb("rest2", [P, CT, E1])
        gparts = sb("gparts", [P, CT, 3 * E1], BF16)
        gT = sb("gT", [3 * E1, CH], BF16)
        gate_bc = sb("gate_bc", [P, 2, E1, CH])
        act_out = sb("act_out", [P, 3, CH])
        hid = sb("hid", [P, 3, CH])
        mixed = sb("mixed", [P, CH])
        gelu_b1 = sb("gelu_b1", [P, HT1])
        b2_sum = sb("b2_sum", [P, 1])
        shared_b2 = sb("shared_b2", [P, 1])
        b2_all = sb("b2_all", [P, 1])
        every = sb("every", [P, 1])
        end_sum = sb("end_sum", [P, D])
        end_bias = sb("end_bias", [P, 2, D])

        u_ps = psum("u", [P, 3, CH])
        acc = psum("acc", [P, 2, CH])
        end = psum("end", [P, CT, D])
        misc = psum("misc", [P, CH])
        misc_bf = misc[0:3 * E1, 0:CH // 2].bitcast(BF16)

        once = sem("dve_once")
        s_gb1 = sem("gelu_b1_ready")
        s_every = sem("every_summed")
        s_everyd = sem("every_ready")
        chain = sem("dve_steps")
        s_var = sem("var_ready")
        s_rstd = sem("rstd_ready")
        s_xn = sem("xn_ready")
        s_T = sem("half_transposed")
        s_Tc = sem("half_kept")
        s_R = sem("scores_ready")
        s_Rc = sem("scores_kept")
        s_core = sem("core_ready")
        s_h = sem("h_ready")
        s_gh = sem("gelu_h_ready")
        s_shift = sem("shifted_ready")
        s_exp = sem("exp_ready")
        s_diff = sem("diff_ready")
        s_tanh = sem("tanh_ready")
        s_gp = sem("gate_parts_ready")
        s_GT = sem("gates_transposed")
        s_gT = sem("gates_kept")
        s_G = sem("gate_spread")
        s_Gc = sem("gate_spread_kept")
        s_u = sem("u_ready")
        s_gelu = sem("gelu_done")
        s_hid = sem("hidden_ready")
        s_down = sem("down_done")
        s_mixed = sem("mixed_ready")
        s_end = sem("end_ready")
        s_add = sem("chunk_added")

        NORM, CHOOSE, PICK, WEIGH = 3, 4, 9, 7
        STEPS = NORM + CHOOSE + PICK + WEIGH
        UNITS = HT1 + 1
        SH = HT1

        def tiles(c, t, n=1):
            return slice(c * CT + t, c * CT + t + n) if isinstance(c, int) else bass.ds(c * CT + t, n)

        def per_expert(a):
            return a.broadcast_to([P, CT, E1])

        block = ctx.enter_context(nc.Block())

        @block.vector
        def _(dve):
            def constants():
                dve.tensor_reduce(b2_sum[:, :], w["b2"][:, 0:E1], AX.X, ALU.add).then_inc(once, 1)
                dve.tensor_scalar(shared_b2[:, :], w["b2"][:, E1:E1 + 1], 0.1, None, ALU.mult).then_inc(once, 1)
                dve.tensor_tensor(end_sum[:, :], w["up_b"][:, :], w["core_b"][:, :], ALU.add).then_inc(once, 1)
                dve.wait_ge(once, 3)
                dve.tensor_tensor(b2_all[:, :], b2_sum[:, :], shared_b2[:, :], ALU.add).then_inc(once, 1)
                for r in range(2):
                    dve.tensor_scalar(end_bias[:, r, :], end_sum[:, :], 0.5, None, ALU.mult).then_inc(once, 1)
                dve.wait_ge(once, 6)
                dve.wait_ge(s_every, 1)
                dve.tensor_tensor(every[:, :], misc[:, 0:1], b2_all[:, :], ALU.add).then_inc(s_everyd, 1)

            def norm_stats(c):
                for t in range(CT):
                    last = dve.bn_stats(stats[:, t, :], x[:, tiles(c, t), :].rearrange("p a d -> p (a d)"))
                last.then_inc(chain, 1)
                dve.wait_ge(chain, c * STEPS + 1)
                dve.sem_inc(chain, 1)
                for t in range(CT):
                    last = dve.bn_aggr(mean_var[:, t, :], stats[:, t, :])
                last.then_inc(chain, 1)
                dve.wait_ge(chain, c * STEPS + 3)
                dve.tensor_scalar(var_eps[:, :], mean_var[:, :, 1], EPS, None, ALU.add).then_inc(s_var, 1)

            def norm_apply(c):
                dve.wait_ge(s_rstd, c + 1)
                dve.wait_ge(s_T, c * KD)
                for t in range(CT):
                    last = dve.tensor_scalar(xn[:, t, :], x[:, tiles(c, t), :].rearrange("p a d -> p (a d)"),
                                             mean_var[:, t, 0:1], rstd[:, t:t + 1], ALU.subtract, ALU.mult)
                last.then_inc(s_xn, 1)

            def choose(c):
                base = c * STEPS + NORM
                dve.wait_ge(s_R, c + 1)
                dve.tensor_tensor(biased[:, :, :], misc[:, 0:CT * E1].rearrange("p (t g) -> p t g", t=CT),
                                  per_expert(w["router_b"][:, :].rearrange("p (a e) -> p a e", a=1)), ALU.add).then_inc(s_Rc, 1)
                dve.wait_ge(s_Rc, c + 1)
                dve.tensor_tensor(logits[:, :, :], biased[:, :, :],
                                  per_expert(const["cost"][:, :].rearrange("p (a e) -> p a e", a=1)), ALU.subtract).then_inc(chain, 1)
                dve.wait_ge(chain, base + 1)
                dve.sem_inc(chain, 1)
                for t in range(CT):
                    last = dve.max(top[:, t, :], logits[:, t, :])
                last.then_inc(chain, 1)
                dve.wait_ge(chain, base + 3)
                dve.tensor_tensor(shifted[:, :, :], logits[:, :, :], per_expert(top[:, :, 0:1]), ALU.subtract).then_inc(s_shift, 1)
                dve.sem_inc(chain, 1)

            def pick(c):
                base = c * STEPS + NORM + CHOOSE
                dve.wait_ge(s_exp, c + 1)
                dve.tensor_reduce(total[:, :], expd[:, :, :], AX.X, ALU.add).then_inc(chain, 1)
                dve.wait_ge(chain, base + 1)
                dve.reciprocal(inverse[:, :], total[:, :]).then_inc(chain, 1)
                dve.wait_ge(chain, base + 2)
                dve.tensor_tensor(probs[:, :, :], expd[:, :, :],
                                  per_expert(inverse[:, :].rearrange("p (t a) -> p t a", a=1)), ALU.mult).then_inc(chain, 1)
                dve.wait_ge(chain, base + 3)
                dve.sem_inc(chain, 1)
                for t in range(CT):
                    last = dve.max(top_p[:, t, :], probs[:, t, :])
                last.then_inc(chain, 1)
                dve.wait_ge(chain, base + 5)
                dve.tensor_tensor(diff[:, :, :], top_p[:, :, 0:1], top_p[:, :, 1:2], ALU.subtract).then_inc(s_diff, 1)
                for t in range(CT):
                    last = dve.max_index(top_at[:, t, :], top_p[:, t, :], probs[:, t, :])
                last.then_inc(chain, 1)
                dve.wait_ge(chain, base + 6)
                dve.tensor_copy(at[:, :, :], top_at[:, :, 0:2]).then_inc(chain, 1)
                dve.wait_ge(chain, base + 7)
                for k in range(2):
                    dve.tensor_tensor(hit[:, k, :, :], per_expert(const["iota"][:, :].rearrange("p (a e) -> p a e", a=1)),
                                      per_expert(at[:, :, k:k + 1]), ALU.is_equal).then_inc(chain, 1)

            def weigh(c):
                base = c * STEPS + NORM + CHOOSE + PICK
                dve.wait_ge(s_tanh, c + 1)
                dve.tensor_scalar(weight[:, :, 0:1], tanh[:, :, :], 0.5, 0.5, ALU.mult, ALU.add)
                dve.tensor_scalar(weight[:, :, 1:2], tanh[:, :, :], -0.5, 0.5, ALU.mult, ALU.add).then_inc(chain, 1)
                dve.wait_ge(chain, base + 1)
                for k in range(2):
                    last = dve.tensor_tensor(hit[:, k, :, :], hit[:, k, :, :], per_expert(weight[:, :, k:k + 1]), ALU.mult)
                last.then_inc(chain, 1)
                dve.wait_ge(chain, base + 2)
                dve.tensor_tensor(gates[:, :, :], hit[:, 0, :, :], hit[:, 1, :, :], ALU.add).then_inc(chain, 1)
                dve.wait_ge(chain, base + 3)
                dve.wait_ge(s_GT, c)
                three_parts(dve, chain, base + 3, gates[:, :, :], gparts[:, :, 0:E1], rest[:, :, :],
                            gparts[:, :, E1:2 * E1], rest2[:, :, :], gparts[:, :, 2 * E1:3 * E1]).then_inc(s_gp, 1)

            def hidden(c, par, u):
                n = c * UNITS + u
                b = u % 3
                dve.wait_ge(s_gelu, n + 4)
                dve.wait_ge(s_down, n + 1)
                if u == SH:
                    dve.tensor_scalar(hid[:, b, :], act_out[:, b, :], 0.1, None, ALU.mult).then_inc(s_hid, 1)
                    return
                e = TILE_EXPERT[u]
                if u == TILE_EXPERT.index(e):
                    dve.wait_ge(s_Gc, c * E1 + e + 1)
                dve.scalar_tensor_tensor(out=hid[:, b, :], in0=act_out[:, b, :], scalar=gelu_b1[:, u:u + 1],
                                         in1=gate_bc[:, par, e, :], op0=ALU.subtract, op1=ALU.mult).then_inc(s_hid, 1)

            def mix(c, par):
                dve.wait_ge(s_down, c * UNITS + UNITS + 3)
                dve.wait_ge(s_end, c + 1)
                dve.tensor_scalar(mixed[:, :], acc[:, par, :], every[:, 0:1], None, ALU.add).then_inc(s_mixed, 1)

            def add(c):
                dve.wait_ge(s_end, c + 2)
                for t in range(0, CT, 2):
                    here = x[:, tiles(c, t, 2), :]
                    last = dve.scalar_tensor_tensor(out=here, in0=end[:, t:t + 2, :], scalar=0.5, in1=here,
                                                    op0=ALU.mult, op1=ALU.add)
                last.then_inc(s_add, 1)
                dve.wait_ge(s_add, 2 * c + 2)
                for t in range(0, CT, 2):
                    here = x[:, tiles(c, t, 2), :]
                    last = dve.tensor_tensor(here, here, end_bias[:, :, :], ALU.add)
                last.then_inc(s_add, 1)

            def chunk(c, par, last=False):
                for u in range(3, UNITS):
                    hidden(c, par, u)
                    if not last:
                        if u == 3:
                            norm_stats(c + 1)
                        if u == 4:
                            norm_apply(c + 1)
                        if u == 9:
                            choose(c + 1)
                        if u == 10:
                            pick(c + 1)
                        if u == 11:
                            weigh(c + 1)
                if not last:
                    hidden(c + 1, 1 - par, 0)
                mix(c, par)
                if not last:
                    hidden(c + 1, 1 - par, 1)
                    hidden(c + 1, 1 - par, 2)
                add(c)

            dve.sem_inc(s_hid, 3)
            dve.sem_inc(s_mixed, 2)
            dve.sem_inc(s_add, 1)
            constants()
            norm_stats(0)
            norm_apply(0)
            choose(0)
            pick(0)
            weigh(0)
            for u in range(3):
                hidden(0, 0, u)
            with dve.Fori(0, CHUNKS - 2, 2) as c:
                chunk(c, 0)
                chunk(c + 1, 1)
            chunk(CHUNKS - 2, 0)
            chunk(CHUNKS - 1, 1, last=True)

        @block.gpsimd
        def _(pool):
            with pool.Fori(0, CHUNKS) as c:
                pool.wait_ge(s_var, c + 1)
                pool.tensor_tensor(rstd[:, :], var_eps[:, :], const["minus_half"][:, 0:CT], ALU.pow).then_inc(s_rstd, 1)

        @block.scalar
        def _(act):
            def keep_half(c, k):
                act.wait_ge(s_T, c * KD + k + 1)
                act.wait_ge(s_h, c)
                act.activation(xnT[:, k, :], misc[:, :], ACT.Copy).then_inc(s_Tc, 1)

            def core_in(c, par):
                act.wait_ge(s_Tc, c * KD + KD)
                if not (isinstance(c, int) and c == 0):
                    act.wait_ge(s_end, c)
                for k in range(KD):
                    last = act.activation(core[:, par, k, :], xnT[:, k, :], ACT.Gelu)
                last.then_inc(s_core, 1)

            def h_in(c, par):
                act.wait_ge(s_h, c + 1)
                act.activation(gelu_h[:, par, :], misc[:, :], ACT.Gelu, bias=w["down_b"][:, 0:1]).then_inc(s_gh, 1)

            def exps(c):
                act.wait_ge(s_shift, c + 1)
                act.activation(expd[:, :, :], shifted[:, :, :], ACT.Exp).then_inc(s_exp, 1)

            def tanhs(c):
                act.wait_ge(s_diff, c + 1)
                act.activation(tanh[:, :, :], diff[:, :, :], ACT.Tanh, scale=0.5).then_inc(s_tanh, 1)

            def keep_gates(c):
                act.wait_ge(s_GT, c + 1)
                act.activation(gT[:, :], misc_bf, ACT.Copy).then_inc(s_gT, 1)

            def keep_spread(c, par, e):
                act.wait_ge(s_G, c * E1 + e + 1)
                act.activation(gate_bc[:, par, e, :], misc[:, :], ACT.Copy).then_inc(s_Gc, 1)

            def unit(c, u):
                n = c * UNITS + u
                act.wait_ge(s_u, n + 1)
                act.wait_ge(s_hid, n + 1)
                act.activation(act_out[:, u % 3, :], u_ps[:, u % 3, :], ACT.Gelu, bias=w["b1"][:, u:u + 1]).then_inc(s_gelu, 1)

            def chunk(c, par, last=False):
                for u in range(3, UNITS):
                    unit(c, u)
                    if not last:
                        if u == 5:
                            keep_half(c + 1, 0)
                        if u == 6:
                            keep_half(c + 1, 1)
                        if u == 7:
                            core_in(c + 1, 1 - par)
                        if u == 9:
                            h_in(c + 1, 1 - par)
                        if u == 10:
                            exps(c + 1)
                        if u == 11:
                            tanhs(c + 1)
                        if u == 12:
                            keep_gates(c + 1)
                        if u >= 13:
                            keep_spread(c + 1, 1 - par, u - 13)
                if not last:
                    for u in range(3):
                        unit(c + 1, u)

            act.activation(gelu_b1[:, :], w["b1"][:, 0:HT1], ACT.Gelu).then_inc(s_gb1, 1)
            act.sem_inc(s_gelu, 3)
            for k in range(KD):
                keep_half(0, k)
            core_in(0, 0)
            h_in(0, 0)
            exps(0)
            tanhs(0)
            keep_gates(0)
            for e in range(E1):
                keep_spread(0, 0, e)
            for u in range(3):
                unit(0, u)
            with act.Fori(0, CHUNKS - 2, 2) as c:
                chunk(c, 0)
                chunk(c + 1, 1)
            chunk(CHUNKS - 2, 0)
            chunk(CHUNKS - 1, 1, last=True)

        @block.tensor
        def _(pe):
            def constants():
                pe.wait_ge(s_gb1, 1)
                for u in range(HT1):
                    last = pe.matmul(misc[:, 0:1], w["w2"][:, u, :], gelu_b1[:, u:u + 1], start=(u == 0), stop=(u == HT1 - 1))
                last.then_inc(s_every, 1)
                pe.wait_ge(s_everyd, 1)

            def turn_half(c, k):
                if k == 0:
                    pe.wait_ge(s_xn, c + 1)
                    pe.wait_ge(s_Gc, c * E1)
                else:
                    pe.wait_ge(s_Tc, c * KD + k)
                for t in range(CT):
                    last = pe.transpose(misc[:, t * P:(t + 1) * P], xn[:, t, k * P:(k + 1) * P], const["ident"][:, :])
                last.then_inc(s_T, 1)

            def route(c):
                pe.wait_ge(s_Tc, c * KD + KD)
                for t in range(CT):
                    for k in range(KD):
                        last = pe.matmul(misc[:, t * E1:(t + 1) * E1], xnT[:, k, t * P:(t + 1) * P],
                                         w["router"][:, k, :], start=(k == 0), stop=(k == KD - 1))
                last.then_inc(s_R, 1)

            def h_out(c):
                pe.wait_ge(s_Rc, c + 1)
                pe.wait_ge(s_core, c + 1)
                for k in range(KD):
                    last = pe.matmul(misc[:, :], w["down_w"][:, k, :], xnT[:, k, :], start=(k == 0), stop=(k == KD - 1))
                last.then_inc(s_h, 1)

            def turn_gates(c):
                pe.wait_ge(s_gh, c + 1)
                pe.wait_ge(s_gp, c + 1)
                for t in range(CT):
                    last = pe.transpose(misc_bf[:, t * P:(t + 1) * P], gparts[:, t, :], const["ident_bf"][:, :])
                last.then_inc(s_GT, 1)

            def spread(c, e):
                if e == 0:
                    pe.wait_ge(s_gT, c + 1)
                else:
                    pe.wait_ge(s_Gc, c * E1 + e)
                pe.matmul(misc[:, :], const["pick_gate1"][:, e, :], gT[:, :], start=True, stop=True).then_inc(s_G, 1)

            def up(c, par, u):
                n = c * UNITS + u
                if u == 0:
                    pe.wait_ge(s_gh, c + 1)
                pe.wait_ge(s_gelu, n + 1)
                pe.matmul(u_ps[:, u % 3, :], w["w1"][:, u, :], gelu_h[:, par, :], start=True, stop=True).then_inc(s_u, 1)

            def down(c, par, u):
                n = c * UNITS + u
                if u == 0:
                    pe.wait_ge(s_mixed, c + 1)
                pe.wait_ge(s_hid, n + 4)
                pe.matmul(acc[:, par, :], w["w2"][:, u, :], hid[:, u % 3, :],
                          start=(u == 0), stop=(u == UNITS - 1)).then_inc(s_down, 1)

            def finish(c, par):
                pe.wait_ge(s_mixed, c + 3)
                pe.wait_ge(s_add, 2 * c + 1)
                for t in range(CT):
                    for k in range(KD):
                        pe.matmul(end[:, t, :], core[:, par, k, t * P:(t + 1) * P], w["core_w"][:, k, :],
                                  start=(k == 0 and t % 2 == 0), stop=False, skip_group_check=True)
                    last = pe.matmul(end[:, t, :], mixed[:, t * P:(t + 1) * P], w["up_w"][:, :],
                                     start=False, stop=True, skip_group_check=True)
                last.then_inc(s_end, 1)

            def chunk(c, par, last=False):
                down(c, par, 0)
                for u in range(3, UNITS):
                    up(c, par, u)
                    down(c, par, u - 2)
                    if not last:
                        if u == 5:
                            turn_half(c + 1, 0)
                        if u == 6:
                            turn_half(c + 1, 1)
                        if u == 7:
                            route(c + 1)
                        if u == 9:
                            h_out(c + 1)
                        if u == 12:
                            turn_gates(c + 1)
                        if u >= 13:
                            spread(c + 1, u - 13)
                if not last:
                    up(c + 1, 1 - par, 0)
                down(c, par, UNITS - 2)
                if not last:
                    up(c + 1, 1 - par, 1)
                down(c, par, UNITS - 1)
                if not last:
                    up(c + 1, 1 - par, 2)
                finish(c, par)

            pe.sem_inc(s_down, 3)
            pe.sem_inc(s_end, 1)
            constants()
            turn_half(0, 0)
            turn_half(0, 1)
            route(0)
            h_out(0)
            turn_gates(0)
            for e in range(E1):
                spread(0, e)
            for u in range(3):
                up(0, 0, u)
            with pe.Fori(0, CHUNKS - 2, 2) as c:
                chunk(c, 0)
                chunk(c + 1, 1)
            chunk(CHUNKS - 2, 0)
            chunk(CHUNKS - 1, 1, last=True)


def attention_inputs(nc, tag, x, w, const, qk_parts, v_rows):
    with ExitStack() as ctx:
        ctx.enter_context(nc.cleanup_on_exit())

        def sb(name, shape, dt=F32):
            return ctx.enter_context(nc.sbuf_tensor(f"{tag}_{name}", shape, dt))

        def psum(name, shape, dt=F32):
            return ctx.enter_context(nc.psum_tensor(f"{tag}_{name}", shape, dt))

        def sem(name):
            return nc.alloc_semaphore(f"{tag}_{name}")

        xn = sb("xn", [P, CT, D])
        xnT = sb("xnT", [P, KD, CH])
        stats = sb("stats", [P, CT, 6])
        mean_var = sb("mean_var", [P, CT, 2])
        var_eps = sb("var_eps", [P, CT])
        rstd = sb("rstd", [P, CT])
        rest = sb("rest", [P, 2, 2, CH])
        parts = sb("parts", [P, 2, 3, CH], BF16)
        v_pad = sb("v_pad", [P, CT, HEADS, 2 * DH])

        half = psum("half", [P, 2, CH])
        qk = psum("qk", [P, 4, CH])
        v_ps = psum("v", [P, 2, 2, D])

        s_stat = sem("stats_ready")
        s_mv = sem("mean_var_ready")
        s_var = sem("var_ready")
        s_rstd = sem("rstd_ready")
        s_xn = sem("xn_ready")
        s_T = sem("half_transposed")
        s_Tc = sem("half_kept")
        s_qk = sem("qk_ready")
        s_v = sem("v_ready")
        s_p1 = sem("part1_ready")
        chain = sem("dve_steps")
        s_parts = sem("parts_ready")
        s_pad = sem("v_kept")
        s_pads = sem("v_pad_set")
        s_st = [sem("parts_stored_even"), sem("parts_stored_odd")]
        s_vst = sem("v_stored")

        TQ = 4

        def tiles(c, t, n=1):
            return slice(c * CT + t, c * CT + t + n) if isinstance(c, int) else bass.ds(c * CT + t, n)

        block = ctx.enter_context(nc.Block())

        @block.vector
        def _(dve):
            def chunk(c):
                for t in range(CT):
                    last = dve.bn_stats(stats[:, t, :], x[:, tiles(c, t), :].rearrange("p a d -> p (a d)"))
                last.then_inc(s_stat, 1)
                dve.wait_ge(s_stat, c + 1)
                dve.sem_inc(s_mv, 1)
                for t in range(CT):
                    last = dve.bn_aggr(mean_var[:, t, :], stats[:, t, :])
                last.then_inc(s_mv, 1)
                dve.wait_ge(s_mv, 2 * c + 2)
                dve.tensor_scalar(var_eps[:, :], mean_var[:, :, 1], EPS, None, ALU.add).then_inc(s_var, 1)
                dve.wait_ge(s_rstd, c + 1)
                dve.wait_ge(s_T, c * KD)
                for t in range(CT):
                    last = dve.tensor_scalar(xn[:, t, :], x[:, tiles(c, t), :].rearrange("p a d -> p (a d)"),
                                             mean_var[:, t, 0:1], rstd[:, t:t + 1], ALU.subtract, ALU.mult)
                last.then_inc(s_xn, 1)
                for m in range(TQ):
                    b = m % 2
                    dve.wait_ge(s_p1, c * TQ + m + 1)
                    dve.tensor_tensor(rest[:, b, 0, :], qk[:, m, :], parts[:, b, 0, :], ALU.subtract).then_inc(chain, 1)
                    dve.wait_ge(chain, c * TQ * 3 + 3 * m + 1)
                    dve.tensor_copy(parts[:, b, 1, :], rest[:, b, 0, :]).then_inc(chain, 1)
                    dve.wait_ge(chain, c * TQ * 3 + 3 * m + 2)
                    dve.tensor_tensor(rest[:, b, 1, :], rest[:, b, 0, :], parts[:, b, 1, :], ALU.subtract).then_inc(chain, 1)
                    dve.wait_ge(chain, c * TQ * 3 + 3 * m + 3)
                    dve.tensor_copy(parts[:, b, 2, :], rest[:, b, 1, :]).then_inc(s_parts, 1)

            chunk(0)
            with dve.Fori(1, CHUNKS) as c:
                chunk(c)

        @block.gpsimd
        def _(pool):
            pool.memset(v_pad[:, :, :, :], 0.0).then_inc(s_pads, 1)
            pool.wait_ge(s_pads, 1)
            pool.memset(v_pad[:, :, :, DH:DH + 1], 1.0).then_inc(s_pads, 1)
            def chunk(c):
                pool.wait_ge(s_var, c + 1)
                pool.tensor_tensor(rstd[:, :], var_eps[:, :], const["minus_half"][:, 0:CT], ALU.pow).then_inc(s_rstd, 1)

            chunk(0)
            with pool.Fori(1, CHUNKS) as c:
                chunk(c)

        @block.scalar
        def _(act):
            act.wait_ge(s_pads, 2)
            def chunk(c):
                for k in range(KD):
                    act.wait_ge(s_T, c * KD + k + 1)
                    act.wait_ge(s_v, 2 * c)
                    act.activation(xnT[:, k, :], half[:, k, :], ACT.Copy).then_inc(s_Tc, 1)
                for m in range(TQ):
                    act.wait_ge(s_qk, c * TQ + m + 1)
                    act.wait_ge(s_st[m % 2], 48 * (2 * c + m // 2))
                    act.activation(parts[:, m % 2, 0, :], qk[:, m, :], ACT.Copy).then_inc(s_p1, 1)
                act.wait_ge(s_vst, 16 * c)
                for r in range(2):
                    act.wait_ge(s_v, 2 * c + r + 1)
                    act.activation(v_pad[:, 2 * r:2 * r + 2, :, 0:DH],
                                   v_ps[:, r, :, :].rearrange("p a (h d) -> p a h d", d=DH), ACT.Copy).then_inc(s_pad, 1)

            chunk(0)
            with act.Fori(1, CHUNKS) as c:
                chunk(c)

        @block.tensor
        def _(pe):
            def chunk(c):
                pe.wait_ge(s_xn, c + 1)
                for k in range(KD):
                    pe.wait_ge(s_Tc, c * KD)
                    for t in range(CT):
                        last = pe.transpose(half[:, k, t * P:(t + 1) * P], xn[:, t, k * P:(k + 1) * P], const["ident"][:, :])
                    last.then_inc(s_T, 1)
                pe.wait_ge(s_Tc, c * KD + KD)
                pe.wait_ge(s_parts, c * TQ)
                for m in range(TQ):
                    weight = w["wq"] if m < 2 else w["wk"]
                    for k in range(KD):
                        last = pe.matmul(qk[:, m, :], weight[:, k, (m % 2) * P:(m % 2 + 1) * P], xnT[:, k, :],
                                         start=(k == 0), stop=(k == KD - 1))
                    last.then_inc(s_qk, 1)
                pe.wait_ge(s_pad, 2 * c)
                for r in range(2):
                    for a in range(2):
                        t = 2 * r + a
                        for k in range(KD):
                            last = pe.matmul(v_ps[:, r, a, :], xnT[:, k, t * P:(t + 1) * P], w["wv"][:, k, :],
                                             start=(k == 0), stop=(k == KD - 1))
                    last.then_inc(s_v, 1)

            chunk(0)
            with pe.Fori(1, CHUNKS) as c:
                chunk(c)

        @block.sync
        def _(sp):
            rows = v_rows.rearrange("(n p) f -> p n f", p=P)
            def chunk(c):
                for m in range(TQ):
                    sp.wait_ge(s_parts, c * TQ + m + 1)
                    for j in range(3):
                        sp.dma_start(qk_parts[m // 2, j, (m % 2) * P:(m % 2 + 1) * P, slice(c * CH, (c + 1) * CH) if isinstance(c, int) else bass.ds(c * CH, CH)],
                                     parts[:, m % 2, j, :]).then_inc(s_st[m % 2], 16)
                sp.wait_ge(s_pad, 2 * c + 2)
                sp.dma_start(rows[:, tiles(c, 0, CT), :],
                             v_pad[:, :, :, :].rearrange("p t h d -> p t (h d)")).then_inc(s_vst, 16)

            chunk(0)
            with sp.Fori(1, CHUNKS) as c:
                chunk(c)
            for s in s_st:
                sp.wait_ge(s, 48 * 2 * CHUNKS)
            sp.wait_ge(s_vst, 16 * CHUNKS)


Q_PART = [0, 0, 1, 1, 0, 2]
K_PART = [0, 1, 0, 1, 2, 0]
QK_ROWS = len(Q_PART) * DH
M_ROWS = 3


def attention(nc, tag, x, w, const, qk_parts, v_rows):
    with ExitStack() as ctx:
        ctx.enter_context(nc.cleanup_on_exit())

        def sb(name, shape, dt=F32):
            return ctx.enter_context(nc.sbuf_tensor(f"{tag}_{name}", shape, dt))

        def psum(name, shape, dt=F32):
            return ctx.enter_context(nc.psum_tensor(f"{tag}_{name}", shape, dt))

        def sem(name):
            return nc.alloc_semaphore(f"{tag}_{name}")

        STEPS = B * HG
        HALF = 512
        qs = [sb(f"q_stack{i}", [QK_ROWS + M_ROWS, GH, T], BF16) for i in range(2)]
        ks = [sb(f"k_stack{i}", [QK_ROWS + M_ROWS, GH, T], BF16) for i in range(2)]
        vg = [sb(f"v_group{i}", [P, BT, P]) for i in range(2)]
        masked = [sb(f"masked{i}", [P, GH, BT, P]) for i in range(2)]
        probs = sb("probs", [P, 2, GH, T])
        max_of = sb("max_of", [P, 2, GH, BT])
        max_diag = sb("max_diag", [P, GH, BT])
        max_half = sb("max_half", [P, GH * BT])
        row_max = sb("row_max", [P, GH * BT])
        m_rest = sb("m_rest", [P, 2, GH * BT])
        m_parts = sb("m_parts", [P, M_ROWS, GH * BT], BF16)
        m_rows = sb("m_rows", [M_ROWS * GH * BT, P], BF16)
        exp_m = sb("exp_m", [P, T])
        v_later = sb("v_later", [P, BT])
        out_sum = sb("out_sum", [P, T])
        inv = sb("inv", [P, BT, GH])
        inv_wide = sb("inv_wide", [P, BT, GH, P // GH])
        out_n = sb("out_n", [P, T])

        a_ps = psum("a", [P, 2, HALF])
        b_ps = psum("b", [P, 3, HALF])
        o_ps = psum("o", [P, T])
        misc = psum("misc", [P, HALF])
        misc_bf = misc[0:M_ROWS * GH * BT, 0:P // 2].bitcast(BF16)

        A_UNITS = {i: [(h, lo, min(lo + HALF, P * (i + 1))) for h in range(GH) for lo in range(0, P * (i + 1), HALF)]
                   for i in range(BT)}
        B_UNITS = {j: [(h, lo, (lo // HALF + 1) * HALF) for h in range(GH)
                       for lo in ([P * j, HALF] if j < BT // 2 else [P * j])] for j in range(BT)}
        A_FIRST = [sum(len(A_UNITS[i]) for i in range(n)) for n in range(BT + 1)]
        B_FIRST = [sum(len(B_UNITS[j]) for j in range(n)) for n in range(BT + 1)]
        BESIDE = {1: [0, 1, 2], 2: [3], 3: [4], 4: [5], 5: [6], 6: [7]}
        DEN, INV0, INV1, PROJ0, EXPM0, PROJ1, EXPM1, PROJ2, LATER, PROJ3, MAXT = range(11)
        BEFORE = (DEN, INV0, INV1, PROJ0, PROJ1, PROJ2, PROJ3)
        TASKS = {0: [DEN], 1: [INV0], 2: [INV1], 3: [PROJ0, EXPM0], 4: [PROJ1, EXPM1], 5: [PROJ2, LATER], 6: [PROJ3], 7: [MAXT]}
        NT = 11

        s_ld = [sem("stacks_loaded_even"), sem("stacks_loaded_odd")]
        s_ones = sem("constants_set")
        s_A = sem("a_scores_ready")
        s_Ac = sem("a_scores_used")
        s_diag = sem("diag_begun")
        s_em = sem("exp_max_begun")
        chain = sem("dve_steps")
        s_mp = sem("max_parts_ready")
        s_m = [sem("max_rows_even"), sem("max_rows_odd")]
        s_B = sem("b_scores_ready")
        s_exp = sem("b_scores_used")
        s_pv = sem("tile_multiplied")
        s_sum = sem("out_sum_ready")
        s_fill = sem("misc_filled")
        s_used = sem("misc_used")
        s_invw = sem("inv_wide_ready")
        s_on = sem("out_normalised")

        def task(it, k):
            if isinstance(it, int) and it == 0:
                return 1 + [EXPM0, EXPM1, LATER, MAXT].index(k)
            if isinstance(it, int) and it == STEPS:
                return it * NT - 6 - 1 + BEFORE.index(k)
            return it * NT - 6 + k

        def group(it):
            return (it % HG) if isinstance(it, int) else it % HG

        block = ctx.enter_context(nc.Block())

        @block.sync
        def _(sp):
            rows = v_rows.rearrange("(n p) f -> p n f", p=P)

            def load(it, par):
                b, g = it // HG, it % HG
                for stack, which, order in ((qs, 0, Q_PART), (ks, 1, K_PART)):
                    for s, part in enumerate(order):
                        sp.dma_start(stack[par][s * DH:(s + 1) * DH, :, :],
                                     qk_parts[which, part, bass.ds(g * GH * DH, GH * DH), bass.ds(b * T, T)]
                                     .rearrange("(h d) t -> d h t", d=DH)).then_inc(s_ld[par], 16)
                sp.dma_start(vg[par][:, :, :], rows[:, bass.ds(b * BT, BT), bass.ds(g * P, P)]).then_inc(s_ld[par], 16)

            def max_rows(it, par):
                sp.wait_ge(s_used, task(it - 1, MAXT) + 1 if not (isinstance(it, int) and it == 0) else 1)
                for j in range(M_ROWS):
                    sp.dma_start(qs[par][QK_ROWS + j:QK_ROWS + j + 1, :, :].rearrange("a h t -> a (h t)"),
                                 m_rows[j * GH * BT:(j + 1) * GH * BT, :]).then_inc(s_m[par], 16)

            def step(it, par, last=False, load_next=True):
                if not last:
                    max_rows(it + 1, 1 - par)
                if load_next:
                    sp.wait_ge(s_pv, it * BT + BT + 2)
                    load(it + 2, par)

            load(0, 0)
            load(1, 1)
            max_rows(0, 0)
            step(0, 0)
            step(1, 1)
            with sp.Fori(1, STEPS // 2 - 1) as pair:
                it = pair * 2
                step(it, 0)
                step(it + 1, 1)
            step(STEPS - 2, 0, load_next=False)

        @block.scalar
        def _(act):
            def exps(it, j):
                act.wait_ge(s_pv, it * BT + j + 1)
                for n, (h, lo, hi) in enumerate(B_UNITS[j], B_FIRST[j]):
                    act.wait_ge(s_B, it * B_FIRST[BT] + n + 1)
                    act.activation(probs[:, j % 2, h, lo:hi], b_ps[:, n % 3, lo % HALF:(hi - 1) % HALF + 1],
                                   ACT.Exp, scale=float(T) ** -0.5).then_inc(s_exp, 1)

            def tasks(it, j, first, last):
                for k in TASKS[j]:
                    if k in (EXPM0, EXPM1):
                        c = (k == EXPM1) * HALF
                        act.wait_ge(s_fill, task(it, k) + 1)
                        if not first:
                            act.wait_ge(s_sum, it)
                        act.activation(exp_m[:, c:c + HALF], misc[:, :], ACT.Exp, scale=float(T) ** -0.5).then_inc(s_used, 1)
                    if k == MAXT and not last:
                        keep_max(it + 1)

            def keep_max(it):
                act.wait_ge(s_fill, task(it - 1, MAXT) + 1 if not (isinstance(it, int) and it == 0) else 1)
                if not (isinstance(it, int) and it == 0):
                    act.wait_ge(s_B, (it - 1) * B_FIRST[BT] + 1)
                act.activation(m_rows[:, :], misc_bf, ACT.Copy).then_inc(s_used, 1)

            def step(it, first=False, last=False):
                for j in range(BT):
                    exps(it, j)
                    tasks(it, j, first, last)

            act.sem_inc(s_exp, 3)
            keep_max(0)
            step(0, first=True)
            step(1)
            with act.Fori(1, STEPS // 2 - 1) as pair:
                it = pair * 2
                step(it)
                step(it + 1)
            step(STEPS - 2)
            step(STEPS - 1, last=True)

        @block.vector
        def _(dve):
            def maxima(it, par, i):
                for n, (h, lo, hi) in enumerate(A_UNITS[i], A_FIRST[i]):
                    bank = a_ps[:, n % 2, :]
                    dve.wait_ge(s_A, it * A_FIRST[BT] + n + 1)
                    full = min(hi, P * i) - lo
                    last = None
                    if full > 0:
                        last = dve.tensor_reduce(max_of[:, lo // HALF, h, i:i + 1], bank[:, 0:full], AX.X, ALU.max)
                    if hi == P * (i + 1):
                        if full <= 0:
                            dve.sem_inc(s_diag, 1)
                        last = dve.tensor_tensor_reduce(masked[par][:, h, i, :], bank[:, hi - P - lo:hi - lo], const["causal"][:, :],
                                                        1.0, 0.0 if i < BT - 1 else -3e38, ALU.mult, ALU.max,
                                                        max_diag[:, h, i:i + 1])
                    last.then_inc(s_Ac, 1)

            M_STEPS = 6

            def finish_maxima(it):
                base = it * M_STEPS
                flat = lambda a: a.rearrange("p h i -> p (h i)")
                dve.wait_ge(s_Ac, it * A_FIRST[BT] + A_FIRST[BT] + 2)
                dve.tensor_tensor(max_half[:, :], flat(max_of[:, 0, :, :]), flat(max_of[:, 1, :, :]), ALU.max).then_inc(chain, 1)
                dve.wait_ge(chain, base + 1)
                dve.tensor_tensor(row_max[:, :], max_half[:, :], flat(max_diag[:, :, :]), ALU.max).then_inc(chain, 1)
                dve.wait_ge(chain, base + 2)
                three_parts(dve, chain, base + 2, row_max[:, :], m_parts[:, 0, :], m_rest[:, 0, :],
                            m_parts[:, 1, :], m_rest[:, 1, :], m_parts[:, 2, :]).then_inc(s_mp, 1)

            def sum_up(it):
                dve.wait_ge(s_pv, it * BT + BT + 2)
                dve.wait_ge(s_used, task(it, LATER) + 1)
                dve.wait_ge(s_on, 2 * it)
                for i in range(BT):
                    c = slice(i * P, (i + 1) * P)
                    last = dve.scalar_tensor_tensor(out=out_sum[:, c], in0=exp_m[:, c], scalar=v_later[:, i:i + 1],
                                                    in1=o_ps[:, c], op0=ALU.mult, op1=ALU.add)
                last.then_inc(s_sum, 1)

            def tasks(it, j, first, only_before=False):
                for k in TASKS[j]:
                    if (first and k in BEFORE) or (only_before and k not in BEFORE):
                        continue
                    here = (lambda: dve.wait_ge(s_fill, task(it, k) + 1))
                    if k == DEN:
                        here()
                        dve.reciprocal(inv[:, :, :].rearrange("p i h -> p (i h)"), misc[:, 0:BT * GH]).then_inc(s_used, 1)
                        dve.wait_ge(s_used, task(it, k) + 1)
                        dve.tensor_copy(inv_wide[:, :, :, :].rearrange("p i h d -> p (i h) d"),
                                        inv[:, :, :].rearrange("p i (h a) -> p (i h) a", a=1).broadcast_to([P, BT * GH, P // GH])
                                        ).then_inc(s_invw, 1)
                    if k in (INV0, INV1):
                        here()
                        c = slice((k - INV0) * HALF, (k - INV0 + 1) * HALF)
                        dve.tensor_tensor(out_n[:, c], out_sum[:, c], misc[:, :], ALU.mult).then_inc(s_on, 1)
                        dve.wait_ge(s_on, 2 * (it - 1) + k - INV0 + 1)
                        dve.sem_inc(s_used, 1)
                    if k in (PROJ0, PROJ1, PROJ2, PROJ3):
                        here()
                        p = [PROJ0, PROJ1, PROJ2, PROJ3].index(k)
                        b = (it - 1) // HG
                        where = x[:, bass.ds(b * BT + 2 * p, 2), :]
                        dve.tensor_tensor(where, misc[:, :].rearrange("p (a d) -> p a d", a=2), where, ALU.add).then_inc(s_used, 1)
                    if k == LATER:
                        here()
                        dve.tensor_copy(v_later[:, :], misc[:, 0:BT]).then_inc(s_used, 1)

            def step(it, par, first=False, last=False):
                for j in range(BT):
                    if j == 0 and not first:
                        sum_up(it - 1)
                    tasks(it, j, first)
                    if not last:
                        for i in BESIDE.get(j, ()):
                            maxima(it + 1, 1 - par, i)
                        if j == 6:
                            finish_maxima(it + 1)

            dve.memset(max_of[:, :, :, :], -3e38).then_inc(s_ones, 1)
            for i in range(2):
                dve.memset(ks[i][QK_ROWS:QK_ROWS + M_ROWS, :, :], -1.0).then_inc(s_ones, 1)
            dve.sem_inc(s_Ac, 2)
            dve.wait_ge(s_ones, 3)
            for i in range(BT):
                maxima(0, 0, i)
            finish_maxima(0)
            step(0, 0, first=True)
            step(1, 1)
            with dve.Fori(1, STEPS // 2 - 1) as pair:
                it = pair * 2
                step(it, 0)
                step(it + 1, 1)
            step(STEPS - 2, 0)
            step(STEPS - 1, 1, last=True)
            sum_up(STEPS - 1)
            for j in range(BT - 1):
                tasks(STEPS, j, False, only_before=True)

        @block.tensor
        def _(pe):
            def scores_a(it, par, i):
                if i == 0:
                    pe.wait_ge(s_ld[par], 13 * 16 * (it // 2 + 1))
                for n, (h, lo, hi) in enumerate(A_UNITS[i], A_FIRST[i]):
                    pe.wait_ge(s_Ac, it * A_FIRST[BT] + n + 1)
                    pe.matmul(a_ps[:, n % 2, 0:hi - lo], qs[par][0:QK_ROWS, h, i * P:(i + 1) * P],
                              ks[par][0:QK_ROWS, h, lo:hi], start=True, stop=True).then_inc(s_A, 1)

            def scores_b(it, par, j):
                if j == 0:
                    pe.wait_ge(s_m[par], 16 * M_ROWS * (it // 2 + 1))
                for n, (h, lo, hi) in enumerate(B_UNITS[j], B_FIRST[j]):
                    pe.wait_ge(s_exp, it * B_FIRST[BT] + n + 1)
                    bank, at = b_ps[:, n % 3, :], lo
                    m_only = slice(QK_ROWS, QK_ROWS + M_ROWS)
                    if lo == P * j:
                        c = slice(lo % HALF, lo % HALF + P)
                        pe.matmul(bank[:, c], masked[par][:, h, j, :], const["ident"][:, :], is_transpose=True,
                                  start=True, stop=False)
                        last = pe.matmul(bank[:, c], ks[par][m_only, h, lo:lo + P], qs[par][m_only, h, lo:lo + P],
                                         start=False, stop=True)
                        at = lo + P
                    if at < hi:
                        last = pe.matmul(bank[:, at % HALF:at % HALF + hi - at], ks[par][:, h, j * P:(j + 1) * P],
                                         qs[par][:, h, at:hi], start=True, stop=True)
                    last.then_inc(s_B, 1)

            def values(it, par, j):
                if j == 0:
                    pe.wait_ge(s_sum, it)
                pe.wait_ge(s_exp, it * B_FIRST[BT] + B_FIRST[j + 1] + 3)
                for half in range(2):
                    for h, lo, hi in B_UNITS[j]:
                        if lo // HALF != half:
                            continue
                        last = pe.matmul(o_ps[32 * h:32 * h + 32, lo:hi], vg[par][:, j, 32 * h:32 * h + 32],
                                         probs[:, j % 2, h, lo:hi], start=(j == 0),
                                         stop=(j == (BT // 2 - 1 if half == 0 else BT - 1)), skip_group_check=True)
                last.then_inc(s_pv, 1)

            def turn_max(it):
                pe.wait_ge(s_mp, it + 1)
                pe.transpose(misc_bf, m_parts[:, :, :].rearrange("p j n -> p (j n)"), const["ident_bf"][:, :]).then_inc(s_fill, 1)

            def tasks(it, par, j, first, last, only_before=False):
                for k in TASKS[j]:
                    if (first and k in BEFORE) or (last and k == MAXT) or (only_before and k not in BEFORE):
                        continue
                    pe.wait_ge(s_used, task(it, k))
                    if k == DEN:
                        pe.wait_ge(s_sum, it)
                        for i in range(BT):
                            mm = pe.matmul(misc[:, i * GH:(i + 1) * GH], out_sum[:, i * P:(i + 1) * P], const["pick_den"][:, :],
                                           start=True, stop=True)
                    if k in (INV0, INV1):
                        pe.wait_ge(s_invw, it)
                        for i in range(BT // 2):
                            mm = pe.matmul(misc[:, i * P:(i + 1) * P],
                                           inv_wide[:, (k - INV0) * (BT // 2) + i, :, :].rearrange("p h d -> p (h d)"),
                                           const["ident"][:, :], start=True, stop=True)
                    if k in (PROJ0, PROJ1, PROJ2, PROJ3):
                        pe.wait_ge(s_on, 2 * it)
                        p = [PROJ0, PROJ1, PROJ2, PROJ3].index(k)
                        g = (it - 1) % HG
                        for a in range(2):
                            i = 2 * p + a
                            mm = pe.matmul(misc[:, a * D:(a + 1) * D], out_n[:, i * P:(i + 1) * P],
                                           w["wo"][:, bass.ds(g, 1), :].rearrange("p a d -> p (a d)"), start=True, stop=True)
                    if k in (EXPM0, EXPM1):
                        c = (k == EXPM1) * HALF
                        pe.sem_inc(s_em, 1)
                        for h in range(GH):
                            mm = pe.matmul(misc[32 * h:32 * h + 32, :], ks[par][QK_ROWS:QK_ROWS + M_ROWS, h, 0:32],
                                           qs[par][QK_ROWS:QK_ROWS + M_ROWS, h, c:c + HALF], start=True, stop=True)
                    if k == LATER:
                        for t in range(1, BT):
                            mm = pe.matmul(misc[:, 0:BT], vg[par][:, t, :], const["later"][:, t, :],
                                           start=(t == 1), stop=(t == BT - 1))
                    if k == MAXT:
                        turn_max(it + 1)
                        continue
                    mm.then_inc(s_fill, 1)

            def step(it, par, first=False, last=False):
                for j in range(BT):
                    scores_b(it, par, j)
                    if j:
                        values(it, par, j - 1)
                    tasks(it, par, j, first, last)
                    if not last:
                        for i in BESIDE.get(j, ()):
                            scores_a(it + 1, 1 - par, i)
                values(it, par, BT - 1)

            pe.sem_inc(s_pv, 2)
            pe.wait_ge(s_ones, 3)
            for i in range(BT):
                scores_a(0, 0, i)
            turn_max(0)
            step(0, 0, first=True)
            step(1, 1)
            with pe.Fori(1, STEPS // 2 - 1) as pair:
                pe.get_value_cache().nocache = True
                it = pair * 2
                step(it, 0)
                step(it + 1, 1)
            step(STEPS - 2, 0)
            step(STEPS - 1, 1, last=True)
            for j in range(BT - 1):
                tasks(STEPS, 0, j, False, True, only_before=True)


def scan_mixer(nc, tag, x, w, const):
    with ExitStack() as ctx:
        ctx.enter_context(nc.cleanup_on_exit())

        def sb(name, shape, dt=F32):
            return ctx.enter_context(nc.sbuf_tensor(f"{tag}_{name}", shape, dt))

        def psum(name, shape, dt=F32):
            return ctx.enter_context(nc.psum_tensor(f"{tag}_{name}", shape, dt))

        def sem(name):
            return nc.alloc_semaphore(f"{tag}_{name}")

        N2 = 2 * STATES
        SLOTS = KD * STATES
        a_exp = sb("a_exp", [P, KD, STATES])
        a_neg = sb("a_neg", [P, KD, STATES])
        xn = sb("xn", [P, CT, D])
        stats = sb("stats", [P, CT, 6])
        mean_var = sb("mean_var", [P, CT, 2])
        var_eps = sb("var_eps", [P, CT])
        rstd = sb("rstd", [P, CT])
        xnT = sb("xnT", [P, 2, KD, CH])
        low = sb("low", [RANK, CH])
        bc_rest = sb("bc_rest", [P, 2, CT, N2])
        bc_parts = sb("bc_parts", [P, CT, 3 * N2], BF16)
        bcT = sb("bcT", [3 * N2, 2, CH], BF16)
        z = sb("z", [P, KD, CH])
        z_abs = sb("z_abs", [P, KD, CH])
        z_exp = sb("z_exp", [P, KD, CH])
        z_log = sb("z_log", [P, KD, CH])
        delta = sb("delta", [P, 2, KD, CH])
        du = sb("du", [P, 2, KD, CH])
        decay = sb("decay", [P, 4, CH])
        drive = sb("drive", [P, 4, CH])
        h = sb("h", [P, 4, CH])
        state = sb("state", [P, SLOTS])
        c_bc = sb("c_bc", [P, 2, CH])
        hc = sb("hc", [P, 4, CH])
        y_out = sb("y_out", [P, KD, CH])

        b_ps = psum("b", [P, 2, CH])
        c_ps = psum("c", [P, CH])
        y_ps = psum("y", [P, KD, CH])
        misc = [psum(f"misc{i}", [P, CH]) for i in range(3)]

        once = sem("a_ready")
        s_stat = sem("stats_ready")
        s_mv = sem("mean_var_ready")
        s_var = sem("var_ready")
        s_rstd = sem("rstd_ready")
        s_xn = sem("xn_ready")
        s_fill = sem("misc_filled")
        s_act = sem("misc_used_by_act")
        s_dve = sem("misc_used_by_dve")
        chain = sem("part_steps")
        s_bcp = sem("bc_parts_ready")
        s_abs = sem("z_abs_ready")
        s_zexp = sem("z_exp_ready")
        s_log = sem("z_log_ready")
        s_delta = sem("delta_ready")
        s_du = sem("du_ready")
        s_b = sem("b_spread")
        s_c = sem("c_spread")
        s_ck = sem("c_kept")
        s_decay = sem("decay_ready")
        s_drive = sem("drive_ready")
        s_h = sem("h_ready")
        s_state = sem("state_kept")
        s_hc = sem("hc_ready")
        s_y = sem("y_added")
        s_yout = sem("y_out_ready")
        s_add = sem("chunk_added")

        TA, TB, LOW, BC, DT0, DT1, BCT, OUT0, OUT1 = range(9)
        ACT_USES = [TA, TB, LOW, BCT]
        DVE_USES = [BC, DT0, DT1, OUT0, OUT1]
        PREP = 7

        def bank(c, k):
            return misc[(k if c is None else PREP + k) % 3]

        def filled(c, k, last=False):
            if c is None:
                return k + 1
            return PREP + c * 9 + (k - PREP if last else k) + 1

        def used_act(c, k):
            return ACT_USES.index(k) + 1 + (0 if c is None else 4 * (c + 1))

        def used_dve(c, k, last=False):
            if c is None:
                return DVE_USES.index(k) + 1
            return 3 + 5 * c + DVE_USES.index(k) + 1 - (3 if last else 0)

        def chunk_of(c):
            return 0 if c is None else c + 1

        def tiles(c, t, n=1):
            return slice(c * CT + t, c * CT + t + n) if isinstance(c, int) else bass.ds(c * CT + t, n)

        block = ctx.enter_context(nc.Block())

        @block.vector
        def _(dve):
            def norm_stats(c):
                for t in range(CT):
                    last = dve.bn_stats(stats[:, t, :], x[:, tiles(c, t), :].rearrange("p a d -> p (a d)"))
                last.then_inc(s_stat, 1)
                dve.wait_ge(s_stat, c + 1)
                dve.sem_inc(s_mv, 1)
                for t in range(CT):
                    last = dve.bn_aggr(mean_var[:, t, :], stats[:, t, :])
                last.then_inc(s_mv, 1)
                dve.wait_ge(s_mv, 2 * c + 2)
                dve.tensor_scalar(var_eps[:, :], mean_var[:, :, 1], EPS, None, ALU.add).then_inc(s_var, 1)

            def norm_apply(c):
                dve.wait_ge(s_rstd, c + 1)
                for t in range(CT):
                    last = dve.tensor_scalar(xn[:, t, :], x[:, tiles(c, t), :].rearrange("p a d -> p (a d)"),
                                             mean_var[:, t, 0:1], rstd[:, t:t + 1], ALU.subtract, ALU.mult)
                last.then_inc(s_xn, 1)

            def split_bc(beside):
                c = chunk_of(beside)
                dve.wait_ge(s_fill, filled(beside, BC))
                whole = bank(beside, BC)[:, 0:CT * N2].rearrange("p (t n) -> p t n", t=CT)
                base = c * 4
                dve.tensor_copy(bc_parts[:, :, 0:N2], whole).then_inc(chain, 1)
                dve.wait_ge(chain, base + 1)
                dve.tensor_tensor(bc_rest[:, 0, :, :], whole, bc_parts[:, :, 0:N2], ALU.subtract).then_inc(s_dve, 1)
                dve.wait_ge(s_dve, used_dve(beside, BC))
                dve.tensor_copy(bc_parts[:, :, N2:2 * N2], bc_rest[:, 0, :, :]).then_inc(chain, 1)
                dve.wait_ge(chain, base + 2)
                dve.tensor_tensor(bc_rest[:, 1, :, :], bc_rest[:, 0, :, :], bc_parts[:, :, N2:2 * N2], ALU.subtract).then_inc(chain, 1)
                dve.wait_ge(chain, base + 3)
                dve.tensor_copy(bc_parts[:, :, 2 * N2:3 * N2], bc_rest[:, 1, :, :]).then_inc(chain, 1)
                dve.wait_ge(chain, base + 4)
                dve.sem_inc(s_bcp, 1)

            def biased(beside, m):
                c = chunk_of(beside)
                dve.wait_ge(s_fill, filled(beside, DT0 + m))
                dve.tensor_scalar(z[:, m, :], bank(beside, DT0 + m)[:, :], w["dt_b"][:, m:m + 1], None, ALU.add).then_inc(s_dve, 1)
                dve.wait_ge(s_dve, used_dve(beside, DT0 + m))
                dve.scalar_tensor_tensor(out=z_abs[:, m, :], in0=z[:, m, :], scalar=-1.0, in1=z[:, m, :], op0=ALU.mult, op1=ALU.max).then_inc(s_abs, 1)

            def soft(c, par, m):
                dve.wait_ge(s_log, 2 * c + m + 1)
                dve.scalar_tensor_tensor(out=delta[:, par, m, :], in0=z[:, m, :], scalar=0.0, in1=z_log[:, m, :],
                                         op0=ALU.max, op1=ALU.add).then_inc(s_delta, 1)
                dve.wait_ge(s_delta, 2 * c + m + 1)
                dve.tensor_tensor(du[:, par, m, :], delta[:, par, m, :], xnT[:, par, m, :], ALU.mult).then_inc(s_du, 1)

            def drives(c, par, s):
                m = s % 2
                if s == 0:
                    dve.wait_ge(s_du, 2 * c + 2)
                if m == 0:
                    dve.wait_ge(s_b, c * STATES + s // 2 + 1)
                dve.tensor_tensor(drive[:, s % 4, :], du[:, par, m, :], b_ps[:, (s // 2) % 2, :], ALU.mult).then_inc(s_drive, 1)

            def slot(c, par, s, last=False):
                n, m = c * SLOTS + s, s % 2
                if s + 1 < SLOTS:
                    drives(c, par, s + 1)
                elif not last:
                    drives(c + 1, 1 - par, 0)
                dve.wait_ge(s_drive, n + 3)
                dve.wait_ge(s_decay, n + 1)
                dve.wait_ge(s_hc, n + 1)
                if par == 0:
                    first = 0.0
                else:
                    dve.wait_ge(s_state, (c - 1) * STATES + s + 1)
                    first = state[:, s:s + 1]
                dve.tensor_tensor_scan(h[:, s % 4, :], decay[:, s % 4, :], drive[:, s % 4, :], first,
                                       ALU.mult, ALU.add).then_inc(s_h, 1)

            def out(c, par):
                dve.wait_ge(s_y, c * SLOTS + SLOTS + 4)
                for m in range(KD):
                    last = dve.scalar_tensor_tensor(out=y_out[:, m, :], in0=xnT[:, par, m, :], scalar=w["D"][:, m:m + 1],
                                                    in1=y_ps[:, m, :], op0=ALU.mult, op1=ALU.add)
                last.then_inc(s_yout, 1)

            def add(c, last):
                for r in range(2):
                    dve.wait_ge(s_fill, filled(c, OUT0 + r, last))
                    here = x[:, tiles(c, 2 * r, 2), :]
                    b = bank(c, OUT0 + r if not last else r)
                    dve.tensor_tensor(here, b[:, :].rearrange("p (a d) -> p a d", a=2), here, ALU.add).then_inc(s_dve, 1)

            def chunk(c, par, last=False):
                for s in range(3, SLOTS):
                    slot(c, par, s, last)
                    if not last:
                        if s == 4:
                            norm_stats(c + 1)
                        if s == 6:
                            norm_apply(c + 1)
                        if s == 14:
                            split_bc(c)
                        if s in (17, 18):
                            biased(c, s - 17)
                        if s in (25, 26):
                            soft(c + 1, 1 - par, s - 25)
                if not last:
                    for s in range(3):
                        slot(c + 1, 1 - par, s)
                out(c, par)
                add(c, last)

            dve.sem_inc(s_drive, 2)
            dve.sem_inc(s_h, 4)
            dve.sem_inc(s_yout, 1)
            dve.wait_ge(once, 1)
            dve.tensor_scalar(a_neg[:, :, :], a_exp[:, :, :], -1.0, None, ALU.mult).then_inc(once, 1)
            norm_stats(0)
            norm_apply(0)
            split_bc(None)
            for m in range(KD):
                biased(None, m)
            for m in range(KD):
                soft(0, 0, m)
            drives(0, 0, 0)
            for s in range(3):
                slot(0, 0, s)
            with dve.Fori(0, CHUNKS // 2 - 1) as pair:
                c = pair * 2
                chunk(c, 0)
                chunk(c + 1, 1)
            chunk(CHUNKS - 2, 0)
            chunk(CHUNKS - 1, 1, last=True)

        @block.gpsimd
        def _(pool):
            def norm_pow(c):
                pool.wait_ge(s_var, c + 1)
                pool.tensor_tensor(rstd[:, :], var_eps[:, :], const["minus_half"][:, 0:CT], ALU.pow).then_inc(s_rstd, 1)

            def chunk(c, par, last=False):
                for s in range(SLOTS):
                    n = c * SLOTS + s
                    pool.wait_ge(s_h, n + 5)
                    if par == 0:
                        end = h[:, s % 4, CH - 1:CH]
                        pool.tensor_tensor(state[:, s:s + 1], end, const["one"][:, 0:1], ALU.mult).then_inc(s_state, 1)
                    if s % 2 == 0:
                        pool.wait_ge(s_ck, c * STATES + s // 2 + 2)
                    pool.wait_ge(s_y, n + 1)
                    pool.tensor_tensor(hc[:, s % 4, :], h[:, s % 4, :], c_bc[:, (s // 2) % 2, :], ALU.mult).then_inc(s_hc, 1)
                    if s == 4 and not last:
                        norm_pow(c + 1)

            pool.sem_inc(s_hc, 4)
            norm_pow(0)
            with pool.Fori(0, CHUNKS // 2 - 1) as pair:
                c = pair * 2
                chunk(c, 0)
                chunk(c + 1, 1)
            chunk(CHUNKS - 2, 0)
            chunk(CHUNKS - 1, 1, last=True)

        @block.scalar
        def _(act):
            def keep(beside, k, out):
                act.wait_ge(s_fill, filled(beside, k))
                src = bank(beside, k)
                if k == LOW:
                    src = src[0:RANK, :]
                elif k == BCT:
                    src = src[0:3 * N2, 0:CH // 2].bitcast(BF16)
                else:
                    src = src[:, :]
                act.activation(out, src, ACT.Copy).then_inc(s_act, 1)

            def logs(c, m):
                act.wait_ge(s_abs, 2 * c + m + 1)
                act.activation(z_exp[:, m, :], z_abs[:, m, :], ACT.Exp, scale=-1.0).then_inc(s_zexp, 1)
                act.wait_ge(s_zexp, 2 * c + m + 1)
                act.activation(z_log[:, m, :], z_exp[:, m, :], ACT.Ln, bias=const["one"][:, 0:1]).then_inc(s_log, 1)

            def slot(c, par, s):
                n, m = c * SLOTS + s, s % 2
                if m == 0:
                    i = c * STATES + s // 2
                    act.wait_ge(s_c, i + 1)
                    act.wait_ge(s_hc, 2 * i + 2)
                    act.activation(c_bc[:, (s // 2) % 2, :], c_ps[:, :], ACT.Copy).then_inc(s_ck, 1)
                act.wait_ge(s_h, n + 1)
                if s < 2:
                    act.wait_ge(s_delta, 2 * c + s + 1)
                act.activation(decay[:, s % 4, :], delta[:, par, m, :], ACT.Exp,
                               scale=a_neg[:, m, s // 2:s // 2 + 1]).then_inc(s_decay, 1)

            def chunk(c, par, last=False):
                for s in range(SLOTS):
                    slot(c, par, s)
                    if not last:
                        if s == 11:
                            keep(c, TA, xnT[:, 1 - par, 0, :])
                            keep(c, TB, xnT[:, 1 - par, 1, :])
                        if s == 14:
                            keep(c, LOW, low[:, :])
                        if s in (21, 22):
                            logs(c + 1, s - 21)
                        if s == 23:
                            keep(c, BCT, bcT[:, 1 - par, :])

            act.activation(a_exp[:, :, :], w["A_log"][:, :, :], ACT.Exp).then_inc(once, 1)
            act.sem_inc(s_ck, 1)
            keep(None, TA, xnT[:, 0, 0, :])
            keep(None, TB, xnT[:, 0, 1, :])
            keep(None, LOW, low[:, :])
            for m in range(KD):
                logs(0, m)
            keep(None, BCT, bcT[:, 0, :])
            act.wait_ge(once, 2)
            with act.Fori(0, CHUNKS // 2 - 1) as pair:
                c = pair * 2
                chunk(c, 0)
                chunk(c + 1, 1)
            chunk(CHUNKS - 2, 0)
            chunk(CHUNKS - 1, 1, last=True)

        @block.tensor
        def _(pe):
            def turn_halves(beside):
                pe.wait_ge(s_xn, chunk_of(beside) + 1)
                if beside is not None:
                    pe.wait_ge(s_act, 4 * (beside + 1))
                    pe.wait_ge(s_dve, 3 + 5 * beside)
                for k in range(KD):
                    for t in range(CT):
                        last = pe.transpose(bank(beside, TA + k)[:, t * P:(t + 1) * P], xn[:, t, k * P:(k + 1) * P], const["ident"][:, :])
                    last.then_inc(s_fill, 1)

            def project(beside, par):
                pe.wait_ge(s_act, used_act(beside, TB))
                for k in range(KD):
                    last = pe.matmul(bank(beside, LOW)[0:RANK, :], w["low"][:, k, :], xnT[:, par, k, :], start=(k == 0), stop=(k == KD - 1))
                last.then_inc(s_fill, 1)
                for t in range(CT):
                    for k in range(KD):
                        last = pe.matmul(bank(beside, BC)[:, t * N2:(t + 1) * N2], xnT[:, par, k, t * P:(t + 1) * P], w["bc"][:, k, :],
                                         start=(k == 0), stop=(k == KD - 1))
                last.then_inc(s_fill, 1)

            def steps(beside):
                pe.wait_ge(s_act, used_act(beside, LOW))
                for m in range(KD):
                    pe.matmul(bank(beside, DT0 + m)[:, :], w["dt_w"][:, m * P:(m + 1) * P], low[:, :], start=True, stop=True).then_inc(s_fill, 1)

            def turn_bc(beside):
                pe.wait_ge(s_bcp, chunk_of(beside) + 1)
                dst = bank(beside, BCT)[0:3 * N2, 0:CH // 2].bitcast(BF16)
                for t in range(CT):
                    last = pe.transpose(dst[:, t * P:(t + 1) * P], bc_parts[:, t, :], const["ident_bf"][:, :])
                last.then_inc(s_fill, 1)

            def spread(c, par, n):
                i = c * STATES + n
                if n == 0:
                    pe.wait_ge(s_act, 4 * (c + 1))
                pe.wait_ge(s_drive, 2 * i)
                pe.matmul(b_ps[:, n % 2, :], const["pick_bc"][:, n, :], bcT[:, par, :], start=True, stop=True).then_inc(s_b, 1)
                pe.wait_ge(s_ck, i + 1)
                pe.matmul(c_ps[:, :], const["pick_bc"][:, STATES + n, :], bcT[:, par, :], start=True, stop=True).then_inc(s_c, 1)

            def collect(c, par, s):
                n, m = c * SLOTS + s, s % 2
                if s == 0:
                    pe.wait_ge(s_yout, c + 1)
                pe.wait_ge(s_hc, n + 5)
                pe.matmul(y_ps[:, m, :], const["ident"][:, :], hc[:, s % 4, :], start=(s < 2), stop=(s >= SLOTS - 2)).then_inc(s_y, 1)

            def turn_out(c, last):
                pe.wait_ge(s_yout, c + 2)
                for r in range(2):
                    pe.wait_ge(s_dve, 3 + 5 * c + (3 if not last else 0))
                    b = bank(c, OUT0 + r if not last else r)
                    for a in range(2):
                        for m in range(KD):
                            t = 2 * r + a
                            mm = pe.transpose(b[:, a * D + m * P:a * D + (m + 1) * P], y_out[:, m, t * P:(t + 1) * P], const["ident"][:, :])
                    mm.then_inc(s_fill, 1)

            def chunk(c, par, last=False):
                for s in range(SLOTS):
                    collect(c, par, s)
                    if not last:
                        if s == 7:
                            turn_halves(c)
                        if s == 9:
                            project(c, 1 - par)
                        if s == 13:
                            steps(c)
                        if s == 16:
                            turn_bc(c)
                    if s % 2:
                        n = s // 2 + 2
                        if n < STATES:
                            spread(c, par, n)
                        elif not last:
                            spread(c + 1, 1 - par, n - STATES)
                turn_out(c, last)

            pe.sem_inc(s_y, 4)
            turn_halves(None)
            project(None, 0)
            steps(None)
            turn_bc(None)
            spread(0, 0, 0)
            spread(0, 0, 1)
            with pe.Fori(0, CHUNKS // 2 - 1) as pair:
                c = pair * 2
                chunk(c, 0)
                chunk(c + 1, 1)
            chunk(CHUNKS - 2, 0)
            chunk(CHUNKS - 1, 1, last=True)


def build(nc, ins, out, stages):
    with ExitStack() as ctx:
        def keep(names):
            return {n: ctx.enter_context(nc.sbuf_tensor("w_" + n, list(ins[n].shape), ins[n].dtype)) for n in names}

        def load(sp, kept, here):
            for n, t in kept.items():
                sp.dma_start(t[tuple(slice(None) for _ in t.shape)], ins[n]).then_inc(here, 16)

        def weights(kept, prefix):
            return {n[len(prefix):]: t for n, t in kept.items() if n.startswith(prefix)}

        x = ctx.enter_context(nc.sbuf_tensor("x", [P, TILES, D], F32))
        late = [n for n in ins if n.startswith(("f1_", "sc_")) or n in ("pick_gate1", "pick_bc", "cost")]
        early = keep([n for n in ins if n != "x" and n not in late])
        qk_parts = nc.dram_tensor("qk_parts", (2, 3, D, TOKENS), BF16, kind="Internal").ap()
        v_rows = nc.dram_tensor("v_rows", (TOKENS, HEADS * 2 * DH), F32, kind="Internal").ap()
        s_x = ctx.enter_context(nc.semaphore("x_here"))
        s_early = ctx.enter_context(nc.semaphore("early_inputs_here"))
        s_late = ctx.enter_context(nc.semaphore("late_inputs_here"))
        s_out = ctx.enter_context(nc.semaphore("outputs_there"))
        with nc.Block() as block:
            @block.sync
            def _(sp):
                x_tiles = ins["x"].rearrange("b (t p) d -> p (b t) d", p=P)
                for c in range(CHUNKS):
                    sp.dma_start(x[:, c * CT:(c + 1) * CT, :], x_tiles[:, c * CT:(c + 1) * CT, :]).then_inc(s_x, 16)
                load(sp, early, s_early)
                sp.wait_ge(s_x, 16 * CHUNKS)
                sp.wait_ge(s_early, 16 * len(early))
        const = dict(early)
        for n, s in enumerate(stages):
            if s == "ffn_moe":
                ffn_moe(nc, f"a{n}", x, weights(early, "f0_"), const)
            if s == "attention":
                attention_inputs(nc, f"a{n}i", x, weights(early, "at_"), const, qk_parts, v_rows)
                attention(nc, f"a{n}", x, weights(early, "at_"), const, qk_parts, v_rows)
            if s == "load_second_layer":
                second = keep(late)
                const.update(second)
                with nc.Block() as block:
                    @block.sync
                    def _(sp):
                        load(sp, second, s_late)
                        sp.wait_ge(s_late, 16 * len(second))
            if s == "scan_mixer":
                scan_mixer(nc, f"a{n}", x, weights(const, "sc_"), const)
            if s == "ffn_gelu":
                ffn_gelu(nc, f"a{n}", x, weights(const, "f1_"), const)
        with nc.Block() as block:
            @block.sync
            def _(sp):
                o_tiles = out.rearrange("b (t p) d -> p (b t) d", p=P)
                for c in range(CHUNKS):
                    sp.dma_start(o_tiles[:, c * CT:(c + 1) * CT, :], x[:, c * CT:(c + 1) * CT, :]).then_inc(s_out, 16)
                sp.wait_ge(s_out, 16 * CHUNKS)


STAGES = ["ffn_moe", "attention", "ffn_moe", "load_second_layer", "ffn_gelu", "scan_mixer", "ffn_gelu"]


def lay_out(inputs):
    a = {k: np.asarray(v) for k, v in inputs.items()}
    bf = mybir.dt.np(BF16)
    rows = lambda m: np.ascontiguousarray(m.reshape(m.shape[0] // P, P, *m.shape[1:]).swapaxes(0, 1))
    g = {"x": a["L0_attn_x"]}
    g["f0_router"] = rows(np.concatenate([a["L0_ffn_gate_w"], a["L0_ffn_se_gate_w"]], 0).T)
    for mine, routed, shared in (("f0_gate", "L0_ffn_w_gate", "L0_ffn_sh_gate"), ("f0_up", "L0_ffn_w_up", "L0_ffn_sh_up")):
        units = np.concatenate([a[routed], a[shared].reshape(2, P, D)], 0)
        g[mine] = np.ascontiguousarray(units.reshape(UNITS0, P, KD, P).transpose(3, 0, 2, 1))
    down = np.concatenate([a["L0_ffn_w_down"].transpose(0, 2, 1), a["L0_ffn_sh_down"].T.reshape(2, P, D)], 0)
    g["f0_down"] = np.ascontiguousarray(down.transpose(1, 0, 2))
    for n in "qkv":
        g["at_w" + n] = rows(a["L0_attn_W" + n])
    wo = np.zeros((HG, GH, 2 * DH, D), np.float32)
    wo[:, :, 0:DH] = a["L0_attn_Wo"].reshape(HG, GH, DH, D)
    g["at_wo"] = np.ascontiguousarray(wo.reshape(HG, P, D).transpose(1, 0, 2))
    cols = lambda v: np.ascontiguousarray(v.reshape(KD, P, *v.shape[1:]).swapaxes(0, 1))
    g["sc_A_log"], g["sc_dt_b"], g["sc_D"] = cols(a["L1_attn_A_log"]), cols(a["L1_attn_dt_proj_b"]), cols(a["L1_attn_D"])
    g["sc_low"] = rows(a["L1_attn_x_proj_w"][0:RANK].T)
    g["sc_bc"] = rows(a["L1_attn_x_proj_w"][RANK:].T)
    g["sc_dt_w"] = np.ascontiguousarray(a["L1_attn_dt_proj_w"].T)
    one = lambda v: np.ascontiguousarray(np.broadcast_to(v[None], (P, v.shape[0])))
    g["f1_router"] = rows(a["L1_ffn_router_w"])
    g["f1_router_b"] = one(a["L1_ffn_router_b"])
    g["f1_down_w"] = rows(a["L1_ffn_down_w"])
    g["f1_down_b"] = a["L1_ffn_down_b"].reshape(P, 1)
    w1 = [a[f"L1_ffn_e{e}_w1"] for e in range(E1)] + [a["L1_ffn_shared_w1"]]
    g["f1_w1"] = np.ascontiguousarray(np.concatenate(w1, 1).reshape(P, HT1 + 1, P))
    b1 = [a[f"L1_ffn_e{e}_b1"] for e in range(E1)] + [a["L1_ffn_shared_b1"]]
    g["f1_b1"] = np.ascontiguousarray(np.concatenate(b1).reshape(HT1 + 1, P).T)
    w2 = [a[f"L1_ffn_e{e}_w2"] for e in range(E1)] + [a["L1_ffn_shared_w2"]]
    g["f1_w2"] = rows(np.concatenate(w2, 0))
    b2 = [a[f"L1_ffn_e{e}_b2"] for e in range(E1)] + [a["L1_ffn_shared_b2"]]
    g["f1_b2"] = np.ascontiguousarray(np.stack(b2, 1))
    g["f1_up_w"], g["f1_core_w"] = a["L1_ffn_up_w"], rows(a["L1_ffn_core_w"])
    g["f1_up_b"], g["f1_core_b"] = one(a["L1_ffn_up_b"]), one(a["L1_ffn_core_b"])
    g["ident"] = np.eye(P, dtype=np.float32)
    g["ident_bf"] = np.eye(P, dtype=bf)
    g["iota"] = np.tile(np.arange(E0, dtype=np.float32), (P, 1))
    g["minus_half"] = np.full((P, 8), -0.5, np.float32)
    g["pick_gate"] = np.ascontiguousarray(
        np.broadcast_to(np.tile(np.eye(G0), (3, 1))[:, :, None], (3 * G0, G0, P)).astype(bf))
    g["causal"] = np.tril(np.ones((P, P), np.float32))
    g["later"] = np.ascontiguousarray(np.broadcast_to(
        (np.arange(BT)[:, None] > np.arange(BT)[None]).astype(np.float32)[None], (P, BT, BT)))
    pick = np.zeros((P, GH), np.float32)
    pick[np.arange(GH) * 2 * DH + DH, np.arange(GH)] = 1
    g["pick_den"] = pick
    g["one"] = np.ones((P, 1), np.float32)
    g["pick_bc"] = np.ascontiguousarray(
        np.broadcast_to(np.tile(np.eye(2 * STATES), (3, 1))[:, :, None], (6 * STATES, 2 * STATES, P)).astype(bf))
    g["pick_gate1"] = np.ascontiguousarray(
        np.broadcast_to(np.tile(np.eye(E1), (3, 1))[:, :, None], (3 * E1, E1, P)).astype(bf))
    g["cost"] = np.tile(np.float32(1e-7) * np.array([2 * P * h for h in HID1], np.float32), (P, 1))
    return g


def kernel(**inputs):
    import concourse.bacc as _bacc
    from concourse.bass_utils import run_bass_kernel_spmd as _run

    nc = _bacc.Bacc("TRN2", target_bir_lowering=False, num_devices=1)
    arrays, ins = {}, {}
    for name, v in lay_out(inputs).items():
        arrays[f"in_{name}"] = v
        ins[name] = nc.dram_tensor(f"in_{name}", v.shape, mybir.dt.from_np(v.dtype), kind="ExternalInput").ap()
    out = nc.dram_tensor("out_0", (B, T, D), F32, kind="ExternalOutput").ap()
    build(nc, ins, out, STAGES)
    return _run(nc, [arrays], core_ids=[0]).results[0]["out_0"]
```

```python
from contextlib import ExitStack

import numpy as np

import concourse.bass as bass
from concourse import mybir

ALU = mybir.AluOpType
ACT = mybir.ActivationFunctionType
AX = mybir.AxisListType
F32 = mybir.dt.float32
BF16 = mybir.dt.bfloat16
U32 = mybir.dt.uint32

P = 128
B, T, D = 4, 1024, 256
KD = D // P
TOKENS = B * T
TILES = TOKENS // P
CH = 512
CT = CH // P
CHUNKS = TOKENS // CH
EPS = 1e-5
FIRST_CHUNKS, FIRST_UNITS = 2, 3
E0 = 8
UNITS0 = E0 + 2
G0 = E0 + 1
E1 = 8
HID1 = [128, 256, 384, 512, 128, 256, 384, 512]
TILE_EXPERT = [e for e in range(E1) for _ in range(HID1[e] // P)]
HT1 = len(TILE_EXPERT)
HEADS, DH = 16, 16
GH = 4
HG = HEADS // GH
BT = T // P
STATES = 16
RANK = 64
Q_PART = [0, 0, 1, 1, 0, 2]
K_PART = [0, 1, 0, 1, 2, 0]
QK_ROWS = len(Q_PART) * DH
M_ROWS = 3
HIDDEN = -1e30


def three_parts(dve, sem, base, whole, part1, rest, part2, rest2, part3):
    dve.tensor_copy(part1, whole).then_inc(sem, 1)
    dve.wait_ge(sem, base + 1)
    dve.tensor_tensor(rest, whole, part1, ALU.subtract).then_inc(sem, 1)
    dve.wait_ge(sem, base + 2)
    dve.tensor_copy(part2, rest).then_inc(sem, 1)
    dve.wait_ge(sem, base + 3)
    dve.tensor_tensor(rest2, rest, part2, ALU.subtract).then_inc(sem, 1)
    dve.wait_ge(sem, base + 4)
    return dve.tensor_copy(part3, rest2)


def ffn_moe(nc, tag, x, w, const, beside, x_rest=None, w_rest=None):
    with ExitStack() as ctx:
        ctx.enter_context(nc.cleanup_on_exit())

        def sb(name, shape, dt=F32):
            return ctx.enter_context(nc.sbuf_tensor(f"{tag}_{name}", shape, dt))

        def psum(name, shape, dt=F32):
            return ctx.enter_context(nc.psum_tensor(f"{tag}_{name}", shape, dt))

        def sem(name):
            return nc.alloc_semaphore(f"{tag}_{name}")

        xn = sb("xn", [P, CT, D])
        xnT = sb("xnT", [P, 2, KD, CH])
        stats = sb("stats", [P, CT, 6])
        mean_var = sb("mean_var", [P, CT, 2])
        var_eps = sb("var_eps", [P, CT])
        rstd = sb("rstd", [P, CT])
        scores = sb("scores", [P, CT, G0])
        top = sb("top", [P, CT, 8])
        top_at = sb("top_at", [P, CT, 8], U32)
        at = sb("at", [P, CT, 2])
        diff = sb("diff", [P, CT, 2])
        tanh = sb("tanh", [P, CT, 2])
        weight = sb("weight", [P, CT, 2])
        hit = sb("hit", [P, 2, CT, E0])
        gates = sb("gates", [P, CT, G0])
        rest = sb("rest", [P, CT, G0])
        rest2 = sb("rest2", [P, CT, G0])
        gparts = sb("gparts", [P, CT, 3 * G0], BF16)
        gT = sb("gT", [3 * G0, 2, CH], BF16)
        silu = sb("silu", [P, 2, CH])
        prod = sb("prod", [P, 2, CH])
        hid = sb("hid", [P, 2, CH])

        x1 = psum("x1", [P, 2, CH])
        x3 = psum("x3", [P, 2, CH])
        gate_bc = psum("gate_bc", [P, CH])
        acc = psum("acc", [P, CT, D])
        misc = psum("misc", [P, CH])
        misc_bf = misc[0:3 * G0, 0:CH // 2].bitcast(BF16)

        chain = sem("dve_steps")
        s_var = sem("var_ready")
        s_rstd = sem("rstd_ready")
        s_xn = sem("xn_ready")
        s_T = sem("half_transposed")
        s_Tc = sem("half_kept")
        s_R = sem("scores_ready")
        s_Rc = sem("scores_kept")
        s_diff = sem("diff_ready")
        s_tanh = sem("tanh_ready")
        s_gp = sem("gate_parts_ready")
        s_GT = sem("gates_transposed")
        s_gT = sem("gates_kept")
        s_x1 = sem("x1_ready")
        s_x3 = sem("x3_and_gate_ready")
        s_silu = sem("silu_done")
        s_prod = sem("product_done")
        s_hid = sem("hidden_ready")
        s_down = sem("down_done")
        s_acc = sem("chunk_added")

        NORM, CHOOSE, WEIGH = 3, 7, 7
        STEPS = NORM + CHOOSE + WEIGH

        def tile_of(c, t):
            return bass.ds(c * CT + t, 1) if not isinstance(c, int) else slice(c * CT + t, c * CT + t + 1)

        block = ctx.enter_context(nc.Block())

        @block.vector
        def _(dve):
            def norm_stats(c):
                for t in range(CT):
                    last = dve.bn_stats(stats[:, t, :], x[:, tile_of(c, t), :].rearrange("p a d -> p (a d)"))
                last.then_inc(chain, 1)
                dve.wait_ge(chain, c * STEPS + 1)
                dve.sem_inc(chain, 1)
                for t in range(CT):
                    last = dve.bn_aggr(mean_var[:, t, :], stats[:, t, :])
                last.then_inc(chain, 1)
                dve.wait_ge(chain, c * STEPS + 3)
                dve.tensor_scalar(var_eps[:, :], mean_var[:, :, 1], EPS, None, ALU.add).then_inc(s_var, 1)

            def norm_apply(c):
                dve.wait_ge(s_rstd, c + 1)
                dve.wait_ge(s_T, c * KD)
                for t in range(CT):
                    last = dve.tensor_scalar(xn[:, t, :], x[:, tile_of(c, t), :].rearrange("p a d -> p (a d)"),
                                             mean_var[:, t, 0:1], rstd[:, t:t + 1], ALU.subtract, ALU.mult)
                last.then_inc(s_xn, 1)

            def choose(c):
                base = c * STEPS + NORM
                dve.wait_ge(s_R, c + 1)
                dve.tensor_copy(scores[:, :, :], misc[:, 0:CT * G0].rearrange("p (t g) -> p t g", t=CT)).then_inc(s_Rc, 1)
                dve.wait_ge(s_Rc, c + 1)
                dve.sem_inc(chain, 1)
                for t in range(CT):
                    last = dve.max(top[:, t, :], scores[:, t, 0:E0])
                last.then_inc(chain, 1)
                dve.wait_ge(chain, base + 2)
                dve.sem_inc(chain, 1)
                for t in range(CT):
                    last = dve.max_index(top_at[:, t, :], top[:, t, :], scores[:, t, 0:E0])
                last.then_inc(chain, 1)
                dve.tensor_tensor(diff[:, :, 0:1], top[:, :, 0:1], top[:, :, 1:2], ALU.subtract)
                dve.tensor_copy(diff[:, :, 1:2], scores[:, :, E0:E0 + 1]).then_inc(s_diff, 1)
                dve.wait_ge(chain, base + 4)
                dve.tensor_copy(at[:, :, :], top_at[:, :, 0:2]).then_inc(chain, 1)
                dve.wait_ge(chain, base + 5)
                for k in range(2):
                    dve.tensor_tensor(hit[:, k, :, :], const["iota"][:, :].rearrange("p (a e) -> p a e", a=1).broadcast_to([P, CT, E0]),
                                      at[:, :, k:k + 1].broadcast_to([P, CT, E0]), ALU.is_equal).then_inc(chain, 1)

            def weigh(c):
                base = c * STEPS + NORM + CHOOSE
                dve.wait_ge(s_tanh, c + 1)
                dve.tensor_scalar(weight[:, :, 0:1], tanh[:, :, 0:1], 0.25, 0.25, ALU.mult, ALU.add)
                dve.tensor_scalar(weight[:, :, 1:2], tanh[:, :, 0:1], -0.25, 0.25, ALU.mult, ALU.add)
                dve.tensor_scalar(gates[:, :, E0:G0], tanh[:, :, 1:2], 0.25, 0.25, ALU.mult, ALU.add).then_inc(chain, 1)
                dve.wait_ge(chain, base + 1)
                for k in range(2):
                    last = dve.tensor_tensor(hit[:, k, :, :], hit[:, k, :, :],
                                             weight[:, :, k:k + 1].broadcast_to([P, CT, E0]), ALU.mult)
                last.then_inc(chain, 1)
                dve.wait_ge(chain, base + 2)
                dve.tensor_tensor(gates[:, :, 0:E0], hit[:, 0, :, :], hit[:, 1, :, :], ALU.add).then_inc(chain, 1)
                dve.wait_ge(chain, base + 3)
                dve.wait_ge(s_GT, c)
                three_parts(dve, chain, base + 3, gates[:, :, :], gparts[:, :, 0:G0], rest[:, :, :],
                            gparts[:, :, G0:2 * G0], rest2[:, :, :], gparts[:, :, 2 * G0:3 * G0]).then_inc(s_gp, 1)

            def hidden(c, u):
                n = c * UNITS0 + u
                b = u % 2
                dve.wait_ge(s_silu, n + 3)
                dve.wait_ge(s_x3, n + 1)
                dve.tensor_tensor(prod[:, b, :], silu[:, b, :], x3[:, b, :], ALU.mult).then_inc(s_prod, 1)
                dve.wait_ge(s_prod, n + 3)
                dve.wait_ge(s_down, n + 1)
                dve.tensor_tensor(hid[:, b, :], prod[:, b, :], gate_bc[:, :], ALU.mult).then_inc(s_hid, 1)

            def add(c):
                dve.wait_ge(s_down, c * UNITS0 + UNITS0 + 2)
                for t in range(0, CT, 2):
                    where = x[:, bass.ds(c * CT + t, 2) if not isinstance(c, int) else slice(c * CT + t, c * CT + t + 2), :]
                    last = dve.tensor_tensor(where, acc[:, t:t + 2, :], where, ALU.add)
                last.then_inc(s_acc, 1)

            def chunk(c, last=False):
                for u in range(1, UNITS0):
                    hidden(c, u)
                    if not last:
                        if u == 1:
                            if x_rest and not (isinstance(c, int) and c + 1 < FIRST_CHUNKS):
                                dve.wait_ge(*x_rest)
                            norm_stats(c + 1)
                        if u == 2:
                            norm_apply(c + 1)
                        if u == 5:
                            choose(c + 1)
                        if u == 6:
                            weigh(c + 1)
                if not last:
                    hidden(c + 1, 0)
                add(c)

            dve.sem_inc(s_prod, 2)
            dve.sem_inc(s_hid, 1)
            dve.sem_inc(s_acc, 1)
            norm_stats(0)
            norm_apply(0)
            choose(0)
            weigh(0)
            hidden(0, 0)
            chunk(0)
            with dve.Fori(0, CHUNKS // 2 - 1) as pair:
                c = pair * 2 + 1
                chunk(c)
                chunk(c + 1)
            chunk(CHUNKS - 1, last=True)

        @block.sync
        def _(sp):
            beside(sp)

        @block.gpsimd
        def _(pool):
            with pool.Fori(0, CHUNKS) as c:
                pool.wait_ge(s_var, c + 1)
                pool.tensor_tensor(rstd[:, :], var_eps[:, :], const["minus_half"][:, 0:CT], ALU.pow).then_inc(s_rstd, 1)

        @block.scalar
        def _(act):
            def keep_half(c, par, k):
                act.wait_ge(s_T, c * KD + k + 1)
                act.activation(xnT[:, par, k, :], misc[:, :], ACT.Copy).then_inc(s_Tc, 1)

            def tanhs(c):
                act.wait_ge(s_diff, c + 1)
                act.activation(tanh[:, :, :], diff[:, :, :], ACT.Tanh, scale=0.5).then_inc(s_tanh, 1)

            def keep_gates(c, par):
                act.wait_ge(s_GT, c + 1)
                act.activation(gT[:, par, :], misc_bf, ACT.Copy).then_inc(s_gT, 1)

            def unit(c, u):
                n = c * UNITS0 + u
                act.wait_ge(s_x1, n + 1)
                act.wait_ge(s_prod, n + 1)
                act.activation(silu[:, u % 2, :], x1[:, u % 2, :], ACT.Silu).then_inc(s_silu, 1)

            def chunk(c, par, last=False):
                for u in range(1, UNITS0):
                    unit(c, u)
                    if not last:
                        if u == 3:
                            keep_half(c + 1, 1 - par, 0)
                        if u == 4:
                            keep_half(c + 1, 1 - par, 1)
                        if u == 6:
                            tanhs(c + 1)
                        if u == 8:
                            keep_gates(c + 1, 1 - par)
                if not last:
                    unit(c + 1, 0)

            act.sem_inc(s_silu, 2)
            for k in range(KD):
                keep_half(0, 0, k)
            tanhs(0)
            keep_gates(0, 0)
            unit(0, 0)
            with act.Fori(0, CHUNKS - 2, 2) as c:
                chunk(c, 0)
                chunk(c + 1, 1)
            chunk(CHUNKS - 2, 0)
            chunk(CHUNKS - 1, 1, last=True)

        @block.tensor
        def _(pe):
            def turn_half(c, k):
                if k == 0:
                    pe.wait_ge(s_xn, c + 1)
                    pe.wait_ge(s_gT, c)
                else:
                    pe.wait_ge(s_Tc, c * KD + k)
                for t in range(CT):
                    last = pe.transpose(misc[:, t * P:(t + 1) * P], xn[:, t, k * P:(k + 1) * P], const["ident"][:, :])
                last.then_inc(s_T, 1)

            def route(c, par):
                pe.wait_ge(s_Tc, c * KD + KD)
                for t in range(CT):
                    for k in range(KD):
                        last = pe.matmul(misc[:, t * G0:(t + 1) * G0], xnT[:, par, k, t * P:(t + 1) * P],
                                         w["router"][:, k, :], start=(k == 0), stop=(k == KD - 1))
                last.then_inc(s_R, 1)

            def turn_gates(c):
                pe.wait_ge(s_gp, c + 1)
                for t in range(CT):
                    last = pe.transpose(misc_bf[:, t * P:(t + 1) * P], gparts[:, t, :], const["ident_bf"][:, :])
                last.then_inc(s_GT, 1)

            def up(c, par, u):
                n = c * UNITS0 + u
                b = u % 2
                if w_rest and u == FIRST_UNITS:
                    pe.wait_ge(*w_rest)
                pe.wait_ge(s_silu, n + 1)
                for k in range(KD):
                    last = pe.matmul(x1[:, b, :], w["gate"][:, u, k, :], xnT[:, par, k, :], start=(k == 0), stop=(k == KD - 1))
                last.then_inc(s_x1, 1)
                pe.wait_ge(s_prod, n + 1)
                for k in range(KD):
                    pe.matmul(x3[:, b, :], w["up"][:, u, k, :], xnT[:, par, k, :], start=(k == 0), stop=(k == KD - 1))
                pe.wait_ge(s_hid, n + 1)
                if u == 0:
                    pe.wait_ge(s_gT, c + 1)
                pe.matmul(gate_bc[:, :], const["pick_gate"][:, min(u, E0), :], gT[:, par, :],
                          start=True, stop=True).then_inc(s_x3, 1)

            def down(c, u):
                n = c * UNITS0 + u
                pe.wait_ge(s_hid, n + 2)
                if u == 0:
                    pe.wait_ge(s_acc, c + 1)
                for t in range(CT):
                    last = pe.matmul(acc[:, t, :], hid[:, u % 2, t * P:(t + 1) * P], w["down"][:, u, :],
                                     start=(u == 0 and t % 2 == 0), stop=(u == UNITS0 - 1), skip_group_check=True)
                last.then_inc(s_down, 1)

            def chunk(c, par, last=False):
                for u in range(1, UNITS0):
                    up(c, par, u)
                    down(c, u - 1)
                    if not last:
                        if u == 2:
                            turn_half(c + 1, 0)
                        if u == 3:
                            turn_half(c + 1, 1)
                        if u == 4:
                            route(c + 1, 1 - par)
                        if u == 7:
                            turn_gates(c + 1)
                if not last:
                    up(c + 1, 1 - par, 0)
                down(c, UNITS0 - 1)

            pe.sem_inc(s_down, 2)
            turn_half(0, 0)
            turn_half(0, 1)
            route(0, 0)
            turn_gates(0)
            up(0, 0, 0)
            with pe.Fori(0, CHUNKS - 2, 2) as c:
                chunk(c, 0)
                chunk(c + 1, 1)
            chunk(CHUNKS - 2, 0)
            chunk(CHUNKS - 1, 1, last=True)


def ffn_gelu(nc, tag, x, w, const):
    with ExitStack() as ctx:
        ctx.enter_context(nc.cleanup_on_exit())

        def sb(name, shape, dt=F32):
            return ctx.enter_context(nc.sbuf_tensor(f"{tag}_{name}", shape, dt))

        def psum(name, shape, dt=F32):
            return ctx.enter_context(nc.psum_tensor(f"{tag}_{name}", shape, dt))

        def sem(name):
            return nc.alloc_semaphore(f"{tag}_{name}")

        xn = sb("xn", [P, CT, D])
        xnT = sb("xnT", [P, KD, CH])
        core = sb("core", [P, 2, KD, CH])
        gelu_h = sb("gelu_h", [P, 2, CH])
        stats = sb("stats", [P, CT, 6])
        mean_var = sb("mean_var", [P, CT, 2])
        var_eps = sb("var_eps", [P, CT])
        rstd = sb("rstd", [P, CT])
        biased = sb("biased", [P, CT, E1])
        logits = sb("logits", [P, CT, E1])
        shifted = sb("shifted", [P, CT, E1])
        expd = sb("expd", [P, CT, E1])
        total = sb("total", [P, CT])
        inverse = sb("inverse", [P, CT])
        probs = sb("probs", [P, CT, E1])
        top = sb("top", [P, CT, 8])
        top_p = sb("top_p", [P, CT, 8])
        top_at = sb("top_at", [P, CT, 8], U32)
        at = sb("at", [P, CT, 2])
        diff = sb("diff", [P, CT, 1])
        tanh = sb("tanh", [P, CT, 1])
        weight = sb("weight", [P, CT, 2])
        hit = sb("hit", [P, 2, CT, E1])
        gates = sb("gates", [P, CT, E1])
        rest = sb("rest", [P, CT, E1])
        rest2 = sb("rest2", [P, CT, E1])
        gparts = sb("gparts", [P, CT, 3 * E1], BF16)
        gT = sb("gT", [3 * E1, CH], BF16)
        gate_bc = sb("gate_bc", [P, 2, E1, CH])
        act_out = sb("act_out", [P, 3, CH])
        hid = sb("hid", [P, 3, CH])
        mixed = sb("mixed", [P, CH])
        gelu_b1 = sb("gelu_b1", [P, HT1])
        b2_sum = sb("b2_sum", [P, 1])
        shared_b2 = sb("shared_b2", [P, 1])
        b2_all = sb("b2_all", [P, 1])
        every = sb("every", [P, 1])
        end_sum = sb("end_sum", [P, D])
        end_bias = sb("end_bias", [P, 2, D])

        u_ps = psum("u", [P, 3, CH])
        acc = psum("acc", [P, 2, CH])
        end = psum("end", [P, CT, D])
        misc = psum("misc", [P, CH])
        misc_bf = misc[0:3 * E1, 0:CH // 2].bitcast(BF16)

        once = sem("dve_once")
        s_gb1 = sem("gelu_b1_ready")
        s_every = sem("every_summed")
        s_everyd = sem("every_ready")
        chain = sem("dve_steps")
        s_var = sem("var_ready")
        s_rstd = sem("rstd_ready")
        s_xn = sem("xn_ready")
        s_T = sem("half_transposed")
        s_Tc = sem("half_kept")
        s_R = sem("scores_ready")
        s_Rc = sem("scores_kept")
        s_core = sem("core_ready")
        s_h = sem("h_ready")
        s_gh = sem("gelu_h_ready")
        s_shift = sem("shifted_ready")
        s_exp = sem("exp_ready")
        s_diff = sem("diff_ready")
        s_tanh = sem("tanh_ready")
        s_gp = sem("gate_parts_ready")
        s_GT = sem("gates_transposed")
        s_gT = sem("gates_kept")
        s_G = sem("gate_spread")
        s_Gc = sem("gate_spread_kept")
        s_u = sem("u_ready")
        s_gelu = sem("gelu_done")
        s_hid = sem("hidden_ready")
        s_down = sem("down_done")
        s_mixed = sem("mixed_ready")
        s_end = sem("end_ready")
        s_add = sem("chunk_added")

        NORM, CHOOSE, PICK, WEIGH = 3, 4, 9, 7
        STEPS = NORM + CHOOSE + PICK + WEIGH
        UNITS = HT1 + 1
        SH = HT1

        def tiles(c, t, n=1):
            return slice(c * CT + t, c * CT + t + n) if isinstance(c, int) else bass.ds(c * CT + t, n)

        def per_expert(a):
            return a.broadcast_to([P, CT, E1])

        block = ctx.enter_context(nc.Block())

        @block.vector
        def _(dve):
            def constants():
                dve.tensor_reduce(b2_sum[:, :], w["b2"][:, 0:E1], AX.X, ALU.add).then_inc(once, 1)
                dve.tensor_scalar(shared_b2[:, :], w["b2"][:, E1:E1 + 1], 0.1, None, ALU.mult).then_inc(once, 1)
                dve.tensor_tensor(end_sum[:, :], w["up_b"][:, :], w["core_b"][:, :], ALU.add).then_inc(once, 1)
                dve.wait_ge(once, 3)
                dve.tensor_tensor(b2_all[:, :], b2_sum[:, :], shared_b2[:, :], ALU.add).then_inc(once, 1)
                for r in range(2):
                    dve.tensor_scalar(end_bias[:, r, :], end_sum[:, :], 0.5, None, ALU.mult).then_inc(once, 1)
                dve.wait_ge(once, 6)
                dve.wait_ge(s_every, 1)
                dve.tensor_tensor(every[:, :], misc[:, 0:1], b2_all[:, :], ALU.add).then_inc(s_everyd, 1)

            def norm_stats(c):
                for t in range(CT):
                    last = dve.bn_stats(stats[:, t, :], x[:, tiles(c, t), :].rearrange("p a d -> p (a d)"))
                last.then_inc(chain, 1)
                dve.wait_ge(chain, c * STEPS + 1)
                dve.sem_inc(chain, 1)
                for t in range(CT):
                    last = dve.bn_aggr(mean_var[:, t, :], stats[:, t, :])
                last.then_inc(chain, 1)
                dve.wait_ge(chain, c * STEPS + 3)
                dve.tensor_scalar(var_eps[:, :], mean_var[:, :, 1], EPS, None, ALU.add).then_inc(s_var, 1)

            def norm_apply(c):
                dve.wait_ge(s_rstd, c + 1)
                dve.wait_ge(s_T, c * KD)
                for t in range(CT):
                    last = dve.tensor_scalar(xn[:, t, :], x[:, tiles(c, t), :].rearrange("p a d -> p (a d)"),
                                             mean_var[:, t, 0:1], rstd[:, t:t + 1], ALU.subtract, ALU.mult)
                last.then_inc(s_xn, 1)

            def choose(c):
                base = c * STEPS + NORM
                dve.wait_ge(s_R, c + 1)
                dve.tensor_tensor(biased[:, :, :], misc[:, 0:CT * E1].rearrange("p (t g) -> p t g", t=CT),
                                  per_expert(w["router_b"][:, :].rearrange("p (a e) -> p a e", a=1)), ALU.add).then_inc(s_Rc, 1)
                dve.wait_ge(s_Rc, c + 1)
                dve.tensor_tensor(logits[:, :, :], biased[:, :, :],
                                  per_expert(const["cost"][:, :].rearrange("p (a e) -> p a e", a=1)), ALU.subtract).then_inc(chain, 1)
                dve.wait_ge(chain, base + 1)
                dve.sem_inc(chain, 1)
                for t in range(CT):
                    last = dve.max(top[:, t, :], logits[:, t, :])
                last.then_inc(chain, 1)
                dve.wait_ge(chain, base + 3)
                dve.tensor_tensor(shifted[:, :, :], logits[:, :, :], per_expert(top[:, :, 0:1]), ALU.subtract).then_inc(s_shift, 1)
                dve.sem_inc(chain, 1)

            def pick(c):
                base = c * STEPS + NORM + CHOOSE
                dve.wait_ge(s_exp, c + 1)
                dve.tensor_reduce(total[:, :], expd[:, :, :], AX.X, ALU.add).then_inc(chain, 1)
                dve.wait_ge(chain, base + 1)
                dve.reciprocal(inverse[:, :], total[:, :]).then_inc(chain, 1)
                dve.wait_ge(chain, base + 2)
                dve.tensor_tensor(probs[:, :, :], expd[:, :, :],
                                  per_expert(inverse[:, :].rearrange("p (t a) -> p t a", a=1)), ALU.mult).then_inc(chain, 1)
                dve.wait_ge(chain, base + 3)
                dve.sem_inc(chain, 1)
                for t in range(CT):
                    last = dve.max(top_p[:, t, :], probs[:, t, :])
                last.then_inc(chain, 1)
                dve.wait_ge(chain, base + 5)
                dve.tensor_tensor(diff[:, :, :], top_p[:, :, 0:1], top_p[:, :, 1:2], ALU.subtract).then_inc(s_diff, 1)
                for t in range(CT):
                    last = dve.max_index(top_at[:, t, :], top_p[:, t, :], probs[:, t, :])
                last.then_inc(chain, 1)
                dve.wait_ge(chain, base + 6)
                dve.tensor_copy(at[:, :, :], top_at[:, :, 0:2]).then_inc(chain, 1)
                dve.wait_ge(chain, base + 7)
                for k in range(2):
                    dve.tensor_tensor(hit[:, k, :, :], per_expert(const["iota"][:, :].rearrange("p (a e) -> p a e", a=1)),
                                      per_expert(at[:, :, k:k + 1]), ALU.is_equal).then_inc(chain, 1)

            def weigh(c):
                base = c * STEPS + NORM + CHOOSE + PICK
                dve.wait_ge(s_tanh, c + 1)
                dve.tensor_scalar(weight[:, :, 0:1], tanh[:, :, :], 0.5, 0.5, ALU.mult, ALU.add)
                dve.tensor_scalar(weight[:, :, 1:2], tanh[:, :, :], -0.5, 0.5, ALU.mult, ALU.add).then_inc(chain, 1)
                dve.wait_ge(chain, base + 1)
                for k in range(2):
                    last = dve.tensor_tensor(hit[:, k, :, :], hit[:, k, :, :], per_expert(weight[:, :, k:k + 1]), ALU.mult)
                last.then_inc(chain, 1)
                dve.wait_ge(chain, base + 2)
                dve.tensor_tensor(gates[:, :, :], hit[:, 0, :, :], hit[:, 1, :, :], ALU.add).then_inc(chain, 1)
                dve.wait_ge(chain, base + 3)
                dve.wait_ge(s_GT, c)
                three_parts(dve, chain, base + 3, gates[:, :, :], gparts[:, :, 0:E1], rest[:, :, :],
                            gparts[:, :, E1:2 * E1], rest2[:, :, :], gparts[:, :, 2 * E1:3 * E1]).then_inc(s_gp, 1)

            def hidden(c, par, u):
                n = c * UNITS + u
                b = u % 3
                dve.wait_ge(s_gelu, n + 4)
                dve.wait_ge(s_down, n + 1)
                if u == SH:
                    dve.tensor_scalar(hid[:, b, :], act_out[:, b, :], 0.1, None, ALU.mult).then_inc(s_hid, 1)
                    return
                e = TILE_EXPERT[u]
                if u == TILE_EXPERT.index(e):
                    dve.wait_ge(s_Gc, c * E1 + e + 1)
                dve.scalar_tensor_tensor(out=hid[:, b, :], in0=act_out[:, b, :], scalar=gelu_b1[:, u:u + 1],
                                         in1=gate_bc[:, par, e, :], op0=ALU.subtract, op1=ALU.mult).then_inc(s_hid, 1)

            def mix(c, par):
                dve.wait_ge(s_down, c * UNITS + UNITS + 3)
                dve.wait_ge(s_end, c + 1)
                dve.tensor_scalar(mixed[:, :], acc[:, par, :], every[:, 0:1], None, ALU.add).then_inc(s_mixed, 1)

            def add(c):
                dve.wait_ge(s_end, c + 2)
                for t in range(0, CT, 2):
                    here = x[:, tiles(c, t, 2), :]
                    last = dve.scalar_tensor_tensor(out=here, in0=end[:, t:t + 2, :], scalar=0.5, in1=here,
                                                    op0=ALU.mult, op1=ALU.add)
                last.then_inc(s_add, 1)
                dve.wait_ge(s_add, 2 * c + 2)
                for t in range(0, CT, 2):
                    here = x[:, tiles(c, t, 2), :]
                    last = dve.tensor_tensor(here, here, end_bias[:, :, :], ALU.add)
                last.then_inc(s_add, 1)

            def chunk(c, par, last=False):
                for u in range(3, UNITS):
                    hidden(c, par, u)
                    if not last:
                        if u == 3:
                            norm_stats(c + 1)
                        if u == 4:
                            norm_apply(c + 1)
                        if u == 9:
                            choose(c + 1)
                        if u == 10:
                            pick(c + 1)
                        if u == 11:
                            weigh(c + 1)
                if not last:
                    hidden(c + 1, 1 - par, 0)
                mix(c, par)
                if not last:
                    hidden(c + 1, 1 - par, 1)
                    hidden(c + 1, 1 - par, 2)
                add(c)

            dve.sem_inc(s_hid, 3)
            dve.sem_inc(s_mixed, 2)
            dve.sem_inc(s_add, 1)
            constants()
            norm_stats(0)
            norm_apply(0)
            choose(0)
            pick(0)
            weigh(0)
            for u in range(3):
                hidden(0, 0, u)
            with dve.Fori(0, CHUNKS - 2, 2) as c:
                chunk(c, 0)
                chunk(c + 1, 1)
            chunk(CHUNKS - 2, 0)
            chunk(CHUNKS - 1, 1, last=True)

        @block.gpsimd
        def _(pool):
            with pool.Fori(0, CHUNKS) as c:
                pool.wait_ge(s_var, c + 1)
                pool.tensor_tensor(rstd[:, :], var_eps[:, :], const["minus_half"][:, 0:CT], ALU.pow).then_inc(s_rstd, 1)

        @block.scalar
        def _(act):
            def keep_half(c, k):
                act.wait_ge(s_T, c * KD + k + 1)
                act.wait_ge(s_h, c)
                act.activation(xnT[:, k, :], misc[:, :], ACT.Copy).then_inc(s_Tc, 1)

            def core_in(c, par):
                act.wait_ge(s_Tc, c * KD + KD)
                if not (isinstance(c, int) and c == 0):
                    act.wait_ge(s_end, c)
                for k in range(KD):
                    last = act.activation(core[:, par, k, :], xnT[:, k, :], ACT.Gelu)
                last.then_inc(s_core, 1)

            def h_in(c, par):
                act.wait_ge(s_h, c + 1)
                act.activation(gelu_h[:, par, :], misc[:, :], ACT.Gelu, bias=w["down_b"][:, 0:1]).then_inc(s_gh, 1)

            def exps(c):
                act.wait_ge(s_shift, c + 1)
                act.activation(expd[:, :, :], shifted[:, :, :], ACT.Exp).then_inc(s_exp, 1)

            def tanhs(c):
                act.wait_ge(s_diff, c + 1)
                act.activation(tanh[:, :, :], diff[:, :, :], ACT.Tanh, scale=0.5).then_inc(s_tanh, 1)

            def keep_gates(c):
                act.wait_ge(s_GT, c + 1)
                act.activation(gT[:, :], misc_bf, ACT.Copy).then_inc(s_gT, 1)

            def keep_spread(c, par, e):
                act.wait_ge(s_G, c * E1 + e + 1)
                act.activation(gate_bc[:, par, e, :], misc[:, :], ACT.Copy).then_inc(s_Gc, 1)

            def unit(c, u):
                n = c * UNITS + u
                act.wait_ge(s_u, n + 1)
                act.wait_ge(s_hid, n + 1)
                act.activation(act_out[:, u % 3, :], u_ps[:, u % 3, :], ACT.Gelu, bias=w["b1"][:, u:u + 1]).then_inc(s_gelu, 1)

            def chunk(c, par, last=False):
                for u in range(3, UNITS):
                    unit(c, u)
                    if not last:
                        if u == 5:
                            keep_half(c + 1, 0)
                        if u == 6:
                            keep_half(c + 1, 1)
                        if u == 7:
                            core_in(c + 1, 1 - par)
                        if u == 9:
                            h_in(c + 1, 1 - par)
                        if u == 10:
                            exps(c + 1)
                        if u == 11:
                            tanhs(c + 1)
                        if u == 12:
                            keep_gates(c + 1)
                        if u >= 13:
                            keep_spread(c + 1, 1 - par, u - 13)
                if not last:
                    for u in range(3):
                        unit(c + 1, u)

            act.activation(gelu_b1[:, :], w["b1"][:, 0:HT1], ACT.Gelu).then_inc(s_gb1, 1)
            act.sem_inc(s_gelu, 3)
            for k in range(KD):
                keep_half(0, k)
            core_in(0, 0)
            h_in(0, 0)
            exps(0)
            tanhs(0)
            keep_gates(0)
            for e in range(E1):
                keep_spread(0, 0, e)
            for u in range(3):
                unit(0, u)
            with act.Fori(0, CHUNKS - 2, 2) as c:
                chunk(c, 0)
                chunk(c + 1, 1)
            chunk(CHUNKS - 2, 0)
            chunk(CHUNKS - 1, 1, last=True)

        @block.tensor
        def _(pe):
            def constants():
                pe.wait_ge(s_gb1, 1)
                for u in range(HT1):
                    last = pe.matmul(misc[:, 0:1], w["w2"][:, u, :], gelu_b1[:, u:u + 1], start=(u == 0), stop=(u == HT1 - 1))
                last.then_inc(s_every, 1)
                pe.wait_ge(s_everyd, 1)

            def turn_half(c, k):
                if k == 0:
                    pe.wait_ge(s_xn, c + 1)
                    pe.wait_ge(s_Gc, c * E1)
                else:
                    pe.wait_ge(s_Tc, c * KD + k)
                for t in range(CT):
                    last = pe.transpose(misc[:, t * P:(t + 1) * P], xn[:, t, k * P:(k + 1) * P], const["ident"][:, :])
                last.then_inc(s_T, 1)

            def route(c):
                pe.wait_ge(s_Tc, c * KD + KD)
                for t in range(CT):
                    for k in range(KD):
                        last = pe.matmul(misc[:, t * E1:(t + 1) * E1], xnT[:, k, t * P:(t + 1) * P],
                                         w["router"][:, k, :], start=(k == 0), stop=(k == KD - 1))
                last.then_inc(s_R, 1)

            def h_out(c):
                pe.wait_ge(s_Rc, c + 1)
                pe.wait_ge(s_core, c + 1)
                for k in range(KD):
                    last = pe.matmul(misc[:, :], w["down_w"][:, k, :], xnT[:, k, :], start=(k == 0), stop=(k == KD - 1))
                last.then_inc(s_h, 1)

            def turn_gates(c):
                pe.wait_ge(s_gh, c + 1)
                pe.wait_ge(s_gp, c + 1)
                for t in range(CT):
                    last = pe.transpose(misc_bf[:, t * P:(t + 1) * P], gparts[:, t, :], const["ident_bf"][:, :])
                last.then_inc(s_GT, 1)

            def spread(c, e):
                if e == 0:
                    pe.wait_ge(s_gT, c + 1)
                else:
                    pe.wait_ge(s_Gc, c * E1 + e)
                pe.matmul(misc[:, :], const["pick_gate1"][:, e, :], gT[:, :], start=True, stop=True).then_inc(s_G, 1)

            def up(c, par, u):
                n = c * UNITS + u
                if u == 0:
                    pe.wait_ge(s_gh, c + 1)
                pe.wait_ge(s_gelu, n + 1)
                pe.matmul(u_ps[:, u % 3, :], w["w1"][:, u, :], gelu_h[:, par, :], start=True, stop=True).then_inc(s_u, 1)

            def down(c, par, u):
                n = c * UNITS + u
                if u == 0:
                    pe.wait_ge(s_mixed, c + 1)
                pe.wait_ge(s_hid, n + 4)
                pe.matmul(acc[:, par, :], w["w2"][:, u, :], hid[:, u % 3, :],
                          start=(u == 0), stop=(u == UNITS - 1)).then_inc(s_down, 1)

            def finish(c, par):
                pe.wait_ge(s_mixed, c + 3)
                pe.wait_ge(s_add, 2 * c + 1)
                for t in range(CT):
                    for k in range(KD):
                        pe.matmul(end[:, t, :], core[:, par, k, t * P:(t + 1) * P], w["core_w"][:, k, :],
                                  start=(k == 0 and t % 2 == 0), stop=False, skip_group_check=True)
                    last = pe.matmul(end[:, t, :], mixed[:, t * P:(t + 1) * P], w["up_w"][:, :],
                                     start=False, stop=True, skip_group_check=True)
                last.then_inc(s_end, 1)

            def chunk(c, par, last=False):
                down(c, par, 0)
                for u in range(3, UNITS):
                    up(c, par, u)
                    down(c, par, u - 2)
                    if not last:
                        if u == 5:
                            turn_half(c + 1, 0)
                        if u == 6:
                            turn_half(c + 1, 1)
                        if u == 7:
                            route(c + 1)
                        if u == 9:
                            h_out(c + 1)
                        if u == 12:
                            turn_gates(c + 1)
                        if u >= 13:
                            spread(c + 1, u - 13)
                if not last:
                    up(c + 1, 1 - par, 0)
                down(c, par, UNITS - 2)
                if not last:
                    up(c + 1, 1 - par, 1)
                down(c, par, UNITS - 1)
                if not last:
                    up(c + 1, 1 - par, 2)
                finish(c, par)

            pe.sem_inc(s_down, 3)
            pe.sem_inc(s_end, 1)
            constants()
            turn_half(0, 0)
            turn_half(0, 1)
            route(0)
            h_out(0)
            turn_gates(0)
            for e in range(E1):
                spread(0, e)
            for u in range(3):
                up(0, 0, u)
            with pe.Fori(0, CHUNKS - 2, 2) as c:
                chunk(c, 0)
                chunk(c + 1, 1)
            chunk(CHUNKS - 2, 0)
            chunk(CHUNKS - 1, 1, last=True)


def attention_inputs(nc, tag, x, w, const, qk_stacks, v_rows):
    with ExitStack() as ctx:
        ctx.enter_context(nc.cleanup_on_exit())

        def sb(name, shape, dt=F32):
            return ctx.enter_context(nc.sbuf_tensor(f"{tag}_{name}", shape, dt))

        def psum(name, shape, dt=F32):
            return ctx.enter_context(nc.psum_tensor(f"{tag}_{name}", shape, dt))

        def sem(name):
            return nc.alloc_semaphore(f"{tag}_{name}")

        TQ = 4
        xn = sb("xn", [P, CT, D])
        xnT = sb("xnT", [P, 2, KD, CH])
        stats = sb("stats", [P, CT, 6])
        mean_var = sb("mean_var", [P, CT, 2])
        var_eps = sb("var_eps", [P, CT])
        rstd = sb("rstd", [P, CT])
        rest = sb("rest", [P, 2, 2, CH])
        parts = sb("parts", [P, TQ, 3, CH], BF16)
        v_pad = sb("v_pad", [P, 2, CT, HEADS, 2 * DH])

        half = psum("half", [P, 2, CH])
        qk = psum("qk", [P, 4, CH])
        v_ps = psum("v", [P, 2, 2, D])

        s_stat = sem("stats_ready")
        s_mv = sem("mean_var_ready")
        s_var = sem("var_ready")
        s_rstd = sem("rstd_ready")
        s_xn = sem("xn_ready")
        s_T = sem("half_transposed")
        s_Tc = sem("half_kept")
        s_qk = sem("qk_ready")
        s_v = sem("v_ready")
        s_p1 = sem("part1_ready")
        chain = sem("dve_steps")
        s_parts = sem("parts_ready")
        s_pad = sem("v_kept")
        s_pads = sem("v_pad_set")
        s_st = [sem(f"parts_stored_{m}") for m in range(TQ)]
        s_vst = [sem("v_stored_even"), sem("v_stored_odd")]

        def tiles(c, t, n=1):
            return slice(c * CT + t, c * CT + t + n) if isinstance(c, int) else bass.ds(c * CT + t, n)

        block = ctx.enter_context(nc.Block())

        @block.vector
        def _(dve):
            def norm(c):
                for t in range(CT):
                    last = dve.bn_stats(stats[:, t, :], x[:, tiles(c, t), :].rearrange("p a d -> p (a d)"))
                last.then_inc(s_stat, 1)
                dve.wait_ge(s_stat, c + 1)
                dve.sem_inc(s_mv, 1)
                for t in range(CT):
                    last = dve.bn_aggr(mean_var[:, t, :], stats[:, t, :])
                last.then_inc(s_mv, 1)
                dve.wait_ge(s_mv, 2 * c + 2)
                dve.tensor_scalar(var_eps[:, :], mean_var[:, :, 1], EPS, None, ALU.add).then_inc(s_var, 1)
                dve.wait_ge(s_rstd, c + 1)
                if not (isinstance(c, int) and c == 0):
                    dve.wait_ge(s_T, c * KD)
                for t in range(CT):
                    last = dve.tensor_scalar(xn[:, t, :], x[:, tiles(c, t), :].rearrange("p a d -> p (a d)"),
                                             mean_var[:, t, 0:1], rstd[:, t:t + 1], ALU.subtract, ALU.mult)
                last.then_inc(s_xn, 1)

            def split(c, m):
                base = c * TQ * 3 + 3 * m
                dve.wait_ge(s_p1, c * TQ + m + 1)
                dve.tensor_tensor(rest[:, m % 2, 0, :], qk[:, m, :], parts[:, m, 0, :], ALU.subtract).then_inc(chain, 1)
                dve.wait_ge(chain, base + 1)
                dve.tensor_copy(parts[:, m, 1, :], rest[:, m % 2, 0, :]).then_inc(chain, 1)
                dve.wait_ge(chain, base + 2)
                dve.tensor_tensor(rest[:, m % 2, 1, :], rest[:, m % 2, 0, :], parts[:, m, 1, :], ALU.subtract).then_inc(chain, 1)
                dve.wait_ge(chain, base + 3)
                dve.tensor_copy(parts[:, m, 2, :], rest[:, m % 2, 1, :]).then_inc(s_parts, 1)

            def chunk(c, par, last=False):
                split(c, 0)
                if not last:
                    norm(c + 1)
                for m in range(1, TQ):
                    split(c, m)

            norm(0)
            chunk(0, 0)
            with dve.Fori(0, CHUNKS // 2 - 1) as pair:
                c = pair * 2 + 1
                chunk(c, 1)
                chunk(c + 1, 0)
            chunk(CHUNKS - 1, 1, last=True)

        @block.gpsimd
        def _(pool):
            pool.memset(v_pad[:, :, :, :, :], 0.0).then_inc(s_pads, 1)
            pool.wait_ge(s_pads, 1)
            for par in range(2):
                pool.memset(v_pad[:, par, :, :, DH:DH + 1], 1.0).then_inc(s_pads, 1)
            with pool.Fori(0, CHUNKS) as c:
                pool.wait_ge(s_var, c + 1)
                pool.tensor_tensor(rstd[:, :], var_eps[:, :], const["minus_half"][:, 0:CT], ALU.pow).then_inc(s_rstd, 1)

        @block.scalar
        def _(act):
            def keep_half(c, par, k):
                act.wait_ge(s_T, c * KD + k + 1)
                if not (isinstance(c, int) and c <= 1):
                    act.wait_ge(s_v, 2 * (c - 1))
                act.activation(xnT[:, par, k, :], half[:, k, :], ACT.Copy).then_inc(s_Tc, 1)

            def part1(c, m):
                act.wait_ge(s_qk, c * TQ + m + 1)
                if not (isinstance(c, int) and c == 0):
                    act.wait_ge(s_st[m], 16 * len(Q_PART) * c)
                act.activation(parts[:, m, 0, :], qk[:, m, :], ACT.Copy).then_inc(s_p1, 1)

            def keep_v(c, par, r):
                act.wait_ge(s_v, 2 * c + r + 1)
                if not (isinstance(c, int) and c <= 1):
                    act.wait_ge(s_vst[par], 16 * (c // 2))
                act.activation(v_pad[:, par, 2 * r:2 * r + 2, :, 0:DH],
                               v_ps[:, r, :, :].rearrange("p a (h d) -> p a h d", d=DH), ACT.Copy).then_inc(s_pad, 1)

            def chunk(c, par, last=False):
                for m in range(TQ):
                    part1(c, m)
                if not last:
                    for k in range(KD):
                        keep_half(c + 1, 1 - par, k)
                for r in range(2):
                    keep_v(c, par, r)

            act.wait_ge(s_pads, 3)
            for k in range(KD):
                keep_half(0, 0, k)
            chunk(0, 0)
            with act.Fori(0, CHUNKS // 2 - 1) as pair:
                c = pair * 2 + 1
                chunk(c, 1)
                chunk(c + 1, 0)
            chunk(CHUNKS - 1, 1, last=True)

        @block.tensor
        def _(pe):
            def turn_halves(c):
                pe.wait_ge(s_xn, c + 1)
                if not (isinstance(c, int) and c == 0):
                    pe.wait_ge(s_Tc, c * KD)
                for k in range(KD):
                    for t in range(CT):
                        last = pe.transpose(half[:, k, t * P:(t + 1) * P], xn[:, t, k * P:(k + 1) * P], const["ident"][:, :])
                    last.then_inc(s_T, 1)

            def project(c, par, m):
                weight = w["wq"] if m < 2 else w["wk"]
                if not (isinstance(c, int) and c == 0):
                    pe.wait_ge(s_parts, (c - 1) * TQ + m + 1)
                for k in range(KD):
                    last = pe.matmul(qk[:, m, :], weight[:, k, (m % 2) * P:(m % 2 + 1) * P], xnT[:, par, k, :],
                                     start=(k == 0), stop=(k == KD - 1))
                last.then_inc(s_qk, 1)

            def project_v(c, par, r):
                if not (isinstance(c, int) and c == 0):
                    pe.wait_ge(s_pad, 2 * (c - 1) + r + 1)
                for a in range(2):
                    t = 2 * r + a
                    for k in range(KD):
                        last = pe.matmul(v_ps[:, r, a, :], xnT[:, par, k, t * P:(t + 1) * P], w["wv"][:, k, :],
                                         start=(k == 0), stop=(k == KD - 1))
                last.then_inc(s_v, 1)

            def chunk(c, par, last=False):
                pe.wait_ge(s_Tc, c * KD + KD)
                for m in range(TQ):
                    project(c, par, m)
                if not last:
                    turn_halves(c + 1)
                for r in range(2):
                    project_v(c, par, r)

            turn_halves(0)
            chunk(0, 0)
            with pe.Fori(0, CHUNKS // 2 - 1) as pair:
                c = pair * 2 + 1
                chunk(c, 1)
                chunk(c + 1, 0)
            chunk(CHUNKS - 1, 1, last=True)

        @block.sync
        def _(sp):
            rows = v_rows.rearrange("(n p) f -> p n f", p=P)

            def chunk(c, par):
                here = slice(c * CH, (c + 1) * CH) if isinstance(c, int) else bass.ds(c * CH, CH)
                for m in range(TQ):
                    heads = slice((m % 2) * P // DH, (m % 2 + 1) * P // DH)
                    sp.wait_ge(s_parts, c * TQ + m + 1)
                    for n, part in enumerate(K_PART if m // 2 else Q_PART):
                        sp.dma_start(qk_stacks[m // 2, heads, n * DH:(n + 1) * DH, here], parts[:, m, part, :]).then_inc(s_st[m], 16)
                sp.wait_ge(s_pad, 2 * c + 2)
                sp.dma_start(rows[:, tiles(c, 0, CT), :],
                             v_pad[:, par, :, :, :].rearrange("p t h d -> p t (h d)")).then_inc(s_vst[par], 16)

            chunk(0, 0)
            with sp.Fori(0, CHUNKS // 2 - 1) as pair:
                c = pair * 2 + 1
                chunk(c, 1)
                chunk(c + 1, 0)
            chunk(CHUNKS - 1, 1)
            for m in range(TQ):
                sp.wait_ge(s_st[m], 16 * len(Q_PART) * CHUNKS)
            for par in range(2):
                sp.wait_ge(s_vst[par], 16 * CHUNKS // 2)


def attention(nc, tag, x, w, const, qk_stacks, v_rows):
    with ExitStack() as ctx:
        ctx.enter_context(nc.cleanup_on_exit())

        def sb(name, shape, dt=F32):
            return ctx.enter_context(nc.sbuf_tensor(f"{tag}_{name}", shape, dt))

        def psum(name, shape, dt=F32):
            return ctx.enter_context(nc.psum_tensor(f"{tag}_{name}", shape, dt))

        def sem(name):
            return nc.alloc_semaphore(f"{tag}_{name}")

        STEPS = B * HG
        HALF = 512
        qs = [sb(f"q_stack{i}", [QK_ROWS + M_ROWS, GH, T], BF16) for i in range(2)]
        ks = [sb(f"k_stack{i}", [QK_ROWS + M_ROWS, GH, T], BF16) for i in range(2)]
        vg = [sb(f"v_group{i}", [P, BT, P]) for i in range(2)]
        probs = sb("probs", [P, 2, GH, T])
        max_of = sb("max_of", [P, 2, GH, BT])
        max_half = sb("max_half", [P, GH * BT])
        row_max = sb("row_max", [P, GH * BT])
        m_rest = sb("m_rest", [P, 2, GH * BT])
        m_parts = sb("m_parts", [P, M_ROWS, GH * BT], BF16)
        m_rows = sb("m_rows", [M_ROWS * GH * BT, P], BF16)
        exp_m = sb("exp_m", [P, T])
        v_masked = sb("v_masked", [P, T])
        masked_out = sb("masked_out", [P, T])
        out_sum = sb("out_sum", [P, T])
        inv = sb("inv", [P, BT, GH])
        inv_wide = sb("inv_wide", [P, BT, GH, P // GH])
        out_n = sb("out_n", [P, T])

        a_ps = psum("a", [P, 2, HALF])
        b_ps = psum("b", [P, 3, HALF])
        o_ps = psum("o", [P, T])
        misc = psum("misc", [P, HALF])
        misc_bf = misc[0:M_ROWS * GH * BT, 0:P // 2].bitcast(BF16)

        A_TILE = [[(h, lo, min(lo + HALF, P * (i + 1))) for h in range(GH) for lo in range(0, P * (i + 1), HALF)]
                  for i in range(BT)]
        A_UNITS = [(i, *u) for i in range(BT) for u in A_TILE[i]]
        B_UNITS = {j: [(h, lo, (lo // HALF + 1) * HALF) for lo in ([P * j, HALF] if j < BT // 2 else [P * j])
                       for h in range(GH)] for j in range(BT)}
        NA = len(A_UNITS)
        B_FIRST = [sum(len(B_UNITS[j]) for j in range(n)) for n in range(BT + 1)]
        NB = B_FIRST[BT]
        EARLY = 10
        NEXT = [EARLY, A_UNITS.index((BT // 2, 0, 0, HALF)), 25, 33, 41, NA, NA, NA, NA]
        AFTER = [0, 0, 0, 0, 0, 0, 2, 6, EARLY]
        EXPM0, EXPM1, DEN, VS1, VS0, INV0, INV1, PROJ0, PROJ1, PROJ2, MAXT, PROJ3 = ORDER = range(12)
        BEFORE = (DEN, INV0, INV1, PROJ0, PROJ1, PROJ2, PROJ3)
        TASKS = [[[EXPM0], [EXPM1]], [[DEN], [VS1]], [[VS0], [INV0]], [[INV1], [PROJ0]],
                 [[PROJ1]], [[PROJ2]], [[MAXT]], [[PROJ3]]]

        s_ld = [sem(f"half{half}_loaded_{par}") for par in ("even", "odd") for half in range(2)]
        s_ldv = [sem("v_loaded_even"), sem("v_loaded_odd")]
        s_vm = sem("v_masked_tile_ready")
        s_ones = sem("constants_set")
        s_em = sem("exp_max_begun")
        s_A = sem("a_scores_ready")
        s_Ac = sem("a_scores_used")
        chain = sem("dve_steps")
        s_mp = sem("max_parts_ready")
        s_m = [sem("max_rows_even"), sem("max_rows_odd")]
        s_B = sem("b_scores_ready")
        s_exp = sem("b_scores_used")
        s_pv = sem("tile_multiplied")
        s_mo = sem("masked_out_ready")
        s_sum = sem("out_sum_ready")
        s_fill = sem("misc_filled")
        s_used = sem("misc_used")
        s_inv = sem("inv_ready")
        s_invw = sem("inv_wide_ready")
        s_on = sem("out_normalised")

        def present(it):
            if not isinstance(it, int):
                return list(ORDER)
            return [k for k in ORDER if not (it == 0 and k in BEFORE) and not (it == STEPS - 1 and k == MAXT)
                    and not (it == STEPS and k not in BEFORE)]

        def task(it, k):
            if isinstance(it, int):
                return 1 + sum(len(present(n)) for n in range(it)) + present(it).index(k)
            return it * len(ORDER) - len(BEFORE) + 1 + k

        def before_max(it):
            return 0 if isinstance(it, int) and it == 0 else task(it - 1, MAXT)

        def plan(j):
            nb, halves = len(B_UNITS[j]), [] if j == 0 else sorted({lo // HALF for _, lo, _ in B_UNITS[j - 1]})
            order = []
            for u in range(nb):
                order.append(("b", u))
                for name, until in (("a", NEXT), ("early a", AFTER)):
                    n = until[j + 1] - until[j]
                    order += [(name, until[j] + k) for k in range(n * u // nb, n * (u + 1) // nb)]
                if u % GH == 1:
                    order += [("t", k) for k in TASKS[j][u // GH]]
                if u % GH == GH - 1:
                    here = halves if u == nb - 1 else halves[:1]
                    halves = halves[len(here):]
                    order += [("v", (half, half == 1)) for half in here]
            return order

        block = ctx.enter_context(nc.Block())

        @block.sync
        def _(sp):
            rows = v_rows.rearrange("(n p) f -> p n f", p=P)

            def load(it, par, half):
                b, g = it // HG, it % HG
                for which, stack in ((0, qs), (1, ks)):
                    sp.dma_start(stack[par][0:QK_ROWS, :, half * HALF:(half + 1) * HALF],
                                 qk_stacks[which, bass.ds(g * GH, GH), :, bass.ds(b * T + half * HALF, HALF)]
                                 .rearrange("h r t -> r h t")).then_inc(s_ld[2 * par + half], 16)

            def load_v(it, par):
                b, g = it // HG, it % HG
                sp.dma_start(vg[par][:, :, :], rows[:, bass.ds(b * BT, BT), bass.ds(g * P, P)]).then_inc(s_ldv[par], 16)

            def max_rows(it, par):
                sp.wait_ge(s_used, before_max(it) + 1)
                for j in range(M_ROWS):
                    sp.dma_start(qs[par][QK_ROWS + j:QK_ROWS + j + 1, :, :].rearrange("a h t -> a (h t)"),
                                 m_rows[j * GH * BT:(j + 1) * GH * BT, :]).then_inc(s_m[par], 16)

            def step(it, par, last=False, load_next=True):
                if load_next:
                    sp.wait_ge(s_used, task(it, EXPM1) + 1)
                    sp.wait_ge(s_B, it * NB + B_FIRST[BT // 2])
                    load(it + 2, par, 0)
                if not last:
                    max_rows(it + 1, 1 - par)
                if load_next:
                    sp.wait_ge(s_pv, it * BT + BT + 2)
                    load(it + 2, par, 1)
                    load_v(it + 2, par)

            for it in range(2):
                for half in range(2):
                    load(it, it, half)
                load_v(it, it)
            max_rows(0, 0)
            step(0, 0)
            step(1, 1)
            with sp.Fori(1, STEPS // 2 - 1) as pair:
                it = pair * 2
                step(it, 0)
                step(it + 1, 1)
            step(STEPS - 2, 0, load_next=False)

        @block.gpsimd
        def _(pool):
            def masked_part(it):
                pool.wait_ge(s_used, task(it, VS0) + 1)
                if not (isinstance(it, int) and it == 0):
                    pool.wait_ge(s_sum, it)
                pool.tensor_tensor(masked_out[:, 0:T - 1], exp_m[:, 0:T - 1], v_masked[:, 0:T - 1], ALU.mult).then_inc(s_mo, 1)

            pool.memset(masked_out[:, T - 1:T], 0.0).then_inc(s_ones, 1)
            masked_part(0)
            masked_part(1)
            with pool.Fori(1, STEPS // 2) as pair:
                it = pair * 2
                masked_part(it)
                masked_part(it + 1)

        @block.scalar
        def _(act):
            def exp_unit(it, j, u):
                h, lo, hi = B_UNITS[j][u]
                n = B_FIRST[j] + u
                if u == 0:
                    act.wait_ge(s_pv, it * BT + j + 1)
                act.wait_ge(s_B, it * NB + n + 1)
                act.activation(probs[:, j % 2, h, lo:hi], b_ps[:, n % 3, lo % HALF:(hi - 1) % HALF + 1],
                               ACT.Exp, scale=float(T) ** -0.5).then_inc(s_exp, 1)

            def keep_max(it):
                act.wait_ge(s_fill, before_max(it) + 1)
                if not (isinstance(it, int) and it == 0):
                    act.wait_ge(s_B, (it - 1) * NB + 1)
                act.activation(m_rows[:, :], misc_bf, ACT.Copy).then_inc(s_used, 1)

            def task_of_act(it, k):
                if k in present(it):
                    if k in (EXPM0, EXPM1):
                        c = (k == EXPM1) * HALF
                        act.wait_ge(s_fill, task(it, k) + 1)
                        if k == EXPM0 and not (isinstance(it, int) and it == 0):
                            act.wait_ge(s_mo, it)
                        act.activation(exp_m[:, c:c + HALF], misc[:, :], ACT.Exp, scale=float(T) ** -0.5).then_inc(s_used, 1)
                    if k in (VS0, VS1):
                        act.wait_ge(s_fill, task(it, k) + 1)
                        for i in reversed(range(BT // 2, BT) if k == VS1 else range(BT // 2)):
                            here = misc[:, (i % (BT // 2)) * P + (i == 0):(i % (BT // 2) + 1) * P]
                            out = v_masked[:, max(i * P - 1, 0):(i + 1) * P - 1]
                            if i == BT - 1:
                                last = act.activation(out, here, ACT.Copy)
                            else:
                                act.wait_ge(s_vm, it * BT + BT - 1 - i)
                                last = act.activation(out, here, ACT.Identity, bias=v_masked[:, (i + 1) * P - 1:(i + 1) * P])
                            last.then_inc(s_vm, 1)
                        act.wait_ge(s_vm, it * BT + (BT // 2 if k == VS1 else BT))
                        act.sem_inc(s_used, 1)
                    if k == DEN:
                        act.wait_ge(s_inv, it)
                        if not (isinstance(it, int) and it == 1):
                            act.wait_ge(s_on, 2 * (it - 1))
                        act.activation(inv_wide[:, :, :, :].rearrange("p i h d -> p (i h) d"),
                                       inv[:, :, :].rearrange("p i (h a) -> p (i h) a", a=1).broadcast_to([P, BT * GH, P // GH]),
                                       ACT.Copy).then_inc(s_invw, 1)
                    if k == MAXT:
                        keep_max(it + 1)

            def step(it):
                for j in range(BT):
                    for what, u in plan(j):
                        if what == "b":
                            exp_unit(it, j, u)
                        if what == "t":
                            task_of_act(it, u)

            act.sem_inc(s_exp, 3)
            keep_max(0)
            step(0)
            step(1)
            with act.Fori(1, STEPS // 2 - 1) as pair:
                it = pair * 2
                step(it)
                step(it + 1)
            step(STEPS - 2)
            step(STEPS - 1)
            for k in BEFORE:
                task_of_act(STEPS, k)

        @block.vector
        def _(dve):
            def maximum(it, n):
                i, h, lo, hi = A_UNITS[n]
                dve.wait_ge(s_A, it * NA + n + 1)
                dve.tensor_reduce(max_of[:, lo // HALF, h, i:i + 1], a_ps[:, n % 2, 0:hi - lo], AX.X, ALU.max).then_inc(s_Ac, 1)

            M_STEPS = 6

            def finish_maxima(it):
                base = it * M_STEPS
                flat = lambda a: a.rearrange("p h i -> p (h i)")
                dve.wait_ge(s_Ac, it * NA + NA + 2)
                dve.tensor_tensor(max_half[:, :], flat(max_of[:, 0, :, :]), flat(max_of[:, 1, :, :]), ALU.max).then_inc(chain, 1)
                dve.wait_ge(chain, base + 1)
                dve.tensor_tensor(row_max[:, :], max_half[:, :], const["floor"][:, :], ALU.max).then_inc(chain, 1)
                dve.wait_ge(chain, base + 2)
                three_parts(dve, chain, base + 2, row_max[:, :], m_parts[:, 0, :], m_rest[:, 0, :],
                            m_parts[:, 1, :], m_rest[:, 1, :], m_parts[:, 2, :]).then_inc(s_mp, 1)

            def sum_up(it):
                dve.wait_ge(s_pv, it * BT + BT + 2)
                dve.wait_ge(s_mo, it + 1)
                if not (isinstance(it, int) and it == 0):
                    dve.wait_ge(s_on, 2 * it)
                for half in range(2):
                    c = slice(half * HALF, (half + 1) * HALF)
                    last = dve.tensor_tensor(out_sum[:, c], masked_out[:, c], o_ps[:, c], ALU.add)
                last.then_inc(s_sum, 1)

            def task_of_dve(it, k):
                if k in present(it):
                    if k == DEN:
                        dve.wait_ge(s_fill, task(it, k) + 1)
                        dve.reciprocal(inv[:, :, :].rearrange("p i h -> p (i h)"), misc[:, 0:BT * GH]).then_inc(s_inv, 1)
                        dve.wait_ge(s_inv, it)
                        dve.sem_inc(s_used, 1)
                    if k in (INV0, INV1):
                        half = (k == INV1) * 1
                        dve.wait_ge(s_fill, task(it, k) + 1)
                        c = slice(half * HALF, (half + 1) * HALF)
                        dve.tensor_tensor(out_n[:, c], out_sum[:, c], misc[:, :], ALU.mult).then_inc(s_on, 1)
                        dve.wait_ge(s_on, 2 * (it - 1) + half + 1)
                        dve.sem_inc(s_used, 1)
                    if k in (PROJ0, PROJ1, PROJ2, PROJ3):
                        dve.wait_ge(s_fill, task(it, k) + 1)
                        p = [PROJ0, PROJ1, PROJ2, PROJ3].index(k)
                        b = (it - 1) // HG
                        where = x[:, bass.ds(b * BT + 2 * p, 2), :]
                        dve.tensor_tensor(where, misc[:, :].rearrange("p (a d) -> p a d", a=2), where, ALU.add).then_inc(s_used, 1)

            def step(it, first=False, ahead=2):
                if not first:
                    sum_up(it - 1)
                for j in range(BT):
                    for what, u in plan(j):
                        if what == "early a" and ahead >= 2:
                            maximum(it + 2, u)
                        if what == "a" and ahead >= 1:
                            maximum(it + 1, u)
                            if u == NA - 1:
                                finish_maxima(it + 1)
                        if what == "t":
                            task_of_dve(it, u)

            dve.memset(max_of[:, :, :, :], -3e38).then_inc(s_ones, 1)
            for i in range(2):
                dve.memset(ks[i][QK_ROWS:QK_ROWS + M_ROWS, :, :], -1.0).then_inc(s_ones, 1)
            dve.sem_inc(s_Ac, 2)
            dve.wait_ge(s_ones, 4)
            for n in range(NA):
                maximum(0, n)
            finish_maxima(0)
            for n in range(EARLY):
                maximum(1, n)
            step(0, first=True)
            step(1)
            with dve.Fori(1, STEPS // 2 - 1) as pair:
                it = pair * 2
                step(it)
                step(it + 1)
            step(STEPS - 2, ahead=1)
            step(STEPS - 1, ahead=0)
            sum_up(STEPS - 1)
            for k in BEFORE:
                task_of_dve(STEPS, k)

        @block.tensor
        def _(pe):
            def score_a(it, par, n):
                i, h, lo, hi = A_UNITS[n]
                if (i, h, lo) in ((0, 0, 0), (BT // 2, 0, 0)):
                    pe.wait_ge(s_ld[2 * par + (i > 0)], 2 * 16 * (it // 2 + 1))
                diagonal = hi == P * (i + 1)
                pe.wait_ge(s_Ac, it * NA + n + 1)
                last = pe.matmul(a_ps[:, n % 2, 0:hi - lo], qs[par][0:QK_ROWS, h, i * P:(i + 1) * P],
                                 ks[par][0:QK_ROWS, h, lo:hi], start=True, stop=True)
                if diagonal:
                    last = pe.matmul(a_ps[:, n % 2, hi - P - lo:hi - lo], const["ident_bf"][:, :], const["hide_right"][:, :],
                                     start=False, stop=True, skip_group_check=True)
                last.then_inc(s_A, 1)

            def score_b(it, par, j, u):
                h, lo, hi = B_UNITS[j][u]
                n = B_FIRST[j] + u
                if n == 0:
                    pe.wait_ge(s_ldv[par], 16 * (it // 2 + 1))
                    pe.wait_ge(s_m[par], 16 * M_ROWS * (it // 2 + 1))
                diagonal = lo == P * j
                at = lo % HALF
                pe.wait_ge(s_exp, it * NB + n + 1)
                last = pe.matmul(b_ps[:, n % 3, at:at + hi - lo], ks[par][:, h, j * P:(j + 1) * P], qs[par][:, h, lo:hi],
                                 start=True, stop=True)
                if diagonal:
                    last = pe.matmul(b_ps[:, n % 3, at:at + P], const["ident_bf"][:, :], const["hide_below"][:, :],
                                     start=False, stop=True, skip_group_check=True)
                last.then_inc(s_B, 1)

            def values(it, par, j, half, end):
                if j == 0 and half == 0 and not (isinstance(it, int) and it == 0):
                    pe.wait_ge(s_sum, it)
                pe.wait_ge(s_exp, it * NB + B_FIRST[j + 1] + 3)
                for h, lo, hi in B_UNITS[j]:
                    if lo // HALF == half:
                        last = pe.matmul(o_ps[32 * h:32 * h + 32, lo:hi], vg[par][:, j, 32 * h:32 * h + 32],
                                         probs[:, j % 2, h, lo:hi], start=(j == 0),
                                         stop=(j == (BT // 2 - 1 if half == 0 else BT - 1)), skip_group_check=True)
                if end:
                    last.then_inc(s_pv, 1)

            def turn_max(it):
                pe.wait_ge(s_mp, it + 1)
                if not (isinstance(it, int) and it == 0):
                    pe.wait_ge(s_used, before_max(it))
                pe.transpose(misc_bf, m_parts[:, :, :].rearrange("p j n -> p (j n)"), const["ident_bf"][:, :]).then_inc(s_fill, 1)

            def task_of_pe(it, par, k):
                if k == MAXT:
                    if k in present(it):
                        turn_max(it + 1)
                elif k in present(it):
                    pe.wait_ge(s_used, task(it, k))
                    if k == DEN:
                        pe.wait_ge(s_sum, it)
                        for i in range(BT):
                            mm = pe.matmul(misc[:, i * GH:(i + 1) * GH], out_sum[:, i * P:(i + 1) * P], const["pick_den"][:, :],
                                           start=True, stop=True)
                    if k in (INV0, INV1):
                        pe.wait_ge(s_invw, it)
                        for i in range(BT // 2):
                            mm = pe.matmul(misc[:, i * P:(i + 1) * P],
                                           inv_wide[:, (k == INV1) * (BT // 2) + i, :, :].rearrange("p h d -> p (h d)"),
                                           const["ident"][:, :], start=True, stop=True)
                    if k in (PROJ0, PROJ1, PROJ2, PROJ3):
                        pe.wait_ge(s_on, 2 * it)
                        p = [PROJ0, PROJ1, PROJ2, PROJ3].index(k)
                        g = (it - 1) % HG
                        for a in range(2):
                            i = 2 * p + a
                            mm = pe.matmul(misc[:, a * D:(a + 1) * D], out_n[:, i * P:(i + 1) * P],
                                           w["wo"][:, bass.ds(g, 1), :].rearrange("p a d -> p (a d)"), start=True, stop=True)
                    if k in (EXPM0, EXPM1):
                        c = (k == EXPM1) * HALF
                        pe.sem_inc(s_em, 1)
                        for h in range(GH):
                            mm = pe.matmul(misc[32 * h:32 * h + 32, :], ks[par][QK_ROWS:QK_ROWS + M_ROWS, h, 0:32],
                                           qs[par][QK_ROWS:QK_ROWS + M_ROWS, h, c:c + HALF], start=True, stop=True)
                    if k in (VS0, VS1):
                        for n in range(BT // 2):
                            mm = pe.matmul(misc[:, n * P:(n + 1) * P], vg[par][:, (k == VS1) * (BT // 2) + n, :],
                                           const["onward"][:, :], start=True, stop=True)
                    mm.then_inc(s_fill, 1)

            def step(it, par, ahead=2):
                for j in range(BT):
                    for what, u in plan(j):
                        if what == "b":
                            score_b(it, par, j, u)
                        if what == "early a" and ahead >= 2:
                            score_a(it + 2, par, u)
                        if what == "a" and ahead >= 1:
                            score_a(it + 1, 1 - par, u)
                        if what == "v":
                            values(it, par, j - 1, *u)
                        if what == "t":
                            task_of_pe(it, par, u)
                values(it, par, BT - 1, 1, end=True)

            pe.sem_inc(s_pv, 2)
            pe.wait_ge(s_ones, 4)
            for n in range(NA):
                score_a(0, 0, n)
            turn_max(0)
            for n in range(EARLY):
                score_a(1, 1, n)
            step(0, 0)
            step(1, 1)
            with pe.Fori(1, STEPS // 2 - 1) as pair:
                pe.get_value_cache().nocache = True
                it = pair * 2
                step(it, 0)
                step(it + 1, 1)
            step(STEPS - 2, 0, ahead=1)
            step(STEPS - 1, 1, ahead=0)
            for k in BEFORE:
                task_of_pe(STEPS, 0, k)


def scan_mixer(nc, tag, x, w, const):
    with ExitStack() as ctx:
        ctx.enter_context(nc.cleanup_on_exit())

        def sb(name, shape, dt=F32):
            return ctx.enter_context(nc.sbuf_tensor(f"{tag}_{name}", shape, dt))

        def psum(name, shape, dt=F32):
            return ctx.enter_context(nc.psum_tensor(f"{tag}_{name}", shape, dt))

        def sem(name):
            return nc.alloc_semaphore(f"{tag}_{name}")

        N2 = 2 * STATES
        SLOTS = KD * STATES
        a_exp = sb("a_exp", [P, KD, STATES])
        a_neg = sb("a_neg", [P, KD, STATES])
        xn = sb("xn", [P, CT, D])
        stats = sb("stats", [P, CT, 6])
        mean_var = sb("mean_var", [P, CT, 2])
        var_eps = sb("var_eps", [P, CT])
        rstd = sb("rstd", [P, CT])
        xnT = sb("xnT", [P, 2, KD, CH])
        low = sb("low", [RANK, CH])
        bc_rest = sb("bc_rest", [P, 2, CT, N2])
        bc_parts = sb("bc_parts", [P, CT, 3 * N2], BF16)
        bcT = sb("bcT", [3 * N2, 2, CH], BF16)
        z = sb("z", [P, KD, CH])
        z_abs = sb("z_abs", [P, KD, CH])
        z_exp = sb("z_exp", [P, KD, CH])
        z_log = sb("z_log", [P, KD, CH])
        delta = sb("delta", [P, 2, KD, CH])
        du = sb("du", [P, 2, KD, CH])
        decay = sb("decay", [P, 4, CH])
        drive = sb("drive", [P, 4, CH])
        h = sb("h", [P, 4, CH])
        state = sb("state", [P, SLOTS])
        c_bc = sb("c_bc", [P, 2, CH])
        hc = sb("hc", [P, 4, CH])
        y_out = sb("y_out", [P, KD, CH])

        b_ps = psum("b", [P, 2, CH])
        c_ps = psum("c", [P, CH])
        y_ps = psum("y", [P, KD, CH])
        misc = [psum(f"misc{i}", [P, CH]) for i in range(3)]

        once = sem("a_ready")
        s_stat = sem("stats_ready")
        s_mv = sem("mean_var_ready")
        s_var = sem("var_ready")
        s_rstd = sem("rstd_ready")
        s_xn = sem("xn_ready")
        s_fill = sem("misc_filled")
        s_act = sem("misc_used_by_act")
        s_dve = sem("misc_used_by_dve")
        chain = sem("part_steps")
        s_bcp = sem("bc_parts_ready")
        s_abs = sem("z_abs_ready")
        s_zexp = sem("z_exp_ready")
        s_log = sem("z_log_ready")
        s_delta = sem("delta_ready")
        s_du = sem("du_ready")
        s_b = sem("b_spread")
        s_c = sem("c_spread")
        s_ck = sem("c_kept")
        s_decay = sem("decay_ready")
        s_drive = sem("drive_ready")
        s_h = sem("h_ready")
        s_state = sem("state_kept")
        s_hc = sem("hc_ready")
        s_y = sem("y_added")
        s_yout = sem("y_out_ready")
        s_add = sem("chunk_added")

        TA, TB, LOW, BC, DT0, DT1, BCT, OUT0, OUT1 = range(9)
        ACT_USES = [TA, TB, LOW, BCT]
        DVE_USES = [BC, DT0, DT1, OUT0, OUT1]
        PREP = 7

        def bank(c, k):
            return misc[(k if c is None else PREP + k) % 3]

        def filled(c, k, last=False):
            if c is None:
                return k + 1
            return PREP + c * 9 + (k - PREP if last else k) + 1

        def used_act(c, k):
            return ACT_USES.index(k) + 1 + (0 if c is None else 4 * (c + 1))

        def used_dve(c, k, last=False):
            if c is None:
                return DVE_USES.index(k) + 1
            return 3 + 5 * c + DVE_USES.index(k) + 1 - (3 if last else 0)

        def chunk_of(c):
            return 0 if c is None else c + 1

        def tiles(c, t, n=1):
            return slice(c * CT + t, c * CT + t + n) if isinstance(c, int) else bass.ds(c * CT + t, n)

        block = ctx.enter_context(nc.Block())

        @block.vector
        def _(dve):
            def norm_stats(c):
                for t in range(CT):
                    last = dve.bn_stats(stats[:, t, :], x[:, tiles(c, t), :].rearrange("p a d -> p (a d)"))
                last.then_inc(s_stat, 1)
                dve.wait_ge(s_stat, c + 1)
                dve.sem_inc(s_mv, 1)
                for t in range(CT):
                    last = dve.bn_aggr(mean_var[:, t, :], stats[:, t, :])
                last.then_inc(s_mv, 1)
                dve.wait_ge(s_mv, 2 * c + 2)
                dve.tensor_scalar(var_eps[:, :], mean_var[:, :, 1], EPS, None, ALU.add).then_inc(s_var, 1)

            def norm_apply(c):
                dve.wait_ge(s_rstd, c + 1)
                for t in range(CT):
                    last = dve.tensor_scalar(xn[:, t, :], x[:, tiles(c, t), :].rearrange("p a d -> p (a d)"),
                                             mean_var[:, t, 0:1], rstd[:, t:t + 1], ALU.subtract, ALU.mult)
                last.then_inc(s_xn, 1)

            def split_bc(beside):
                c = chunk_of(beside)
                dve.wait_ge(s_fill, filled(beside, BC))
                whole = bank(beside, BC)[:, 0:CT * N2].rearrange("p (t n) -> p t n", t=CT)
                base = c * 4
                dve.tensor_copy(bc_parts[:, :, 0:N2], whole).then_inc(chain, 1)
                dve.wait_ge(chain, base + 1)
                dve.tensor_tensor(bc_rest[:, 0, :, :], whole, bc_parts[:, :, 0:N2], ALU.subtract).then_inc(s_dve, 1)
                dve.wait_ge(s_dve, used_dve(beside, BC))
                dve.tensor_copy(bc_parts[:, :, N2:2 * N2], bc_rest[:, 0, :, :]).then_inc(chain, 1)
                dve.wait_ge(chain, base + 2)
                dve.tensor_tensor(bc_rest[:, 1, :, :], bc_rest[:, 0, :, :], bc_parts[:, :, N2:2 * N2], ALU.subtract).then_inc(chain, 1)
                dve.wait_ge(chain, base + 3)
                dve.tensor_copy(bc_parts[:, :, 2 * N2:3 * N2], bc_rest[:, 1, :, :]).then_inc(chain, 1)
                dve.wait_ge(chain, base + 4)
                dve.sem_inc(s_bcp, 1)

            def biased(beside, m):
                c = chunk_of(beside)
                dve.wait_ge(s_fill, filled(beside, DT0 + m))
                dve.tensor_scalar(z[:, m, :], bank(beside, DT0 + m)[:, :], w["dt_b"][:, m:m + 1], None, ALU.add).then_inc(s_dve, 1)
                dve.wait_ge(s_dve, used_dve(beside, DT0 + m))
                dve.scalar_tensor_tensor(out=z_abs[:, m, :], in0=z[:, m, :], scalar=-1.0, in1=z[:, m, :], op0=ALU.mult, op1=ALU.max).then_inc(s_abs, 1)

            def soft(c, par, m):
                dve.wait_ge(s_log, 2 * c + m + 1)
                dve.scalar_tensor_tensor(out=delta[:, par, m, :], in0=z[:, m, :], scalar=0.0, in1=z_log[:, m, :],
                                         op0=ALU.max, op1=ALU.add).then_inc(s_delta, 1)
                dve.wait_ge(s_delta, 2 * c + m + 1)
                dve.tensor_tensor(du[:, par, m, :], delta[:, par, m, :], xnT[:, par, m, :], ALU.mult).then_inc(s_du, 1)

            def drives(c, par, s):
                m = s % 2
                if s == 0:
                    dve.wait_ge(s_du, 2 * c + 2)
                if m == 0:
                    dve.wait_ge(s_b, c * STATES + s // 2 + 1)
                dve.tensor_tensor(drive[:, s % 4, :], du[:, par, m, :], b_ps[:, (s // 2) % 2, :], ALU.mult).then_inc(s_drive, 1)

            def slot(c, par, s, last=False):
                n, m = c * SLOTS + s, s % 2
                if s + 1 < SLOTS:
                    drives(c, par, s + 1)
                elif not last:
                    drives(c + 1, 1 - par, 0)
                dve.wait_ge(s_drive, n + 3)
                dve.wait_ge(s_decay, n + 1)
                dve.wait_ge(s_hc, n + 1)
                if par == 0:
                    first = 0.0
                else:
                    dve.wait_ge(s_state, (c - 1) * STATES + s + 1)
                    first = state[:, s:s + 1]
                dve.tensor_tensor_scan(h[:, s % 4, :], decay[:, s % 4, :], drive[:, s % 4, :], first,
                                       ALU.mult, ALU.add).then_inc(s_h, 1)

            def out(c, par):
                dve.wait_ge(s_y, c * SLOTS + SLOTS + 4)
                for m in range(KD):
                    last = dve.scalar_tensor_tensor(out=y_out[:, m, :], in0=xnT[:, par, m, :], scalar=w["D"][:, m:m + 1],
                                                    in1=y_ps[:, m, :], op0=ALU.mult, op1=ALU.add)
                last.then_inc(s_yout, 1)

            def add(c, last):
                for r in range(2):
                    dve.wait_ge(s_fill, filled(c, OUT0 + r, last))
                    here = x[:, tiles(c, 2 * r, 2), :]
                    b = bank(c, OUT0 + r if not last else r)
                    dve.tensor_tensor(here, b[:, :].rearrange("p (a d) -> p a d", a=2), here, ALU.add).then_inc(s_dve, 1)

            def chunk(c, par, last=False):
                for s in range(3, SLOTS):
                    slot(c, par, s, last)
                    if not last:
                        if s == 4:
                            norm_stats(c + 1)
                        if s == 6:
                            norm_apply(c + 1)
                        if s == 14:
                            split_bc(c)
                        if s in (17, 18):
                            biased(c, s - 17)
                        if s in (25, 26):
                            soft(c + 1, 1 - par, s - 25)
                if not last:
                    for s in range(3):
                        slot(c + 1, 1 - par, s)
                out(c, par)
                add(c, last)

            dve.sem_inc(s_drive, 2)
            dve.sem_inc(s_h, 4)
            dve.sem_inc(s_yout, 1)
            dve.wait_ge(once, 1)
            dve.tensor_scalar(a_neg[:, :, :], a_exp[:, :, :], -1.0, None, ALU.mult).then_inc(once, 1)
            norm_stats(0)
            norm_apply(0)
            split_bc(None)
            for m in range(KD):
                biased(None, m)
            for m in range(KD):
                soft(0, 0, m)
            drives(0, 0, 0)
            for s in range(3):
                slot(0, 0, s)
            with dve.Fori(0, CHUNKS // 2 - 1) as pair:
                c = pair * 2
                chunk(c, 0)
                chunk(c + 1, 1)
            chunk(CHUNKS - 2, 0)
            chunk(CHUNKS - 1, 1, last=True)

        @block.gpsimd
        def _(pool):
            def norm_pow(c):
                pool.wait_ge(s_var, c + 1)
                pool.tensor_tensor(rstd[:, :], var_eps[:, :], const["minus_half"][:, 0:CT], ALU.pow).then_inc(s_rstd, 1)

            def chunk(c, par, last=False):
                for s in range(SLOTS):
                    n = c * SLOTS + s
                    pool.wait_ge(s_h, n + 5)
                    if par == 0:
                        end = h[:, s % 4, CH - 1:CH]
                        pool.tensor_tensor(state[:, s:s + 1], end, const["one"][:, 0:1], ALU.mult).then_inc(s_state, 1)
                    if s % 2 == 0:
                        pool.wait_ge(s_ck, c * STATES + s // 2 + 2)
                    pool.wait_ge(s_y, n + 1)
                    pool.tensor_tensor(hc[:, s % 4, :], h[:, s % 4, :], c_bc[:, (s // 2) % 2, :], ALU.mult).then_inc(s_hc, 1)
                    if s == 4 and not last:
                        norm_pow(c + 1)

            pool.sem_inc(s_hc, 4)
            norm_pow(0)
            with pool.Fori(0, CHUNKS // 2 - 1) as pair:
                c = pair * 2
                chunk(c, 0)
                chunk(c + 1, 1)
            chunk(CHUNKS - 2, 0)
            chunk(CHUNKS - 1, 1, last=True)

        @block.scalar
        def _(act):
            def keep(beside, k, out):
                act.wait_ge(s_fill, filled(beside, k))
                src = bank(beside, k)
                if k == LOW:
                    src = src[0:RANK, :]
                elif k == BCT:
                    src = src[0:3 * N2, 0:CH // 2].bitcast(BF16)
                else:
                    src = src[:, :]
                act.activation(out, src, ACT.Copy).then_inc(s_act, 1)

            def logs(c, m):
                act.wait_ge(s_abs, 2 * c + m + 1)
                act.activation(z_exp[:, m, :], z_abs[:, m, :], ACT.Exp, scale=-1.0).then_inc(s_zexp, 1)
                act.wait_ge(s_zexp, 2 * c + m + 1)
                act.activation(z_log[:, m, :], z_exp[:, m, :], ACT.Ln, bias=const["one"][:, 0:1]).then_inc(s_log, 1)

            def slot(c, par, s):
                n, m = c * SLOTS + s, s % 2
                if m == 0:
                    i = c * STATES + s // 2
                    act.wait_ge(s_c, i + 1)
                    act.wait_ge(s_hc, 2 * i + 2)
                    act.activation(c_bc[:, (s // 2) % 2, :], c_ps[:, :], ACT.Copy).then_inc(s_ck, 1)
                act.wait_ge(s_h, n + 1)
                if s < 2:
                    act.wait_ge(s_delta, 2 * c + s + 1)
                act.activation(decay[:, s % 4, :], delta[:, par, m, :], ACT.Exp,
                               scale=a_neg[:, m, s // 2:s // 2 + 1]).then_inc(s_decay, 1)

            def chunk(c, par, last=False):
                for s in range(SLOTS):
                    slot(c, par, s)
                    if not last:
                        if s == 11:
                            keep(c, TA, xnT[:, 1 - par, 0, :])
                            keep(c, TB, xnT[:, 1 - par, 1, :])
                        if s == 14:
                            keep(c, LOW, low[:, :])
                        if s in (21, 22):
                            logs(c + 1, s - 21)
                        if s == 23:
                            keep(c, BCT, bcT[:, 1 - par, :])

            act.activation(a_exp[:, :, :], w["A_log"][:, :, :], ACT.Exp).then_inc(once, 1)
            act.sem_inc(s_ck, 1)
            keep(None, TA, xnT[:, 0, 0, :])
            keep(None, TB, xnT[:, 0, 1, :])
            keep(None, LOW, low[:, :])
            for m in range(KD):
                logs(0, m)
            keep(None, BCT, bcT[:, 0, :])
            act.wait_ge(once, 2)
            with act.Fori(0, CHUNKS // 2 - 1) as pair:
                c = pair * 2
                chunk(c, 0)
                chunk(c + 1, 1)
            chunk(CHUNKS - 2, 0)
            chunk(CHUNKS - 1, 1, last=True)

        @block.tensor
        def _(pe):
            def turn_halves(beside):
                pe.wait_ge(s_xn, chunk_of(beside) + 1)
                if beside is not None:
                    pe.wait_ge(s_act, 4 * (beside + 1))
                    pe.wait_ge(s_dve, 3 + 5 * beside)
                for k in range(KD):
                    for t in range(CT):
                        last = pe.transpose(bank(beside, TA + k)[:, t * P:(t + 1) * P], xn[:, t, k * P:(k + 1) * P], const["ident"][:, :])
                    last.then_inc(s_fill, 1)

            def project(beside, par):
                pe.wait_ge(s_act, used_act(beside, TB))
                for k in range(KD):
                    last = pe.matmul(bank(beside, LOW)[0:RANK, :], w["low"][:, k, :], xnT[:, par, k, :], start=(k == 0), stop=(k == KD - 1))
                last.then_inc(s_fill, 1)
                for t in range(CT):
                    for k in range(KD):
                        last = pe.matmul(bank(beside, BC)[:, t * N2:(t + 1) * N2], xnT[:, par, k, t * P:(t + 1) * P], w["bc"][:, k, :],
                                         start=(k == 0), stop=(k == KD - 1))
                last.then_inc(s_fill, 1)

            def steps(beside):
                pe.wait_ge(s_act, used_act(beside, LOW))
                for m in range(KD):
                    pe.matmul(bank(beside, DT0 + m)[:, :], w["dt_w"][:, m * P:(m + 1) * P], low[:, :], start=True, stop=True).then_inc(s_fill, 1)

            def turn_bc(beside):
                pe.wait_ge(s_bcp, chunk_of(beside) + 1)
                dst = bank(beside, BCT)[0:3 * N2, 0:CH // 2].bitcast(BF16)
                for t in range(CT):
                    last = pe.transpose(dst[:, t * P:(t + 1) * P], bc_parts[:, t, :], const["ident_bf"][:, :])
                last.then_inc(s_fill, 1)

            def spread(c, par, n):
                i = c * STATES + n
                if n == 0:
                    pe.wait_ge(s_act, 4 * (c + 1))
                pe.wait_ge(s_drive, 2 * i)
                pe.matmul(b_ps[:, n % 2, :], const["pick_bc"][:, n, :], bcT[:, par, :], start=True, stop=True).then_inc(s_b, 1)
                pe.wait_ge(s_ck, i + 1)
                pe.matmul(c_ps[:, :], const["pick_bc"][:, STATES + n, :], bcT[:, par, :], start=True, stop=True).then_inc(s_c, 1)

            def collect(c, par, s):
                n, m = c * SLOTS + s, s % 2
                if s == 0:
                    pe.wait_ge(s_yout, c + 1)
                pe.wait_ge(s_hc, n + 5)
                pe.matmul(y_ps[:, m, :], const["ident"][:, :], hc[:, s % 4, :], start=(s < 2), stop=(s >= SLOTS - 2)).then_inc(s_y, 1)

            def turn_out(c, last):
                pe.wait_ge(s_yout, c + 2)
                for r in range(2):
                    pe.wait_ge(s_dve, 3 + 5 * c + (3 if not last else 0))
                    b = bank(c, OUT0 + r if not last else r)
                    for a in range(2):
                        for m in range(KD):
                            t = 2 * r + a
                            mm = pe.transpose(b[:, a * D + m * P:a * D + (m + 1) * P], y_out[:, m, t * P:(t + 1) * P], const["ident"][:, :])
                    mm.then_inc(s_fill, 1)

            def chunk(c, par, last=False):
                for s in range(SLOTS):
                    if s % 2 == 0:
                        n = s // 2 + 2
                        if n < STATES:
                            spread(c, par, n)
                        elif not last:
                            spread(c + 1, 1 - par, n - STATES)
                    collect(c, par, s)
                    if not last:
                        if s == 7:
                            turn_halves(c)
                        if s == 9:
                            project(c, 1 - par)
                        if s == 13:
                            steps(c)
                        if s == 16:
                            turn_bc(c)
                turn_out(c, last)

            pe.sem_inc(s_y, 4)
            turn_halves(None)
            project(None, 0)
            steps(None)
            turn_bc(None)
            spread(0, 0, 0)
            spread(0, 0, 1)
            with pe.Fori(0, CHUNKS // 2 - 1) as pair:
                c = pair * 2
                chunk(c, 0)
                chunk(c + 1, 1)
            chunk(CHUNKS - 2, 0)
            chunk(CHUNKS - 1, 1, last=True)


def build(nc, ins, out, stages):
    with ExitStack() as ctx:
        def keep(names):
            return {n: ctx.enter_context(nc.sbuf_tensor("w_" + n, list(ins[n].shape), ins[n].dtype)) for n in names}

        def load(sp, kept, here):
            for n, t in kept.items():
                sp.dma_start(t[tuple(slice(None) for _ in t.shape)], ins[n]).then_inc(here, 16)

        def weights(kept, prefix):
            return {n[len(prefix):]: t for n, t in kept.items() if n.startswith(prefix)}

        x = ctx.enter_context(nc.sbuf_tensor("x", [P, TILES, D], F32))
        x_tiles = ins["x"].rearrange("b (t p) d -> p (b t) d", p=P)
        first = ["ident", "ident_bf", "minus_half", "iota", "pick_gate", "f0_router"]
        by_unit = ["f0_gate", "f0_up", "f0_down"]
        late = [n for n in ins if n.startswith(("f1_", "sc_")) or n in ("pick_gate1", "pick_bc", "cost")]
        early = keep([n for n in ins if n != "x" and n not in late])
        qk_stacks = nc.dram_tensor("qk_stacks", (2, HEADS, QK_ROWS, TOKENS), BF16, kind="Internal").ap()
        v_rows = nc.dram_tensor("v_rows", (TOKENS, HEADS * 2 * DH), F32, kind="Internal").ap()
        s_first = ctx.enter_context(nc.semaphore("first_inputs_here"))
        s_x = ctx.enter_context(nc.semaphore("rest_of_x_here"))
        s_w = ctx.enter_context(nc.semaphore("rest_of_units_here"))
        s_early = ctx.enter_context(nc.semaphore("early_inputs_here"))
        s_late = ctx.enter_context(nc.semaphore("late_inputs_here"))
        s_out = ctx.enter_context(nc.semaphore("outputs_there"))

        def load_x(sp, c, here):
            sp.dma_start(x[:, c * CT:(c + 1) * CT, :], x_tiles[:, c * CT:(c + 1) * CT, :]).then_inc(here, 16)

        with nc.Block() as block:
            @block.sync
            def _(sp):
                load_x(sp, 0, s_first)
                load(sp, {n: early[n] for n in first}, s_first)
                for n in by_unit:
                    sp.dma_start(early[n][:, 0:FIRST_UNITS], ins[n][:, 0:FIRST_UNITS]).then_inc(s_first, 16)
                for c in range(1, FIRST_CHUNKS):
                    load_x(sp, c, s_first)
                sp.wait_ge(s_first, 16 * (FIRST_CHUNKS + len(first) + len(by_unit)))

        def load_early(sp):
            rest = {n: t for n, t in early.items() if n not in first + by_unit}
            for n in by_unit:
                sp.dma_start(early[n][:, FIRST_UNITS:UNITS0], ins[n][:, FIRST_UNITS:UNITS0]).then_inc(s_w, 16)
            for c in range(FIRST_CHUNKS, CHUNKS):
                load_x(sp, c, s_x)
            load(sp, rest, s_early)
            sp.wait_ge(s_w, 16 * len(by_unit))
            sp.wait_ge(s_x, 16 * (CHUNKS - FIRST_CHUNKS))
            sp.wait_ge(s_early, 16 * len(rest))

        const = dict(early)
        for n, s in enumerate(stages):
            if n == 0:
                ffn_moe(nc, f"a{n}", x, weights(early, "f0_"), const, load_early,
                        x_rest=(s_x, 16 * (CHUNKS - FIRST_CHUNKS)), w_rest=(s_w, 16 * len(by_unit)))
            elif s == "ffn_moe":
                second = keep(late)
                const.update(second)

                def load_late(sp):
                    load(sp, second, s_late)
                    sp.wait_ge(s_late, 16 * len(second))

                ffn_moe(nc, f"a{n}", x, weights(early, "f0_"), const, load_late)
            if s == "attention":
                attention_inputs(nc, f"a{n}i", x, weights(early, "at_"), const, qk_stacks, v_rows)
                attention(nc, f"a{n}", x, weights(early, "at_"), const, qk_stacks, v_rows)
            if s == "scan_mixer":
                scan_mixer(nc, f"a{n}", x, weights(const, "sc_"), const)
            if s == "ffn_gelu":
                ffn_gelu(nc, f"a{n}", x, weights(const, "f1_"), const)
        with nc.Block() as block:
            @block.sync
            def _(sp):
                o_tiles = out.rearrange("b (t p) d -> p (b t) d", p=P)
                for c in range(CHUNKS):
                    sp.dma_start(o_tiles[:, c * CT:(c + 1) * CT, :], x[:, c * CT:(c + 1) * CT, :]).then_inc(s_out, 16)
                sp.wait_ge(s_out, 16 * CHUNKS)


STAGES = ["ffn_moe", "attention", "ffn_moe", "ffn_gelu", "scan_mixer", "ffn_gelu"]


def lay_out(inputs):
    a = {k: np.asarray(v) for k, v in inputs.items()}
    bf = mybir.dt.np(BF16)
    rows = lambda m: np.ascontiguousarray(m.reshape(m.shape[0] // P, P, *m.shape[1:]).swapaxes(0, 1))
    g = {"x": a["L0_attn_x"]}
    g["f0_router"] = rows(np.concatenate([a["L0_ffn_gate_w"], a["L0_ffn_se_gate_w"]], 0).T)
    for mine, routed, shared in (("f0_gate", "L0_ffn_w_gate", "L0_ffn_sh_gate"), ("f0_up", "L0_ffn_w_up", "L0_ffn_sh_up")):
        units = np.concatenate([a[routed], a[shared].reshape(2, P, D)], 0)
        g[mine] = np.ascontiguousarray(units.reshape(UNITS0, P, KD, P).transpose(3, 0, 2, 1))
    down = np.concatenate([a["L0_ffn_w_down"].transpose(0, 2, 1), a["L0_ffn_sh_down"].T.reshape(2, P, D)], 0)
    g["f0_down"] = np.ascontiguousarray(down.transpose(1, 0, 2))
    for n in "qkv":
        g["at_w" + n] = rows(a["L0_attn_W" + n])
    wo = np.zeros((HG, GH, 2 * DH, D), np.float32)
    wo[:, :, 0:DH] = a["L0_attn_Wo"].reshape(HG, GH, DH, D)
    g["at_wo"] = np.ascontiguousarray(wo.reshape(HG, P, D).transpose(1, 0, 2))
    cols = lambda v: np.ascontiguousarray(v.reshape(KD, P, *v.shape[1:]).swapaxes(0, 1))
    g["sc_A_log"], g["sc_dt_b"], g["sc_D"] = cols(a["L1_attn_A_log"]), cols(a["L1_attn_dt_proj_b"]), cols(a["L1_attn_D"])
    g["sc_low"] = rows(a["L1_attn_x_proj_w"][0:RANK].T)
    g["sc_bc"] = rows(a["L1_attn_x_proj_w"][RANK:].T)
    g["sc_dt_w"] = np.ascontiguousarray(a["L1_attn_dt_proj_w"].T)
    one = lambda v: np.ascontiguousarray(np.broadcast_to(v[None], (P, v.shape[0])))
    g["f1_router"] = rows(a["L1_ffn_router_w"])
    g["f1_router_b"] = one(a["L1_ffn_router_b"])
    g["f1_down_w"] = rows(a["L1_ffn_down_w"])
    g["f1_down_b"] = a["L1_ffn_down_b"].reshape(P, 1)
    w1 = [a[f"L1_ffn_e{e}_w1"] for e in range(E1)] + [a["L1_ffn_shared_w1"]]
    g["f1_w1"] = np.ascontiguousarray(np.concatenate(w1, 1).reshape(P, HT1 + 1, P))
    b1 = [a[f"L1_ffn_e{e}_b1"] for e in range(E1)] + [a["L1_ffn_shared_b1"]]
    g["f1_b1"] = np.ascontiguousarray(np.concatenate(b1).reshape(HT1 + 1, P).T)
    w2 = [a[f"L1_ffn_e{e}_w2"] for e in range(E1)] + [a["L1_ffn_shared_w2"]]
    g["f1_w2"] = rows(np.concatenate(w2, 0))
    b2 = [a[f"L1_ffn_e{e}_b2"] for e in range(E1)] + [a["L1_ffn_shared_b2"]]
    g["f1_b2"] = np.ascontiguousarray(np.stack(b2, 1))
    g["f1_up_w"], g["f1_core_w"] = a["L1_ffn_up_w"], rows(a["L1_ffn_core_w"])
    g["f1_up_b"], g["f1_core_b"] = one(a["L1_ffn_up_b"]), one(a["L1_ffn_core_b"])
    g["ident"] = np.eye(P, dtype=np.float32)
    g["ident_bf"] = np.eye(P, dtype=bf)
    g["iota"] = np.tile(np.arange(E0, dtype=np.float32), (P, 1))
    g["minus_half"] = np.full((P, 8), -0.5, np.float32)
    g["pick_gate"] = np.ascontiguousarray(
        np.broadcast_to(np.tile(np.eye(G0), (3, 1))[:, :, None], (3 * G0, G0, P)).astype(bf))
    query, key = np.arange(P)[:, None], np.arange(P)[None]
    g["hide_right"] = np.where(key > query, np.float32(HIDDEN), np.float32(0)).astype(bf)
    g["hide_below"] = np.ascontiguousarray(g["hide_right"].T)
    g["onward"] = np.ascontiguousarray((key >= query).astype(np.float32).T)
    floor = np.zeros((P, GH, BT), np.float32)
    floor[P - 1, :, BT - 1] = -3e38
    g["floor"] = floor.reshape(P, GH * BT)
    pick = np.zeros((P, GH), np.float32)
    pick[np.arange(GH) * 2 * DH + DH, np.arange(GH)] = 1
    g["pick_den"] = pick
    g["one"] = np.ones((P, 1), np.float32)
    g["pick_bc"] = np.ascontiguousarray(
        np.broadcast_to(np.tile(np.eye(2 * STATES), (3, 1))[:, :, None], (6 * STATES, 2 * STATES, P)).astype(bf))
    g["pick_gate1"] = np.ascontiguousarray(
        np.broadcast_to(np.tile(np.eye(E1), (3, 1))[:, :, None], (3 * E1, E1, P)).astype(bf))
    g["cost"] = np.tile(np.float32(1e-7) * np.array([2 * P * h for h in HID1], np.float32), (P, 1))
    return g


def kernel(**inputs):
    import concourse.bacc as _bacc
    from concourse.bass_utils import run_bass_kernel_spmd as _run

    nc = _bacc.Bacc("TRN2", target_bir_lowering=False, num_devices=1)
    arrays, ins = {}, {}
    for name, v in lay_out(inputs).items():
        arrays[f"in_{name}"] = v
        ins[name] = nc.dram_tensor(f"in_{name}", v.shape, mybir.dt.from_np(v.dtype), kind="ExternalInput").ap()
    out = nc.dram_tensor("out_0", (B, T, D), F32, kind="ExternalOutput").ap()
    build(nc, ins, out, STAGES)
    return _run(nc, [arrays], core_ids=[0]).results[0]["out_0"]
```

```python
from contextlib import ExitStack

import numpy as np

import concourse.bass as bass
from concourse import mybir

ALU = mybir.AluOpType
ACT = mybir.ActivationFunctionType
AX = mybir.AxisListType
F32 = mybir.dt.float32
BF16 = mybir.dt.bfloat16
U32 = mybir.dt.uint32
R32 = mybir.dt.float32r

P = 128
B, T, D = 4, 1024, 256
KD = D // P
TOKENS = B * T
TILES = TOKENS // P
CH = 512
CT = CH // P
CHUNKS = TOKENS // CH
EPS = 1e-5
FIRST_CHUNKS, FIRST_UNITS = 2, 3
E0 = 8
UNITS0 = E0 + 2
G0 = E0 + 1
E1 = 8
HID1 = [128, 256, 384, 512, 128, 256, 384, 512]
TILE_EXPERT = [e for e in range(E1) for _ in range(HID1[e] // P)]
HT1 = len(TILE_EXPERT)
HEADS, DH = 16, 16
GH = 4
HG = HEADS // GH
BT = T // P
STATES = 16
RANK = 64
Q_PART = [0, 1, 2, 0, 1, 0]
K_PART = [1, 0, 0, 0, 1, 2]
PARTS = 3


def runs(order):
    starts = [n for n in range(len(order)) if n == 0 or order[n] != order[n - 1] + 1]
    return [(n, order[n], m - n) for n, m in zip(starts, starts[1:] + [len(order)])]


RUNS = (runs(Q_PART), runs(K_PART))
QK_ROWS = len(Q_PART) * DH
M_ROWS = 3
HIDDEN = -1e30


def three_parts(dve, sem, base, whole, part1, rest, part2, rest2, part3):
    dve.tensor_copy(part1, whole).then_inc(sem, 1)
    dve.wait_ge(sem, base + 1)
    dve.tensor_tensor(rest, whole, part1, ALU.subtract).then_inc(sem, 1)
    dve.wait_ge(sem, base + 2)
    dve.tensor_copy(part2, rest).then_inc(sem, 1)
    dve.wait_ge(sem, base + 3)
    dve.tensor_tensor(rest2, rest, part2, ALU.subtract).then_inc(sem, 1)
    dve.wait_ge(sem, base + 4)
    return dve.tensor_copy(part3, rest2)


def ffn_moe(nc, tag, x, w, const, beside, x_rest=None, raw=None):
    with ExitStack() as ctx:
        ctx.enter_context(nc.cleanup_on_exit())

        def sb(name, shape, dt=F32):
            return ctx.enter_context(nc.sbuf_tensor(f"{tag}_{name}", shape, dt))

        def psum(name, shape, dt=F32):
            return ctx.enter_context(nc.psum_tensor(f"{tag}_{name}", shape, dt))

        def sem(name):
            return nc.alloc_semaphore(f"{tag}_{name}")

        RING = 4
        WEIGHTS = ("gate", "up", "down")
        xn = sb("xn", [P, CT, D])
        xnT = sb("xnT", [P, KD, CH])
        xnT_hi = sb("xnT_hi", [P, 2, KD, CH], R32)
        xnT_lo = sb("xnT_lo", [P, 2, KD, CH], R32)
        stats = sb("stats", [P, CT, 6])
        mean_var = sb("mean_var", [P, CT, 2])
        var_eps = sb("var_eps", [P, CT])
        rstd = sb("rstd", [P, CT])
        scores = sb("scores", [P, CT, G0])
        top = sb("top", [P, CT, 8])
        top_at = sb("top_at", [P, CT, 8], U32)
        at = sb("at", [P, CT, 2])
        diff = sb("diff", [P, CT, 2])
        tanh = sb("tanh", [P, CT, 2])
        weight = sb("weight", [P, CT, 2])
        hit = sb("hit", [P, 2, CT, E0])
        gates = sb("gates", [P, CT, G0])
        rest = sb("rest", [P, CT, G0])
        rest2 = sb("rest2", [P, CT, G0])
        gparts = sb("gparts", [P, CT, 3 * G0], BF16)
        gT = sb("gT", [3 * G0, 2, CH], BF16)
        silu = sb("silu", [P, 2, CH])
        prod = sb("prod", [P, 2, CH])
        hid = sb("hid", [P, 2, CH])
        hid_hi = sb("hid_hi", [P, RING, CH], R32)
        hid_lo = sb("hid_lo", [P, RING, CH], R32)

        x1 = psum("x1", [P, 2, CH])
        x3 = psum("x3", [P, 2, CH])
        gate_bc = psum("gate_bc", [P, CH])
        acc = psum("acc", [P, CT, D])
        misc = psum("misc", [P, CH])
        misc_bf = misc[0:3 * G0, 0:CH // 2].bitcast(BF16)

        chain = sem("dve_steps")
        s_var = sem("var_ready")
        s_rstd = sem("rstd_ready")
        s_xn = sem("xn_ready")
        s_T = sem("half_transposed")
        s_Tc = sem("half_kept")
        s_R = sem("scores_ready")
        s_Rc = sem("scores_kept")
        s_diff = sem("diff_ready")
        s_tanh = sem("tanh_ready")
        s_gp = sem("gate_parts_ready")
        s_GT = sem("gates_transposed")
        s_gT = sem("gates_kept")
        s_x1 = sem("x1_ready")
        s_x3 = sem("x3_and_gate_ready")
        s_silu = sem("silu_done")
        s_prod = sem("product_done")
        s_hid = sem("hidden_ready")
        s_hi = sem("hidden_high_ready")
        s_lo = sem("hidden_low_ready")
        s_down = sem("down_done")
        s_Th = sem("half_high_ready")
        s_Tl = sem("half_low_ready")
        s_wh = sem("weights_high_ready")
        s_wl = sem("weights_low_ready")
        s_acc = sem("chunk_added")

        NORM, CHOOSE, WEIGH = 3, 7, 7
        STEPS = NORM + CHOOSE + WEIGH

        def tile_of(c, t):
            return bass.ds(c * CT + t, 1) if not isinstance(c, int) else slice(c * CT + t, c * CT + t + 1)

        block = ctx.enter_context(nc.Block())

        @block.vector
        def _(dve):
            def norm_stats(c):
                for t in range(CT):
                    last = dve.bn_stats(stats[:, t, :], x[:, tile_of(c, t), :].rearrange("p a d -> p (a d)"))
                last.then_inc(chain, 1)
                dve.wait_ge(chain, c * STEPS + 1)
                dve.sem_inc(chain, 1)
                for t in range(CT):
                    last = dve.bn_aggr(mean_var[:, t, :], stats[:, t, :])
                last.then_inc(chain, 1)
                dve.wait_ge(chain, c * STEPS + 3)
                dve.tensor_scalar(var_eps[:, :], mean_var[:, :, 1], EPS, None, ALU.add).then_inc(s_var, 1)

            def norm_apply(c):
                dve.wait_ge(s_rstd, c + 1)
                dve.wait_ge(s_T, c * KD)
                for t in range(CT):
                    last = dve.tensor_scalar(xn[:, t, :], x[:, tile_of(c, t), :].rearrange("p a d -> p (a d)"),
                                             mean_var[:, t, 0:1], rstd[:, t:t + 1], ALU.subtract, ALU.mult)
                last.then_inc(s_xn, 1)

            def choose(c):
                base = c * STEPS + NORM
                dve.wait_ge(s_R, c + 1)
                dve.tensor_copy(scores[:, :, :], misc[:, 0:CT * G0].rearrange("p (t g) -> p t g", t=CT)).then_inc(s_Rc, 1)
                dve.wait_ge(s_Rc, c + 1)
                dve.sem_inc(chain, 1)
                for t in range(CT):
                    last = dve.max(top[:, t, :], scores[:, t, 0:E0])
                last.then_inc(chain, 1)
                dve.wait_ge(chain, base + 2)
                dve.sem_inc(chain, 1)
                for t in range(CT):
                    last = dve.max_index(top_at[:, t, :], top[:, t, :], scores[:, t, 0:E0])
                last.then_inc(chain, 1)
                dve.tensor_tensor(diff[:, :, 0:1], top[:, :, 0:1], top[:, :, 1:2], ALU.subtract)
                dve.tensor_copy(diff[:, :, 1:2], scores[:, :, E0:E0 + 1]).then_inc(s_diff, 1)
                dve.wait_ge(chain, base + 4)
                dve.tensor_copy(at[:, :, :], top_at[:, :, 0:2]).then_inc(chain, 1)
                dve.wait_ge(chain, base + 5)
                for k in range(2):
                    dve.tensor_tensor(hit[:, k, :, :], const["iota"][:, :].rearrange("p (a e) -> p a e", a=1).broadcast_to([P, CT, E0]),
                                      at[:, :, k:k + 1].broadcast_to([P, CT, E0]), ALU.is_equal).then_inc(chain, 1)

            def weigh(c):
                base = c * STEPS + NORM + CHOOSE
                dve.wait_ge(s_tanh, c + 1)
                dve.tensor_scalar(weight[:, :, 0:1], tanh[:, :, 0:1], 0.25, 0.25, ALU.mult, ALU.add)
                dve.tensor_scalar(weight[:, :, 1:2], tanh[:, :, 0:1], -0.25, 0.25, ALU.mult, ALU.add)
                dve.tensor_scalar(gates[:, :, E0:G0], tanh[:, :, 1:2], 0.25, 0.25, ALU.mult, ALU.add).then_inc(chain, 1)
                dve.wait_ge(chain, base + 1)
                for k in range(2):
                    last = dve.tensor_tensor(hit[:, k, :, :], hit[:, k, :, :],
                                             weight[:, :, k:k + 1].broadcast_to([P, CT, E0]), ALU.mult)
                last.then_inc(chain, 1)
                dve.wait_ge(chain, base + 2)
                dve.tensor_tensor(gates[:, :, 0:E0], hit[:, 0, :, :], hit[:, 1, :, :], ALU.add).then_inc(chain, 1)
                dve.wait_ge(chain, base + 3)
                dve.wait_ge(s_GT, c)
                three_parts(dve, chain, base + 3, gates[:, :, :], gparts[:, :, 0:G0], rest[:, :, :],
                            gparts[:, :, G0:2 * G0], rest2[:, :, :], gparts[:, :, 2 * G0:3 * G0]).then_inc(s_gp, 1)

            def hidden(c, u):
                n = c * UNITS0 + u
                b = u % 2
                dve.wait_ge(s_silu, n + 3)
                dve.wait_ge(s_x3, n + 1)
                dve.tensor_tensor(prod[:, b, :], silu[:, b, :], x3[:, b, :], ALU.mult).then_inc(s_prod, 1)
                dve.wait_ge(s_prod, n + 3)
                dve.wait_ge(s_lo, n + 1)
                dve.tensor_tensor(hid[:, b, :], prod[:, b, :], gate_bc[:, :], ALU.mult).then_inc(s_hid, 1)

            def low(c, par, u):
                n = c * UNITS0 + u
                r = (par * UNITS0 + u) % RING
                dve.wait_ge(s_hi, n + 1)
                dve.tensor_tensor(hid_lo[:, r, :], hid[:, u % 2, :], hid_hi[:, r, :].bitcast(F32), ALU.subtract).then_inc(s_lo, 1)

            def weights_low(units, n):
                for k, part in enumerate(WEIGHTS):
                    high, low = (h[:, units] for h in w[part])
                    dve.wait_ge(s_wh, 3 * n + k + 1)
                    dve.tensor_tensor(low, raw[0][part][:, units], high.bitcast(F32), ALU.subtract).then_inc(s_wl, 1)

            def add(c):
                dve.wait_ge(s_down, c * UNITS0 + UNITS0 + RING)
                for t in range(0, CT, 2):
                    where = x[:, bass.ds(c * CT + t, 2) if not isinstance(c, int) else slice(c * CT + t, c * CT + t + 2), :]
                    last = dve.tensor_tensor(where, acc[:, t:t + 2, :], where, ALU.add)
                last.then_inc(s_acc, 1)

            def chunk(c, par, last=False):
                for u in range(2, UNITS0):
                    hidden(c, u)
                    low(c, par, u - 1)
                    if not last:
                        if u == 2:
                            if x_rest and not (isinstance(c, int) and c + 1 < FIRST_CHUNKS):
                                dve.wait_ge(*x_rest)
                            norm_stats(c + 1)
                        if u == 3:
                            norm_apply(c + 1)
                        if u == 7:
                            choose(c + 1)
                        if u == 8:
                            weigh(c + 1)
                if not last:
                    hidden(c + 1, 0)
                low(c, par, UNITS0 - 1)
                if not last:
                    hidden(c + 1, 1)
                    low(c + 1, 1 - par, 0)
                add(c)

            dve.sem_inc(s_prod, 2)
            dve.sem_inc(s_hid, 1)
            dve.sem_inc(s_acc, 1)
            dve.sem_inc(s_lo, 2)
            norm_stats(0)
            norm_apply(0)
            if raw:
                weights_low(slice(0, FIRST_UNITS), 0)
            choose(0)
            weigh(0)
            hidden(0, 0)
            if raw:
                weights_low(slice(FIRST_UNITS, UNITS0), 1)
            hidden(0, 1)
            low(0, 0, 0)
            chunk(0, 0)
            with dve.Fori(0, CHUNKS // 2 - 1) as pair:
                c = pair * 2 + 1
                chunk(c, 1)
                chunk(c + 1, 0)
            chunk(CHUNKS - 1, 1, last=True)

        @block.sync
        def _(sp):
            beside(sp)

        @block.gpsimd
        def _(pool):
            def chunk(c, par):
                pool.wait_ge(s_var, c + 1)
                pool.tensor_tensor(rstd[:, :], var_eps[:, :], const["minus_half"][:, 0:CT], ALU.pow).then_inc(s_rstd, 1)
                for k in range(KD):
                    pool.wait_ge(s_Th, c * KD + k + 1)
                    pool.tensor_tensor(xnT_lo[:, par, k, :], xnT[:, k, :], xnT_hi[:, par, k, :].bitcast(F32), ALU.subtract).then_inc(s_Tl, 1)

            with pool.Fori(0, CHUNKS // 2) as pair:
                c = pair * 2
                chunk(c, 0)
                chunk(c + 1, 1)

        @block.scalar
        def _(act):
            def keep_half(c, par, k):
                act.wait_ge(s_T, c * KD + k + 1)
                if not (isinstance(c, int) and c == 0):
                    act.wait_ge(s_Tl, c * KD)
                    act.wait_ge(s_R, c)
                act.activation(xnT_hi[:, par, k, :], misc[:, :], ACT.Copy)
                act.activation(xnT[:, k, :], misc[:, :], ACT.Copy).then_inc(s_Tc, 1)
                act.wait_ge(s_Tc, c * KD + k + 1)
                act.sem_inc(s_Th, 1)

            def tanhs(c):
                act.wait_ge(s_diff, c + 1)
                act.activation(tanh[:, :, :], diff[:, :, :], ACT.Tanh, scale=0.5).then_inc(s_tanh, 1)

            def keep_gates(c, par):
                act.wait_ge(s_GT, c + 1)
                act.activation(gT[:, par, :], misc_bf, ACT.Copy).then_inc(s_gT, 1)

            def unit(c, u):
                n = c * UNITS0 + u
                act.wait_ge(s_x1, n + 1)
                act.wait_ge(s_prod, n + 1)
                act.activation(silu[:, u % 2, :], x1[:, u % 2, :], ACT.Silu).then_inc(s_silu, 1)

            def high(c, par, u):
                n = c * UNITS0 + u
                act.wait_ge(s_hid, n + 2)
                act.wait_ge(s_down, n + 1)
                act.activation(hid_hi[:, (par * UNITS0 + u) % RING, :], hid[:, u % 2, :], ACT.Copy).then_inc(s_hi, 1)

            def weights_high(units, n):
                act.wait_ge(*raw[1 + n])
                for part in WEIGHTS:
                    act.activation(w[part][0][:, units], raw[0][part][:, units], ACT.Copy).then_inc(s_wh, 1)

            def chunk(c, par, last=False):
                for u in range(2, UNITS0):
                    unit(c, u)
                    high(c, par, u - 1)
                    if not last:
                        if u == 5:
                            keep_half(c + 1, 1 - par, 0)
                        if u == 6:
                            keep_half(c + 1, 1 - par, 1)
                        if u == 8:
                            tanhs(c + 1)
                        if u == 9:
                            keep_gates(c + 1, 1 - par)
                if not last:
                    unit(c + 1, 0)
                high(c, par, UNITS0 - 1)
                if not last:
                    unit(c + 1, 1)
                    high(c + 1, 1 - par, 0)

            act.sem_inc(s_silu, 2)
            if raw:
                weights_high(slice(0, FIRST_UNITS), 0)
            for k in range(KD):
                keep_half(0, 0, k)
            tanhs(0)
            keep_gates(0, 0)
            unit(0, 0)
            if raw:
                weights_high(slice(FIRST_UNITS, UNITS0), 1)
            unit(0, 1)
            high(0, 0, 0)
            with act.Fori(0, CHUNKS - 2, 2) as c:
                chunk(c, 0)
                chunk(c + 1, 1)
            chunk(CHUNKS - 2, 0)
            chunk(CHUNKS - 1, 1, last=True)

        @block.tensor
        def _(pe):
            def turn_half(c, k):
                if k == 0:
                    pe.wait_ge(s_xn, c + 1)
                    pe.wait_ge(s_gT, c)
                else:
                    pe.wait_ge(s_Tc, c * KD + k)
                for t in range(CT):
                    last = pe.transpose(misc[:, t * P:(t + 1) * P], xn[:, t, k * P:(k + 1) * P], const["ident"][:, :])
                last.then_inc(s_T, 1)

            def route(c, par):
                pe.wait_ge(s_Tc, c * KD + KD)
                for t in range(CT):
                    for k in range(KD):
                        last = pe.matmul(misc[:, t * G0:(t + 1) * G0], xnT[:, k, t * P:(t + 1) * P],
                                         w["router"][:, k, :], start=(k == 0), stop=(k == KD - 1))
                last.then_inc(s_R, 1)

            def turn_gates(c):
                pe.wait_ge(s_gp, c + 1)
                for t in range(CT):
                    last = pe.transpose(misc_bf[:, t * P:(t + 1) * P], gparts[:, t, :], const["ident_bf"][:, :])
                last.then_inc(s_GT, 1)

            HALVES = ((1, 0), (0, 1), (0, 0))

            def up(c, par, u):
                n = c * UNITS0 + u
                b = u % 2
                xs = (xnT_hi, xnT_lo)
                if u == 0:
                    pe.wait_ge(s_Tl, c * KD + KD)
                if raw and u in (0, FIRST_UNITS):
                    pe.wait_ge(s_wl, 3 if u == 0 else 6)
                pe.wait_ge(s_silu, n + 1)
                for k in range(KD):
                    for i, j in HALVES:
                        last = pe.matmul(x1[:, b, :], w["gate"][i][:, u, k, :], xs[j][:, par, k, :],
                                         start=(k == 0 and i == 1), stop=(k == KD - 1 and i == j))
                last.then_inc(s_x1, 1)
                pe.wait_ge(s_prod, n + 1)
                for k in range(KD):
                    for i, j in HALVES:
                        pe.matmul(x3[:, b, :], w["up"][i][:, u, k, :], xs[j][:, par, k, :],
                                  start=(k == 0 and i == 1), stop=(k == KD - 1 and i == j))
                pe.wait_ge(s_hid, n + 1)
                if u == 0:
                    pe.wait_ge(s_gT, c + 1)
                pe.matmul(gate_bc[:, :], const["pick_gate"][:, min(u, E0), :], gT[:, par, :],
                          start=True, stop=True).then_inc(s_x3, 1)

            def down(c, par, u):
                n = c * UNITS0 + u
                hs = (hid_hi, hid_lo)
                r = (par * UNITS0 + u) % RING
                pe.wait_ge(s_lo, n + 3)
                if u == 0:
                    pe.wait_ge(s_acc, c + 1)
                for t in range(CT):
                    for i, j in HALVES:
                        last = pe.matmul(acc[:, t, :], hs[j][:, r, t * P:(t + 1) * P], w["down"][i][:, u, :],
                                         start=(u == 0 and t % 2 == 0 and i == 1), stop=(u == UNITS0 - 1 and i == j),
                                         skip_group_check=True)
                last.then_inc(s_down, 1)

            def chunk(c, par, last=False):
                for u in range(2, UNITS0):
                    up(c, par, u)
                    down(c, par, u - 2)
                    if not last:
                        if u == 4:
                            turn_half(c + 1, 0)
                        if u == 5:
                            turn_half(c + 1, 1)
                        if u == 6:
                            route(c + 1, 1 - par)
                        if u == 9:
                            turn_gates(c + 1)
                if not last:
                    up(c + 1, 1 - par, 0)
                down(c, par, UNITS0 - 2)
                if not last:
                    up(c + 1, 1 - par, 1)
                down(c, par, UNITS0 - 1)

            pe.sem_inc(s_down, RING)
            turn_half(0, 0)
            turn_half(0, 1)
            route(0, 0)
            turn_gates(0)
            up(0, 0, 0)
            up(0, 0, 1)
            with pe.Fori(0, CHUNKS - 2, 2) as c:
                chunk(c, 0)
                chunk(c + 1, 1)
            chunk(CHUNKS - 2, 0)
            chunk(CHUNKS - 1, 1, last=True)


def ffn_gelu(nc, tag, x, w, const):
    with ExitStack() as ctx:
        ctx.enter_context(nc.cleanup_on_exit())

        def sb(name, shape, dt=F32):
            return ctx.enter_context(nc.sbuf_tensor(f"{tag}_{name}", shape, dt))

        def psum(name, shape, dt=F32):
            return ctx.enter_context(nc.psum_tensor(f"{tag}_{name}", shape, dt))

        def sem(name):
            return nc.alloc_semaphore(f"{tag}_{name}")

        UNITS = HT1 + 1
        SH = HT1
        RING = 6
        xn = sb("xn", [P, CT, D])
        xnT = sb("xnT", [P, KD, CH])
        core = sb("core", [P, 2, KD, CH])
        gelu_h = sb("gelu_h", [P, CH])
        gelu_h_hi = sb("gelu_h_hi", [P, 2, CH], R32)
        gelu_h_lo = sb("gelu_h_lo", [P, 2, CH], R32)
        stats = sb("stats", [P, CT, 6])
        mean_var = sb("mean_var", [P, CT, 2])
        var_eps = sb("var_eps", [P, CT])
        rstd = sb("rstd", [P, CT])
        biased = sb("biased", [P, CT, E1])
        logits = sb("logits", [P, CT, E1])
        shifted = sb("shifted", [P, CT, E1])
        expd = sb("expd", [P, CT, E1])
        total = sb("total", [P, CT])
        inverse = sb("inverse", [P, CT])
        probs = sb("probs", [P, CT, E1])
        top = sb("top", [P, CT, 8])
        top_p = sb("top_p", [P, CT, 8])
        top_at = sb("top_at", [P, CT, 8], U32)
        at = sb("at", [P, CT, 2])
        diff = sb("diff", [P, CT, 1])
        tanh = sb("tanh", [P, CT, 1])
        weight = sb("weight", [P, CT, 2])
        hit = sb("hit", [P, 2, CT, E1])
        gates = sb("gates", [P, CT, E1])
        rest = sb("rest", [P, CT, E1])
        rest2 = sb("rest2", [P, CT, E1])
        gparts = sb("gparts", [P, CT, 3 * E1], BF16)
        gT = sb("gT", [3 * E1, CH], BF16)
        gate_bc = sb("gate_bc", [P, E1, CH])
        act_out = sb("act_out", [P, 3, CH])
        hid = sb("hid", [P, 3, CH])
        hid_hi = sb("hid_hi", [P, RING, CH], R32)
        hid_lo = sb("hid_lo", [P, RING, CH], R32)
        mixed = sb("mixed", [P, CH])
        gelu_b1 = sb("gelu_b1", [P, HT1])
        gelu_b1_hi = sb("gelu_b1_hi", [P, HT1, 2], R32)
        gelu_b1_lo = sb("gelu_b1_lo", [P, HT1, 2], R32)
        gelu_b1_twice = gelu_b1[:, :].rearrange("p (u a) -> p u a", a=1).broadcast_to([P, HT1, 2])
        b2_sum = sb("b2_sum", [P, 1])
        shared_b2 = sb("shared_b2", [P, 1])
        b2_all = sb("b2_all", [P, 1])
        every = sb("every", [P, 1])
        end_sum = sb("end_sum", [P, D])
        end_bias = sb("end_bias", [P, CT, D])

        u_ps = psum("u", [P, 3, CH])
        acc = psum("acc", [P, 2, CH])
        end = psum("end", [P, CT, D])
        misc = psum("misc", [P, CH])
        misc_bf = misc[0:3 * E1, 0:CH // 2].bitcast(BF16)

        once = sem("dve_once")
        s_gb1 = sem("gelu_b1_ready")
        s_every = sem("every_summed")
        s_everyd = sem("every_ready")
        chain_n = sem("norm_steps")
        chain = sem("dve_steps")
        s_centred = sem("x_centred")
        s_bias = sem("end_bias_ready")
        s_xb = sem("bias_in_x")
        s_var = sem("var_ready")
        s_rstd = sem("rstd_ready")
        s_xn = sem("xn_ready")
        s_T = sem("half_transposed")
        s_Tc = sem("half_kept")
        s_R = sem("scores_ready")
        s_Rc = sem("scores_kept")
        s_core = sem("core_ready")
        s_h = sem("h_ready")
        s_gh = sem("gelu_h_ready")
        s_ghh = sem("gelu_h_high_ready")
        s_ghl = sem("gelu_h_low_ready")
        s_shift = sem("shifted_ready")
        s_exp = sem("exp_ready")
        s_diff = sem("diff_ready")
        s_tanh = sem("tanh_ready")
        s_gp = sem("gate_parts_ready")
        s_GT = sem("gates_transposed")
        s_gT = sem("gates_kept")
        s_G = sem("gate_spread")
        s_Gc = sem("gate_spread_kept")
        s_u = sem("u_ready")
        s_gelu = sem("gelu_done")
        s_hid = sem("hidden_ready")
        s_hi = sem("hidden_high_ready")
        s_lo = sem("hidden_low_ready")
        s_down = sem("down_done")
        s_mixed = sem("mixed_ready")
        s_end = sem("end_ready")
        s_add = sem("chunk_added")

        NORM, CHOOSE, PICK, WEIGH = 3, 4, 9, 7
        STEPS = CHOOSE + PICK + WEIGH
        def tiles(c, t, n=1):
            return slice(c * CT + t, c * CT + t + n) if isinstance(c, int) else bass.ds(c * CT + t, n)

        def per_expert(a):
            return a.broadcast_to([P, CT, E1])

        block = ctx.enter_context(nc.Block())

        @block.vector
        def _(dve):
            def constants_of_biases():
                dve.tensor_reduce(b2_sum[:, :], w["b2"][:, 0:E1], AX.X, ALU.add).then_inc(once, 1)
                dve.tensor_scalar(shared_b2[:, :], w["b2"][:, E1:E1 + 1], 0.1, None, ALU.mult).then_inc(once, 1)
                dve.tensor_tensor(end_sum[:, :], w["up_b"][:, :], w["core_b"][:, :], ALU.add).then_inc(once, 1)
                dve.wait_ge(once, 3)
                dve.tensor_tensor(b2_all[:, :], b2_sum[:, :], shared_b2[:, :], ALU.add).then_inc(once, 1)
                for t in range(CT):
                    dve.tensor_scalar(end_bias[:, t, :], end_sum[:, :], 0.5, None, ALU.mult).then_inc(once, 1)
                dve.wait_ge(once, 4 + CT)
                dve.sem_inc(s_bias, 1)
                dve.wait_ge(s_gb1, 2)
                dve.tensor_tensor(gelu_b1_lo[:, :, :], gelu_b1_twice, gelu_b1_hi[:, :, :].bitcast(F32), ALU.subtract).then_inc(s_gb1, 1)

            def constants():
                dve.wait_ge(s_every, 1)
                dve.tensor_tensor(every[:, :], end[:, 0, 0:1], b2_all[:, :], ALU.add).then_inc(s_everyd, 1)

            def norm_stats(c, t):
                last = dve.bn_stats(stats[:, t, :], x[:, tiles(c, t), :].rearrange("p a d -> p (a d)"))
                if t == CT - 1:
                    last.then_inc(chain_n, 1)

            def norm_gather(c):
                dve.wait_ge(chain_n, c * NORM + 1)
                if not (isinstance(c, int) and c == 0):
                    dve.wait_ge(s_xn, c)
                dve.sem_inc(chain_n, 1)
                for t in range(CT):
                    last = dve.bn_aggr(mean_var[:, t, :], stats[:, t, :])
                last.then_inc(chain_n, 1)
                dve.wait_ge(chain_n, c * NORM + 3)
                dve.tensor_scalar(var_eps[:, :], mean_var[:, :, 1], EPS, None, ALU.add).then_inc(s_var, 1)

            def choose(c):
                base = c * STEPS
                dve.wait_ge(s_R, c + 1)
                dve.tensor_tensor(biased[:, :, :], misc[:, 0:CT * E1].rearrange("p (t g) -> p t g", t=CT),
                                  per_expert(w["router_b"][:, :].rearrange("p (a e) -> p a e", a=1)), ALU.add).then_inc(s_Rc, 1)
                dve.wait_ge(s_Rc, c + 1)
                dve.tensor_tensor(logits[:, :, :], biased[:, :, :],
                                  per_expert(const["cost"][:, :].rearrange("p (a e) -> p a e", a=1)), ALU.subtract).then_inc(chain, 1)
                dve.wait_ge(chain, base + 1)
                dve.sem_inc(chain, 1)
                for t in range(CT):
                    last = dve.max(top[:, t, :], logits[:, t, :])
                last.then_inc(chain, 1)
                dve.wait_ge(chain, base + 3)
                dve.tensor_tensor(shifted[:, :, :], logits[:, :, :], per_expert(top[:, :, 0:1]), ALU.subtract).then_inc(s_shift, 1)
                dve.sem_inc(chain, 1)

            def pick(c):
                base = c * STEPS + CHOOSE
                dve.wait_ge(s_exp, c + 1)
                dve.tensor_reduce(total[:, :], expd[:, :, :], AX.X, ALU.add).then_inc(chain, 1)
                dve.wait_ge(chain, base + 1)
                dve.reciprocal(inverse[:, :], total[:, :]).then_inc(chain, 1)
                dve.wait_ge(chain, base + 2)
                dve.tensor_tensor(probs[:, :, :], expd[:, :, :],
                                  per_expert(inverse[:, :].rearrange("p (t a) -> p t a", a=1)), ALU.mult).then_inc(chain, 1)
                dve.wait_ge(chain, base + 3)
                dve.sem_inc(chain, 1)
                for t in range(CT):
                    last = dve.max(top_p[:, t, :], probs[:, t, :])
                last.then_inc(chain, 1)
                dve.wait_ge(chain, base + 5)
                dve.tensor_tensor(diff[:, :, :], top_p[:, :, 0:1], top_p[:, :, 1:2], ALU.subtract).then_inc(s_diff, 1)
                for t in range(CT):
                    last = dve.max_index(top_at[:, t, :], top_p[:, t, :], probs[:, t, :])
                last.then_inc(chain, 1)
                dve.wait_ge(chain, base + 6)
                dve.tensor_copy(at[:, :, :], top_at[:, :, 0:2]).then_inc(chain, 1)
                dve.wait_ge(chain, base + 7)
                for k in range(2):
                    dve.tensor_tensor(hit[:, k, :, :], per_expert(const["iota"][:, :].rearrange("p (a e) -> p a e", a=1)),
                                      per_expert(at[:, :, k:k + 1]), ALU.is_equal).then_inc(chain, 1)

            def weigh(c):
                base = c * STEPS + CHOOSE + PICK
                dve.wait_ge(s_tanh, c + 1)
                dve.tensor_scalar(weight[:, :, 0:1], tanh[:, :, :], 0.5, 0.5, ALU.mult, ALU.add)
                dve.tensor_scalar(weight[:, :, 1:2], tanh[:, :, :], -0.5, 0.5, ALU.mult, ALU.add).then_inc(chain, 1)
                dve.wait_ge(chain, base + 1)
                for k in range(2):
                    last = dve.tensor_tensor(hit[:, k, :, :], hit[:, k, :, :], per_expert(weight[:, :, k:k + 1]), ALU.mult)
                last.then_inc(chain, 1)
                dve.wait_ge(chain, base + 2)
                dve.tensor_tensor(gates[:, :, :], hit[:, 0, :, :], hit[:, 1, :, :], ALU.add).then_inc(chain, 1)
                dve.wait_ge(chain, base + 3)
                dve.wait_ge(s_GT, c)
                three_parts(dve, chain, base + 3, gates[:, :, :], gparts[:, :, 0:E1], rest[:, :, :],
                            gparts[:, :, E1:2 * E1], rest2[:, :, :], gparts[:, :, 2 * E1:3 * E1]).then_inc(s_gp, 1)

            def hidden(c, par, u):
                n = c * UNITS + u
                b = u % 3
                dve.wait_ge(s_gelu, n + 4)
                dve.wait_ge(s_lo, n + 1)
                if u == SH:
                    dve.tensor_scalar(hid[:, b, :], act_out[:, b, :], 0.1, None, ALU.mult).then_inc(s_hid, 1)
                    return
                e = TILE_EXPERT[u]
                if u == TILE_EXPERT.index(e):
                    dve.wait_ge(s_Gc, c * E1 + e + 1)
                dve.scalar_tensor_tensor(out=hid[:, b, :], in0=act_out[:, b, :], scalar=gelu_b1[:, u:u + 1],
                                         in1=gate_bc[:, e, :], op0=ALU.subtract, op1=ALU.mult).then_inc(s_hid, 1)

            def low(c, par, u):
                n = c * UNITS + u
                r = (par * UNITS + u) % RING
                dve.wait_ge(s_hi, n + 1)
                dve.tensor_tensor(hid_lo[:, r, :], hid[:, u % 3, :], hid_hi[:, r, :].bitcast(F32), ALU.subtract).then_inc(s_lo, 1)

            def low_h(c, par):
                dve.wait_ge(s_ghh, c + 1)
                dve.tensor_tensor(gelu_h_lo[:, par, :], gelu_h[:, :], gelu_h_hi[:, par, :].bitcast(F32), ALU.subtract).then_inc(s_ghl, 1)

            def mix(c, par):
                dve.wait_ge(s_down, c * UNITS + UNITS + RING)
                dve.wait_ge(s_end, c + 1)
                dve.tensor_scalar(mixed[:, :], acc[:, par, :], every[:, 0:1], None, ALU.add).then_inc(s_mixed, 1)

            def add(c):
                dve.wait_ge(s_end, c + 2)
                dve.wait_ge(s_xb, c + 1)
                for t in range(0, CT, 2):
                    here = x[:, tiles(c, t, 2), :]
                    last = dve.scalar_tensor_tensor(out=here, in0=end[:, t:t + 2, :], scalar=0.5, in1=here,
                                                    op0=ALU.mult, op1=ALU.add)
                last.then_inc(s_add, 1)

            def chunk(c, par, norm_ahead=True, last=False):
                for u in range(3, UNITS):
                    hidden(c, par, u)
                    low(c, par, u - 1)
                    if not last:
                        if u == 6:
                            choose(c + 1)
                        if u == 8:
                            pick(c + 1)
                        if u == 9:
                            low_h(c + 1, 1 - par)
                        if u == 10:
                            weigh(c + 1)
                    if norm_ahead:
                        if u in range(13, 13 + CT):
                            norm_stats(c + 2, u - 13)
                        if u == 13 + CT:
                            norm_gather(c + 2)
                if not last:
                    hidden(c + 1, 1 - par, 0)
                low(c, par, SH)
                if not last:
                    hidden(c + 1, 1 - par, 1)
                    low(c + 1, 1 - par, 0)
                mix(c, par)
                if not last:
                    hidden(c + 1, 1 - par, 2)
                    low(c + 1, 1 - par, 1)
                add(c)

            dve.sem_inc(s_hid, 3)
            dve.sem_inc(s_lo, 3)
            dve.sem_inc(s_mixed, 2)
            dve.sem_inc(s_add, 1)
            constants_of_biases()
            for c in range(2):
                for t in range(CT):
                    norm_stats(c, t)
                norm_gather(c)
            choose(0)
            pick(0)
            low_h(0, 0)
            weigh(0)
            constants()
            dve.wait_ge(s_everyd, 1)
            for u in range(3):
                hidden(0, 0, u)
                if u:
                    low(0, 0, u - 1)
            with dve.Fori(0, CHUNKS // 2 - 1) as pair:
                c = pair * 2
                chunk(c, 0)
                chunk(c + 1, 1)
            chunk(CHUNKS - 2, 0, norm_ahead=False)
            chunk(CHUNKS - 1, 1, norm_ahead=False, last=True)

        @block.gpsimd
        def _(pool):
            def chunk(c):
                here = x[:, tiles(c, 0, CT), :]
                wide = lambda a: a.broadcast_to([P, CT, D])
                pool.wait_ge(s_var, c + 1)
                pool.tensor_tensor(rstd[:, :], var_eps[:, :], const["minus_half"][:, 0:CT], ALU.pow).then_inc(s_rstd, 1)
                if not (isinstance(c, int) and c == 0):
                    pool.wait_ge(s_T, c * KD)
                pool.tensor_tensor(xn[:, :, :], here, wide(mean_var[:, :, 0:1]), ALU.subtract).then_inc(s_centred, 1)
                pool.wait_ge(s_rstd, c + 1)
                pool.wait_ge(s_centred, c + 1)
                pool.tensor_tensor(xn[:, :, :], xn[:, :, :], wide(rstd[:, :].rearrange("p (t a) -> p t a", a=1)), ALU.mult).then_inc(s_xn, 1)
                pool.tensor_tensor(here, here, end_bias[:, :, :], ALU.add).then_inc(s_xb, 1)

            pool.wait_ge(s_bias, 1)
            chunk(0)
            with pool.Fori(1, CHUNKS) as c:
                chunk(c)

        @block.scalar
        def _(act):
            def keep_half(c, k):
                act.wait_ge(s_T, c * KD + k + 1)
                act.wait_ge(s_h, c)
                act.activation(xnT[:, k, :], misc[:, :], ACT.Copy).then_inc(s_Tc, 1)

            def core_in(c, par):
                act.wait_ge(s_Tc, c * KD + KD)
                if not (isinstance(c, int) and c == 0):
                    act.wait_ge(s_end, c)
                for k in range(KD):
                    last = act.activation(core[:, par, k, :], xnT[:, k, :], ACT.Gelu)
                last.then_inc(s_core, 1)

            def h_in(c, par):
                act.wait_ge(s_h, c + 1)
                if not (isinstance(c, int) and c == 0):
                    act.wait_ge(s_ghl, c)
                act.activation(gelu_h[:, :], misc[:, :], ACT.Gelu, bias=w["down_b"][:, 0:1]).then_inc(s_gh, 1)
                act.wait_ge(s_gh, c + 1)
                act.activation(gelu_h_hi[:, par, :], gelu_h[:, :], ACT.Copy).then_inc(s_ghh, 1)

            def exps(c):
                act.wait_ge(s_shift, c + 1)
                act.activation(expd[:, :, :], shifted[:, :, :], ACT.Exp).then_inc(s_exp, 1)

            def tanhs(c):
                act.wait_ge(s_diff, c + 1)
                act.activation(tanh[:, :, :], diff[:, :, :], ACT.Tanh, scale=0.5).then_inc(s_tanh, 1)

            def keep_gates(c):
                act.wait_ge(s_GT, c + 1)
                act.activation(gT[:, :], misc_bf, ACT.Copy).then_inc(s_gT, 1)

            def keep_spread(c, e):
                act.wait_ge(s_G, c * E1 + e + 1)
                if not (isinstance(c, int) and c == 0):
                    act.wait_ge(s_hid, (c - 1) * UNITS + HT1 - TILE_EXPERT[::-1].index(e) + 3)
                act.activation(gate_bc[:, e, :], misc[:, :], ACT.Copy).then_inc(s_Gc, 1)

            def high(c, par, u):
                n = c * UNITS + u
                act.wait_ge(s_hid, n + 4)
                act.wait_ge(s_down, n + 1)
                act.activation(hid_hi[:, (par * UNITS + u) % RING, :], hid[:, u % 3, :], ACT.Copy).then_inc(s_hi, 1)

            def unit(c, u):
                n = c * UNITS + u
                act.wait_ge(s_u, n + 1)
                act.wait_ge(s_hid, n + 1)
                act.activation(act_out[:, u % 3, :], u_ps[:, u % 3, :], ACT.Gelu, bias=w["b1"][:, u:u + 1]).then_inc(s_gelu, 1)

            def chunk(c, par, last=False):
                for u in range(3, UNITS):
                    unit(c, u)
                    high(c, par, u - 1)
                    if not last:
                        if u == 3:
                            keep_half(c + 1, 0)
                        if u == 4:
                            keep_half(c + 1, 1)
                        if u == 5:
                            core_in(c + 1, 1 - par)
                        if u == 7:
                            h_in(c + 1, 1 - par)
                        if u == 8:
                            exps(c + 1)
                        if u == 10:
                            tanhs(c + 1)
                        if u == 13:
                            keep_gates(c + 1)
                        if u >= 13:
                            keep_spread(c + 1, u - 13)
                if not last:
                    unit(c + 1, 0)
                high(c, par, SH)
                if not last:
                    for u in range(1, 3):
                        unit(c + 1, u)
                        high(c + 1, 1 - par, u - 1)

            act.activation(gelu_b1[:, :], w["b1"][:, 0:HT1], ACT.Gelu).then_inc(s_gb1, 1)
            act.wait_ge(s_gb1, 1)
            act.activation(gelu_b1_hi[:, :, :], gelu_b1_twice, ACT.Copy).then_inc(s_gb1, 1)
            act.sem_inc(s_gelu, 3)
            for k in range(KD):
                keep_half(0, k)
            core_in(0, 0)
            h_in(0, 0)
            exps(0)
            tanhs(0)
            keep_gates(0)
            for e in range(E1):
                keep_spread(0, e)
                if e < 3:
                    unit(0, e)
            for u in range(2):
                high(0, 0, u)
            with act.Fori(0, CHUNKS - 2, 2) as c:
                chunk(c, 0)
                chunk(c + 1, 1)
            chunk(CHUNKS - 2, 0)
            chunk(CHUNKS - 1, 1, last=True)

        @block.tensor
        def _(pe):
            def constants():
                pe.wait_ge(s_gb1, 3)
                for u in range(HT1):
                    for weight, b, first, stop in (("w2_lo", gelu_b1_hi, True, False), ("w2_hi", gelu_b1_lo, False, False),
                                                   ("w2_hi", gelu_b1_hi, False, True)):
                        last = pe.matmul(end[:, 0, 0:2], w[weight][:, u, :], b[:, u, :],
                                         start=(u == 0 and first), stop=(u == HT1 - 1 and stop))
                last.then_inc(s_every, 1)

            def turn_half(c, k):
                if k == 0:
                    pe.wait_ge(s_xn, c + 1)
                    pe.wait_ge(s_Gc, c * E1)
                else:
                    pe.wait_ge(s_Tc, c * KD + k)
                for t in range(CT):
                    last = pe.transpose(misc[:, t * P:(t + 1) * P], xn[:, t, k * P:(k + 1) * P], const["ident"][:, :])
                last.then_inc(s_T, 1)

            def route(c):
                pe.wait_ge(s_Tc, c * KD + KD)
                for t in range(CT):
                    for k in range(KD):
                        last = pe.matmul(misc[:, t * E1:(t + 1) * E1], xnT[:, k, t * P:(t + 1) * P],
                                         w["router"][:, k, :], start=(k == 0), stop=(k == KD - 1))
                last.then_inc(s_R, 1)

            def h_out(c):
                pe.wait_ge(s_Rc, c + 1)
                pe.wait_ge(s_core, c + 1)
                for k in range(KD):
                    last = pe.matmul(misc[:, :], w["down_w"][:, k, :], xnT[:, k, :], start=(k == 0), stop=(k == KD - 1))
                last.then_inc(s_h, 1)

            def turn_gates(c):
                pe.wait_ge(s_gh, c + 1)
                pe.wait_ge(s_gp, c + 1)
                for t in range(CT):
                    last = pe.transpose(misc_bf[:, t * P:(t + 1) * P], gparts[:, t, :], const["ident_bf"][:, :])
                last.then_inc(s_GT, 1)

            def spread(c, e):
                if e == 0:
                    pe.wait_ge(s_gT, c + 1)
                else:
                    pe.wait_ge(s_Gc, c * E1 + e)
                pe.matmul(misc[:, :], const["pick_gate1"][:, e, :], gT[:, :], start=True, stop=True).then_inc(s_G, 1)

            def up(c, par, u):
                n = c * UNITS + u
                if u == 0:
                    pe.wait_ge(s_ghl, c + 1)
                pe.wait_ge(s_gelu, n + 1)
                for weight, h, start, stop in (("w1_lo", gelu_h_hi, True, False), ("w1_hi", gelu_h_lo, False, False),
                                               ("w1_hi", gelu_h_hi, False, True)):
                    last = pe.matmul(u_ps[:, u % 3, :], w[weight][:, u, :], h[:, par, :], start=start, stop=stop)
                last.then_inc(s_u, 1)

            def down(c, par, u):
                n = c * UNITS + u
                if u == 0:
                    pe.wait_ge(s_mixed, c + 1)
                pe.wait_ge(s_lo, n + 4)
                for weight, h, first, end in (("w2_lo", hid_hi, True, False), ("w2_hi", hid_lo, False, False),
                                              ("w2_hi", hid_hi, False, True)):
                    last = pe.matmul(acc[:, par, :], w[weight][:, u, :], h[:, (par * UNITS + u) % RING, :],
                                     start=(u == 0 and first), stop=(u == UNITS - 1 and end))
                last.then_inc(s_down, 1)

            def finish(c, par):
                pe.wait_ge(s_mixed, c + 3)
                pe.wait_ge(s_add, c + 1)
                for t in range(CT):
                    for k in range(KD):
                        pe.matmul(end[:, t, :], core[:, par, k, t * P:(t + 1) * P], w["core_w"][:, k, :],
                                  start=(k == 0 and t % 2 == 0), stop=False, skip_group_check=True)
                    last = pe.matmul(end[:, t, :], mixed[:, t * P:(t + 1) * P], w["up_w"][:, :],
                                     start=False, stop=True, skip_group_check=True)
                last.then_inc(s_end, 1)

            def chunk(c, par, last=False):
                for u in range(3, UNITS):
                    up(c, par, u)
                    down(c, par, u - 3)
                    if not last:
                        if u == 3:
                            turn_half(c + 1, 0)
                        if u == 4:
                            turn_half(c + 1, 1)
                        if u == 5:
                            route(c + 1)
                        if u == 7:
                            h_out(c + 1)
                        if u == 13:
                            turn_gates(c + 1)
                        if u >= 13:
                            spread(c + 1, u - 13)
                if not last:
                    up(c + 1, 1 - par, 0)
                down(c, par, UNITS - 3)
                if not last:
                    up(c + 1, 1 - par, 1)
                down(c, par, UNITS - 2)
                down(c, par, UNITS - 1)
                if not last:
                    up(c + 1, 1 - par, 2)
                finish(c, par)

            pe.sem_inc(s_down, RING)
            pe.sem_inc(s_end, 1)
            turn_half(0, 0)
            turn_half(0, 1)
            route(0)
            h_out(0)
            constants()
            turn_gates(0)
            for e in range(E1):
                spread(0, e)
                if e < 3:
                    up(0, 0, e)
            with pe.Fori(0, CHUNKS - 2, 2) as c:
                chunk(c, 0)
                chunk(c + 1, 1)
            chunk(CHUNKS - 2, 0)
            chunk(CHUNKS - 1, 1, last=True)


def split_weights(nc, raw_and_halves):
    with ExitStack() as ctx:
        ctx.enter_context(nc.cleanup_on_exit())
        s_high = nc.alloc_semaphore("weights_high_ready")
        s_low = nc.alloc_semaphore("weights_low_ready")
        block = ctx.enter_context(nc.Block())

        @block.scalar
        def _(act):
            for raw, high, low in raw_and_halves:
                act.activation(high[:, :, :], raw[:, :, :], ACT.Copy).then_inc(s_high, 1)

        @block.vector
        def _(dve):
            for n, (raw, high, low) in enumerate(raw_and_halves):
                dve.wait_ge(s_high, n + 1)
                dve.tensor_tensor(low[:, :, :], raw[:, :, :], high[:, :, :].bitcast(F32), ALU.subtract).then_inc(s_low, 1)
            dve.wait_ge(s_low, len(raw_and_halves))


def attention_inputs(nc, tag, x, w, const, qk_parts, v_rows):
    with ExitStack() as ctx:
        ctx.enter_context(nc.cleanup_on_exit())

        def sb(name, shape, dt=F32):
            return ctx.enter_context(nc.sbuf_tensor(f"{tag}_{name}", shape, dt))

        def psum(name, shape, dt=F32):
            return ctx.enter_context(nc.psum_tensor(f"{tag}_{name}", shape, dt))

        def sem(name):
            return nc.alloc_semaphore(f"{tag}_{name}")

        TQ = 4
        weight = {n: sb(n, list(w[n].shape)) for n in w}
        xn = sb("xn", [P, CT, D])
        xnT = sb("xnT", [P, 2, KD, CH])
        stats = sb("stats", [P, CT, 6])
        mean_var = sb("mean_var", [P, CT, 2])
        var_eps = sb("var_eps", [P, CT])
        rstd = sb("rstd", [P, CT])
        rest = sb("rest", [P, 2, 2, CH])
        parts = sb("parts", [P, TQ, 3, CH], BF16)
        v_pad = sb("v_pad", [P, 2, CT, HEADS, 2 * DH])

        half = psum("half", [P, 2, CH])
        qk = psum("qk", [P, 4, CH])
        v_ps = psum("v", [P, 2, 2, D])

        s_w = sem("weights_here")
        s_stat = sem("stats_ready")
        s_mv = sem("mean_var_ready")
        s_var = sem("var_ready")
        s_rstd = sem("rstd_ready")
        s_xn = sem("xn_ready")
        s_T = sem("half_transposed")
        s_Tc = sem("half_kept")
        s_qk = sem("qk_ready")
        s_v = sem("v_ready")
        s_p1 = sem("part1_ready")
        chain = sem("dve_steps")
        s_parts = sem("parts_ready")
        s_pad = sem("v_kept")
        s_pads = sem("v_pad_set")
        s_st = [sem(f"parts_stored_{m}") for m in range(TQ)]
        s_vst = [sem("v_stored_even"), sem("v_stored_odd")]

        def tiles(c, t, n=1):
            return slice(c * CT + t, c * CT + t + n) if isinstance(c, int) else bass.ds(c * CT + t, n)

        block = ctx.enter_context(nc.Block())

        @block.vector
        def _(dve):
            def norm(c):
                for t in range(CT):
                    last = dve.bn_stats(stats[:, t, :], x[:, tiles(c, t), :].rearrange("p a d -> p (a d)"))
                last.then_inc(s_stat, 1)
                dve.wait_ge(s_stat, c + 1)
                dve.sem_inc(s_mv, 1)
                for t in range(CT):
                    last = dve.bn_aggr(mean_var[:, t, :], stats[:, t, :])
                last.then_inc(s_mv, 1)
                dve.wait_ge(s_mv, 2 * c + 2)
                dve.tensor_scalar(var_eps[:, :], mean_var[:, :, 1], EPS, None, ALU.add).then_inc(s_var, 1)
                dve.wait_ge(s_rstd, c + 1)
                if not (isinstance(c, int) and c == 0):
                    dve.wait_ge(s_T, c * KD)
                for t in range(CT):
                    last = dve.tensor_scalar(xn[:, t, :], x[:, tiles(c, t), :].rearrange("p a d -> p (a d)"),
                                             mean_var[:, t, 0:1], rstd[:, t:t + 1], ALU.subtract, ALU.mult)
                last.then_inc(s_xn, 1)

            def split(c, m):
                base = c * TQ * 3 + 3 * m
                dve.wait_ge(s_p1, c * TQ + m + 1)
                dve.tensor_tensor(rest[:, m % 2, 0, :], qk[:, m, :], parts[:, m, 0, :], ALU.subtract).then_inc(chain, 1)
                dve.wait_ge(chain, base + 1)
                dve.tensor_copy(parts[:, m, 1, :], rest[:, m % 2, 0, :]).then_inc(chain, 1)
                dve.wait_ge(chain, base + 2)
                dve.tensor_tensor(rest[:, m % 2, 1, :], rest[:, m % 2, 0, :], parts[:, m, 1, :], ALU.subtract).then_inc(chain, 1)
                dve.wait_ge(chain, base + 3)
                dve.tensor_copy(parts[:, m, 2, :], rest[:, m % 2, 1, :]).then_inc(s_parts, 1)

            def chunk(c, par, last=False):
                split(c, 0)
                if not last:
                    norm(c + 1)
                for m in range(1, TQ):
                    split(c, m)

            norm(0)
            chunk(0, 0)
            with dve.Fori(0, CHUNKS // 2 - 1) as pair:
                c = pair * 2 + 1
                chunk(c, 1)
                chunk(c + 1, 0)
            chunk(CHUNKS - 1, 1, last=True)

        @block.gpsimd
        def _(pool):
            pool.memset(v_pad[:, :, :, :, :], 0.0).then_inc(s_pads, 1)
            pool.wait_ge(s_pads, 1)
            for par in range(2):
                pool.memset(v_pad[:, par, :, :, DH:DH + 1], 1.0).then_inc(s_pads, 1)
            with pool.Fori(0, CHUNKS) as c:
                pool.wait_ge(s_var, c + 1)
                pool.tensor_tensor(rstd[:, :], var_eps[:, :], const["minus_half"][:, 0:CT], ALU.pow).then_inc(s_rstd, 1)

        @block.scalar
        def _(act):
            def keep_half(c, par, k):
                act.wait_ge(s_T, c * KD + k + 1)
                if not (isinstance(c, int) and c <= 1):
                    act.wait_ge(s_v, 2 * (c - 1))
                act.activation(xnT[:, par, k, :], half[:, k, :], ACT.Copy).then_inc(s_Tc, 1)

            def part1(c, m):
                act.wait_ge(s_qk, c * TQ + m + 1)
                if not (isinstance(c, int) and c == 0):
                    act.wait_ge(s_st[m], 16 * PARTS * c)
                act.activation(parts[:, m, 0, :], qk[:, m, :], ACT.Copy).then_inc(s_p1, 1)

            def keep_v(c, par, r):
                act.wait_ge(s_v, 2 * c + r + 1)
                if not (isinstance(c, int) and c <= 1):
                    act.wait_ge(s_vst[par], 16 * (c // 2))
                act.activation(v_pad[:, par, 2 * r:2 * r + 2, :, 0:DH],
                               v_ps[:, r, :, :].rearrange("p a (h d) -> p a h d", d=DH), ACT.Copy).then_inc(s_pad, 1)

            def chunk(c, par, last=False):
                for m in range(TQ):
                    part1(c, m)
                keep_v(c, par, 0)
                if not last:
                    for k in range(KD):
                        keep_half(c + 1, 1 - par, k)
                keep_v(c, par, 1)

            act.wait_ge(s_pads, 3)
            for k in range(KD):
                keep_half(0, 0, k)
            chunk(0, 0)
            with act.Fori(0, CHUNKS // 2 - 1) as pair:
                c = pair * 2 + 1
                chunk(c, 1)
                chunk(c + 1, 0)
            chunk(CHUNKS - 1, 1, last=True)

        @block.tensor
        def _(pe):
            def turn_halves(c):
                pe.wait_ge(s_xn, c + 1)
                if not (isinstance(c, int) and c == 0):
                    pe.wait_ge(s_Tc, c * KD)
                for k in range(KD):
                    for t in range(CT):
                        last = pe.transpose(half[:, k, t * P:(t + 1) * P], xn[:, t, k * P:(k + 1) * P], const["ident"][:, :])
                    last.then_inc(s_T, 1)

            def project(c, par, m):
                wide = weight["wq" if m < 2 else "wk"]
                if not (isinstance(c, int) and c == 0):
                    pe.wait_ge(s_parts, (c - 1) * TQ + m + 1)
                for k in range(KD):
                    last = pe.matmul(qk[:, m, :], wide[:, k, (m % 2) * P:(m % 2 + 1) * P], xnT[:, par, k, :],
                                     start=(k == 0), stop=(k == KD - 1))
                last.then_inc(s_qk, 1)

            def project_v(c, par, r):
                if not (isinstance(c, int) and c == 0):
                    pe.wait_ge(s_pad, 2 * (c - 1) + r + 1)
                for a in range(2):
                    t = 2 * r + a
                    for k in range(KD):
                        last = pe.matmul(v_ps[:, r, a, :], xnT[:, par, k, t * P:(t + 1) * P], weight["wv"][:, k, :],
                                         start=(k == 0), stop=(k == KD - 1))
                last.then_inc(s_v, 1)

            def chunk(c, par, last=False):
                pe.wait_ge(s_Tc, c * KD + KD)
                for m in range(TQ):
                    project(c, par, m)
                project_v(c, par, 0)
                if not last:
                    turn_halves(c + 1)
                project_v(c, par, 1)

            turn_halves(0)
            pe.wait_ge(s_w, 16 * len(w))
            chunk(0, 0)
            with pe.Fori(0, CHUNKS // 2 - 1) as pair:
                c = pair * 2 + 1
                chunk(c, 1)
                chunk(c + 1, 0)
            chunk(CHUNKS - 1, 1, last=True)

        @block.sync
        def _(sp):
            rows = v_rows.rearrange("(n p) f -> p n f", p=P)
            for n in w:
                sp.dma_start(weight[n][:, :, :], w[n]).then_inc(s_w, 16)

            def chunk(c, par):
                here = slice(c * CH, (c + 1) * CH) if isinstance(c, int) else bass.ds(c * CH, CH)
                for m in range(TQ):
                    heads = slice((m % 2) * P // DH, (m % 2 + 1) * P // DH)
                    sp.wait_ge(s_parts, c * TQ + m + 1)
                    for part in range(PARTS):
                        sp.dma_start(qk_parts[m // 2, heads, part * DH:(part + 1) * DH, here], parts[:, m, part, :]).then_inc(s_st[m], 16)
                sp.wait_ge(s_pad, 2 * c + 2)
                sp.dma_start(rows[:, tiles(c, 0, CT), :],
                             v_pad[:, par, :, :, :].rearrange("p t h d -> p t (h d)")).then_inc(s_vst[par], 16)

            chunk(0, 0)
            with sp.Fori(0, CHUNKS // 2 - 1) as pair:
                c = pair * 2 + 1
                chunk(c, 1)
                chunk(c + 1, 0)
            chunk(CHUNKS - 1, 1)
            for m in range(TQ):
                sp.wait_ge(s_st[m], 16 * PARTS * CHUNKS)
            for par in range(2):
                sp.wait_ge(s_vst[par], 16 * CHUNKS // 2)


def attention(nc, tag, x, w, const, qk_parts, v_rows):
    with ExitStack() as ctx:
        ctx.enter_context(nc.cleanup_on_exit())

        def sb(name, shape, dt=F32):
            return ctx.enter_context(nc.sbuf_tensor(f"{tag}_{name}", shape, dt))

        def psum(name, shape, dt=F32):
            return ctx.enter_context(nc.psum_tensor(f"{tag}_{name}", shape, dt))

        def sem(name):
            return nc.alloc_semaphore(f"{tag}_{name}")

        STEPS = B * HG
        HALF = 512
        qs = [sb(f"q_stack{i}", [QK_ROWS + M_ROWS, GH, T], BF16) for i in range(2)]
        ks = [sb(f"k_stack{i}", [QK_ROWS + M_ROWS, GH, T], BF16) for i in range(2)]
        vg = [sb(f"v_group{i}", [P, BT, P]) for i in range(2)]
        probs = sb("probs", [P, 2, GH, T])
        max_of = sb("max_of", [P, 2, GH, BT])
        max_half = sb("max_half", [P, GH * BT])
        row_max = sb("row_max", [P, GH * BT])
        m_rest = sb("m_rest", [P, 2, GH * BT])
        m_parts = sb("m_parts", [P, M_ROWS, GH * BT], BF16)
        m_rows = sb("m_rows", [M_ROWS * GH * BT, P], BF16)
        exp_m = sb("exp_m", [P, T])
        v_masked = sb("v_masked", [P, T])
        masked_out = sb("masked_out", [P, T])
        out_sum = sb("out_sum", [P, T])
        inv = sb("inv", [P, BT, GH])
        inv_wide = sb("inv_wide", [P, BT, GH, P // GH])
        out_n = sb("out_n", [P, T])

        a_ps = psum("a", [P, 2, HALF])
        b_ps = psum("b", [P, 3, HALF])
        o_ps = psum("o", [P, T])
        misc = psum("misc", [P, HALF])
        misc_bf = misc[0:M_ROWS * GH * BT, 0:P // 2].bitcast(BF16)

        A_TILE = [[(h, lo, min(lo + HALF, P * (i + 1))) for h in range(GH) for lo in range(0, P * (i + 1), HALF)]
                  for i in range(BT)]
        A_UNITS = [(i, *u) for i in range(BT) for u in A_TILE[i]]
        B_UNITS = {j: [(h, lo, (lo // HALF + 1) * HALF) for lo in ([P * j, HALF] if j < BT // 2 else [P * j])
                       for h in range(GH)] for j in range(BT)}
        NA = len(A_UNITS)
        B_FIRST = [sum(len(B_UNITS[j]) for j in range(n)) for n in range(BT + 1)]
        NB = B_FIRST[BT]
        EARLY = 10
        NEXT = [EARLY, A_UNITS.index((BT // 2, 0, 0, HALF)), 25, 33, 41, NA, NA, NA, NA]
        AFTER = [0, 0, 0, 0, 0, 0, 2, 6, EARLY]
        EXPM0, EXPM1, DEN, VS1, VS0, INV0, INV1, PROJ0, PROJ1, PROJ2, MAXT, PROJ3 = ORDER = range(12)
        BEFORE = (DEN, INV0, INV1, PROJ0, PROJ1, PROJ2, PROJ3)
        TASKS = [[[EXPM0], [EXPM1]], [[DEN], [VS1]], [[VS0], [INV0]], [[INV1], [PROJ0]],
                 [[PROJ1]], [[PROJ2]], [[MAXT]], [[PROJ3]]]

        s_ld = [sem(f"half{half}_loaded_{par}") for par in ("even", "odd") for half in range(2)]
        s_ldv = [sem("v_loaded_even"), sem("v_loaded_odd")]
        s_vm = sem("v_masked_tile_ready")
        s_ones = sem("constants_set")
        s_em = sem("exp_max_begun")
        s_A = sem("a_scores_ready")
        s_Ac = sem("a_scores_used")
        chain = sem("dve_steps")
        s_mp = sem("max_parts_ready")
        s_m = [sem("max_rows_even"), sem("max_rows_odd")]
        s_B = sem("b_scores_ready")
        s_exp = sem("b_scores_used")
        s_pv = sem("tile_multiplied")
        s_mo = sem("masked_out_ready")
        s_sum = sem("out_sum_ready")
        s_fill = sem("misc_filled")
        s_used = sem("misc_used")
        s_inv = sem("inv_ready")
        s_invw = sem("inv_wide_ready")
        s_on = sem("out_normalised")

        def present(it):
            if not isinstance(it, int):
                return list(ORDER)
            return [k for k in ORDER if not (it == 0 and k in BEFORE) and not (it == STEPS - 1 and k == MAXT)
                    and not (it == STEPS and k not in BEFORE)]

        def task(it, k):
            if isinstance(it, int):
                return 1 + sum(len(present(n)) for n in range(it)) + present(it).index(k)
            return it * len(ORDER) - len(BEFORE) + 1 + k

        def before_max(it):
            return 0 if isinstance(it, int) and it == 0 else task(it - 1, MAXT)

        def plan(j):
            nb, halves = len(B_UNITS[j]), [] if j == 0 else sorted({lo // HALF for _, lo, _ in B_UNITS[j - 1]})
            order = []
            for u in range(nb):
                order.append(("b", u))
                for name, until in (("a", NEXT), ("early a", AFTER)):
                    n = until[j + 1] - until[j]
                    order += [(name, until[j] + k) for k in range(n * u // nb, n * (u + 1) // nb)]
                if u % GH == 1:
                    order += [("t", k) for k in TASKS[j][u // GH]]
                if u % GH == GH - 1:
                    here = halves if u == nb - 1 else halves[:1]
                    halves = halves[len(here):]
                    order += [("v", (half, half == 1)) for half in here]
            return order

        block = ctx.enter_context(nc.Block())

        @block.sync
        def _(sp):
            rows = v_rows.rearrange("(n p) f -> p n f", p=P)

            def load(it, par, half):
                b, g = it // HG, it % HG
                for which, stack in ((0, qs), (1, ks)):
                    for row, part, n in RUNS[which]:
                        sp.dma_start(stack[par][row * DH:(row + n) * DH, :, half * HALF:(half + 1) * HALF],
                                     qk_parts[which, bass.ds(g * GH, GH), part * DH:(part + n) * DH, bass.ds(b * T + half * HALF, HALF)]
                                     .rearrange("h r t -> r h t")).then_inc(s_ld[2 * par + half], 16)

            def load_v(it, par):
                b, g = it // HG, it % HG
                sp.dma_start(vg[par][:, :, :], rows[:, bass.ds(b * BT, BT), bass.ds(g * P, P)]).then_inc(s_ldv[par], 16)

            def max_rows(it, par):
                sp.wait_ge(s_used, before_max(it) + 1)
                for j in range(M_ROWS):
                    sp.dma_start(qs[par][QK_ROWS + j:QK_ROWS + j + 1, :, :].rearrange("a h t -> a (h t)"),
                                 m_rows[j * GH * BT:(j + 1) * GH * BT, :]).then_inc(s_m[par], 16)

            def step(it, par, last=False, load_next=True):
                if load_next:
                    sp.wait_ge(s_used, task(it, EXPM1) + 1)
                    sp.wait_ge(s_B, it * NB + B_FIRST[BT // 2])
                    load(it + 2, par, 0)
                if not last:
                    max_rows(it + 1, 1 - par)
                if load_next:
                    sp.wait_ge(s_pv, it * BT + BT + 2)
                    load(it + 2, par, 1)
                    load_v(it + 2, par)

            for it in range(2):
                for half in range(2):
                    load(it, it, half)
                load_v(it, it)
            max_rows(0, 0)
            step(0, 0)
            step(1, 1)
            with sp.Fori(1, STEPS // 2 - 1) as pair:
                it = pair * 2
                step(it, 0)
                step(it + 1, 1)
            step(STEPS - 2, 0, load_next=False)

        @block.gpsimd
        def _(pool):
            def masked_part(it):
                pool.wait_ge(s_used, task(it, VS0) + 1)
                if not (isinstance(it, int) and it == 0):
                    pool.wait_ge(s_sum, it)
                pool.tensor_tensor(masked_out[:, 0:T - 1], exp_m[:, 0:T - 1], v_masked[:, 0:T - 1], ALU.mult).then_inc(s_mo, 1)

            pool.memset(masked_out[:, T - 1:T], 0.0).then_inc(s_ones, 1)
            masked_part(0)
            masked_part(1)
            with pool.Fori(1, STEPS // 2) as pair:
                it = pair * 2
                masked_part(it)
                masked_part(it + 1)

        @block.scalar
        def _(act):
            def exp_unit(it, j, u):
                h, lo, hi = B_UNITS[j][u]
                n = B_FIRST[j] + u
                if u == 0:
                    act.wait_ge(s_pv, it * BT + j + 1)
                act.wait_ge(s_B, it * NB + n + 1)
                act.activation(probs[:, j % 2, h, lo:hi], b_ps[:, n % 3, lo % HALF:(hi - 1) % HALF + 1],
                               ACT.Exp, scale=float(T) ** -0.5).then_inc(s_exp, 1)

            def keep_max(it):
                act.wait_ge(s_fill, before_max(it) + 1)
                if not (isinstance(it, int) and it == 0):
                    act.wait_ge(s_B, (it - 1) * NB + 1)
                act.activation(m_rows[:, :], misc_bf, ACT.Copy).then_inc(s_used, 1)

            def task_of_act(it, k):
                if k in present(it):
                    if k in (EXPM0, EXPM1):
                        c = (k == EXPM1) * HALF
                        act.wait_ge(s_fill, task(it, k) + 1)
                        if k == EXPM0 and not (isinstance(it, int) and it == 0):
                            act.wait_ge(s_mo, it)
                        act.activation(exp_m[:, c:c + HALF], misc[:, :], ACT.Exp, scale=float(T) ** -0.5).then_inc(s_used, 1)
                    if k in (VS0, VS1):
                        act.wait_ge(s_fill, task(it, k) + 1)
                        for i in reversed(range(BT // 2, BT) if k == VS1 else range(BT // 2)):
                            here = misc[:, (i % (BT // 2)) * P + (i == 0):(i % (BT // 2) + 1) * P]
                            out = v_masked[:, max(i * P - 1, 0):(i + 1) * P - 1]
                            if i == BT - 1:
                                last = act.activation(out, here, ACT.Copy)
                            else:
                                act.wait_ge(s_vm, it * BT + BT - 1 - i)
                                last = act.activation(out, here, ACT.Identity, bias=v_masked[:, (i + 1) * P - 1:(i + 1) * P])
                            last.then_inc(s_vm, 1)
                        act.wait_ge(s_vm, it * BT + (BT // 2 if k == VS1 else BT))
                        act.sem_inc(s_used, 1)
                    if k == DEN:
                        act.wait_ge(s_inv, it)
                        if not (isinstance(it, int) and it == 1):
                            act.wait_ge(s_on, 2 * (it - 1))
                        act.activation(inv_wide[:, :, :, :].rearrange("p i h d -> p (i h) d"),
                                       inv[:, :, :].rearrange("p i (h a) -> p (i h) a", a=1).broadcast_to([P, BT * GH, P // GH]),
                                       ACT.Copy).then_inc(s_invw, 1)
                    if k == MAXT:
                        keep_max(it + 1)

            def step(it):
                for j in range(BT):
                    for what, u in plan(j):
                        if what == "b":
                            exp_unit(it, j, u)
                        if what == "t":
                            task_of_act(it, u)

            act.sem_inc(s_exp, 3)
            keep_max(0)
            step(0)
            step(1)
            with act.Fori(1, STEPS // 2 - 1) as pair:
                it = pair * 2
                step(it)
                step(it + 1)
            step(STEPS - 2)
            step(STEPS - 1)
            for k in BEFORE:
                task_of_act(STEPS, k)

        @block.vector
        def _(dve):
            def maximum(it, n):
                i, h, lo, hi = A_UNITS[n]
                dve.wait_ge(s_A, it * NA + n + 1)
                dve.tensor_reduce(max_of[:, lo // HALF, h, i:i + 1], a_ps[:, n % 2, 0:hi - lo], AX.X, ALU.max).then_inc(s_Ac, 1)

            M_STEPS = 6

            def finish_maxima(it):
                base = it * M_STEPS
                flat = lambda a: a.rearrange("p h i -> p (h i)")
                dve.wait_ge(s_Ac, it * NA + NA + 2)
                dve.tensor_tensor(max_half[:, :], flat(max_of[:, 0, :, :]), flat(max_of[:, 1, :, :]), ALU.max).then_inc(chain, 1)
                dve.wait_ge(chain, base + 1)
                dve.tensor_tensor(row_max[:, :], max_half[:, :], const["floor"][:, :], ALU.max).then_inc(chain, 1)
                dve.wait_ge(chain, base + 2)
                three_parts(dve, chain, base + 2, row_max[:, :], m_parts[:, 0, :], m_rest[:, 0, :],
                            m_parts[:, 1, :], m_rest[:, 1, :], m_parts[:, 2, :]).then_inc(s_mp, 1)

            def sum_up(it):
                dve.wait_ge(s_pv, it * BT + BT + 2)
                dve.wait_ge(s_mo, it + 1)
                if not (isinstance(it, int) and it == 0):
                    dve.wait_ge(s_on, 2 * it)
                for half in range(2):
                    c = slice(half * HALF, (half + 1) * HALF)
                    last = dve.tensor_tensor(out_sum[:, c], masked_out[:, c], o_ps[:, c], ALU.add)
                last.then_inc(s_sum, 1)

            def task_of_dve(it, k):
                if k in present(it):
                    if k == DEN:
                        dve.wait_ge(s_fill, task(it, k) + 1)
                        dve.reciprocal(inv[:, :, :].rearrange("p i h -> p (i h)"), misc[:, 0:BT * GH]).then_inc(s_inv, 1)
                        dve.wait_ge(s_inv, it)
                        dve.sem_inc(s_used, 1)
                    if k in (INV0, INV1):
                        half = (k == INV1) * 1
                        dve.wait_ge(s_fill, task(it, k) + 1)
                        c = slice(half * HALF, (half + 1) * HALF)
                        dve.tensor_tensor(out_n[:, c], out_sum[:, c], misc[:, :], ALU.mult).then_inc(s_on, 1)
                        dve.wait_ge(s_on, 2 * (it - 1) + half + 1)
                        dve.sem_inc(s_used, 1)
                    if k in (PROJ0, PROJ1, PROJ2, PROJ3):
                        dve.wait_ge(s_fill, task(it, k) + 1)
                        p = [PROJ0, PROJ1, PROJ2, PROJ3].index(k)
                        b = (it - 1) // HG
                        where = x[:, bass.ds(b * BT + 2 * p, 2), :]
                        dve.tensor_tensor(where, misc[:, :].rearrange("p (a d) -> p a d", a=2), where, ALU.add).then_inc(s_used, 1)

            def step(it, first=False, ahead=2):
                if not first:
                    sum_up(it - 1)
                for j in range(BT):
                    for what, u in plan(j):
                        if what == "early a" and ahead >= 2:
                            maximum(it + 2, u)
                        if what == "a" and ahead >= 1:
                            maximum(it + 1, u)
                            if u == NA - 1:
                                finish_maxima(it + 1)
                        if what == "t":
                            task_of_dve(it, u)

            dve.memset(max_of[:, :, :, :], -3e38).then_inc(s_ones, 1)
            for i in range(2):
                dve.memset(ks[i][QK_ROWS:QK_ROWS + M_ROWS, :, :], -1.0).then_inc(s_ones, 1)
            dve.sem_inc(s_Ac, 2)
            dve.wait_ge(s_ones, 4)
            for n in range(NA):
                maximum(0, n)
            finish_maxima(0)
            for n in range(EARLY):
                maximum(1, n)
            step(0, first=True)
            step(1)
            with dve.Fori(1, STEPS // 2 - 1) as pair:
                it = pair * 2
                step(it)
                step(it + 1)
            step(STEPS - 2, ahead=1)
            step(STEPS - 1, ahead=0)
            sum_up(STEPS - 1)
            for k in BEFORE:
                task_of_dve(STEPS, k)

        @block.tensor
        def _(pe):
            def score_a(it, par, n):
                i, h, lo, hi = A_UNITS[n]
                if (i, h, lo) in ((0, 0, 0), (BT // 2, 0, 0)):
                    pe.wait_ge(s_ld[2 * par + (i > 0)], 16 * sum(map(len, RUNS)) * (it // 2 + 1))
                diagonal = hi == P * (i + 1)
                pe.wait_ge(s_Ac, it * NA + n + 1)
                last = pe.matmul(a_ps[:, n % 2, 0:hi - lo], qs[par][0:QK_ROWS, h, i * P:(i + 1) * P],
                                 ks[par][0:QK_ROWS, h, lo:hi], start=True, stop=True)
                if diagonal:
                    last = pe.matmul(a_ps[:, n % 2, hi - P - lo:hi - lo], const["ident_bf"][:, :], const["hide_right"][:, :],
                                     start=False, stop=True, skip_group_check=True)
                last.then_inc(s_A, 1)

            def score_b(it, par, j, u):
                h, lo, hi = B_UNITS[j][u]
                n = B_FIRST[j] + u
                if n == 0:
                    pe.wait_ge(s_ldv[par], 16 * (it // 2 + 1))
                    pe.wait_ge(s_m[par], 16 * M_ROWS * (it // 2 + 1))
                diagonal = lo == P * j
                at = lo % HALF
                pe.wait_ge(s_exp, it * NB + n + 1)
                last = pe.matmul(b_ps[:, n % 3, at:at + hi - lo], ks[par][:, h, j * P:(j + 1) * P], qs[par][:, h, lo:hi],
                                 start=True, stop=True)
                if diagonal:
                    last = pe.matmul(b_ps[:, n % 3, at:at + P], const["ident_bf"][:, :], const["hide_below"][:, :],
                                     start=False, stop=True, skip_group_check=True)
                last.then_inc(s_B, 1)

            def values(it, par, j, half, end):
                if j == 0 and half == 0 and not (isinstance(it, int) and it == 0):
                    pe.wait_ge(s_sum, it)
                pe.wait_ge(s_exp, it * NB + B_FIRST[j + 1] + 3)
                for h, lo, hi in B_UNITS[j]:
                    if lo // HALF == half:
                        last = pe.matmul(o_ps[32 * h:32 * h + 32, lo:hi], vg[par][:, j, 32 * h:32 * h + 32],
                                         probs[:, j % 2, h, lo:hi], start=(j == 0),
                                         stop=(j == (BT // 2 - 1 if half == 0 else BT - 1)), skip_group_check=True)
                if end:
                    last.then_inc(s_pv, 1)

            def turn_max(it):
                pe.wait_ge(s_mp, it + 1)
                if not (isinstance(it, int) and it == 0):
                    pe.wait_ge(s_used, before_max(it))
                pe.transpose(misc_bf, m_parts[:, :, :].rearrange("p j n -> p (j n)"), const["ident_bf"][:, :]).then_inc(s_fill, 1)

            def task_of_pe(it, par, k):
                if k == MAXT:
                    if k in present(it):
                        turn_max(it + 1)
                elif k in present(it):
                    pe.wait_ge(s_used, task(it, k))
                    if k == DEN:
                        pe.wait_ge(s_sum, it)
                        for i in range(BT):
                            mm = pe.matmul(misc[:, i * GH:(i + 1) * GH], out_sum[:, i * P:(i + 1) * P], const["pick_den"][:, :],
                                           start=True, stop=True)
                    if k in (INV0, INV1):
                        pe.wait_ge(s_invw, it)
                        for i in range(BT // 2):
                            mm = pe.matmul(misc[:, i * P:(i + 1) * P],
                                           inv_wide[:, (k == INV1) * (BT // 2) + i, :, :].rearrange("p h d -> p (h d)"),
                                           const["ident"][:, :], start=True, stop=True)
                    if k in (PROJ0, PROJ1, PROJ2, PROJ3):
                        pe.wait_ge(s_on, 2 * it)
                        p = [PROJ0, PROJ1, PROJ2, PROJ3].index(k)
                        g = (it - 1) % HG
                        for a in range(2):
                            i = 2 * p + a
                            mm = pe.matmul(misc[:, a * D:(a + 1) * D], out_n[:, i * P:(i + 1) * P],
                                           w["wo"][:, bass.ds(g, 1), :].rearrange("p a d -> p (a d)"), start=True, stop=True)
                    if k in (EXPM0, EXPM1):
                        c = (k == EXPM1) * HALF
                        pe.sem_inc(s_em, 1)
                        for h in range(GH):
                            mm = pe.matmul(misc[32 * h:32 * h + 32, :], ks[par][QK_ROWS:QK_ROWS + M_ROWS, h, 0:32],
                                           qs[par][QK_ROWS:QK_ROWS + M_ROWS, h, c:c + HALF], start=True, stop=True)
                    if k in (VS0, VS1):
                        for n in range(BT // 2):
                            mm = pe.matmul(misc[:, n * P:(n + 1) * P], vg[par][:, (k == VS1) * (BT // 2) + n, :],
                                           const["onward"][:, :], start=True, stop=True)
                    mm.then_inc(s_fill, 1)

            def step(it, par, ahead=2):
                for j in range(BT):
                    for what, u in plan(j):
                        if what == "b":
                            score_b(it, par, j, u)
                        if what == "early a" and ahead >= 2:
                            score_a(it + 2, par, u)
                        if what == "a" and ahead >= 1:
                            score_a(it + 1, 1 - par, u)
                        if what == "v":
                            values(it, par, j - 1, *u)
                        if what == "t":
                            task_of_pe(it, par, u)
                values(it, par, BT - 1, 1, end=True)

            pe.sem_inc(s_pv, 2)
            pe.wait_ge(s_ones, 4)
            for n in range(NA):
                score_a(0, 0, n)
            turn_max(0)
            for n in range(EARLY):
                score_a(1, 1, n)
            step(0, 0)
            step(1, 1)
            with pe.Fori(1, STEPS // 2 - 1) as pair:
                pe.get_value_cache().nocache = True
                it = pair * 2
                step(it, 0)
                step(it + 1, 1)
            step(STEPS - 2, 0, ahead=1)
            step(STEPS - 1, 1, ahead=0)
            for k in BEFORE:
                task_of_pe(STEPS, 0, k)


def scan_mixer(nc, tag, x, w, const, pick_in):
    with ExitStack() as ctx:
        ctx.enter_context(nc.cleanup_on_exit())

        def sb(name, shape, dt=F32):
            return ctx.enter_context(nc.sbuf_tensor(f"{tag}_{name}", shape, dt))

        def psum(name, shape, dt=F32):
            return ctx.enter_context(nc.psum_tensor(f"{tag}_{name}", shape, dt))

        def sem(name):
            return nc.alloc_semaphore(f"{tag}_{name}")

        N2 = 2 * STATES
        SLOTS = KD * STATES
        pick_bc = sb("pick_bc", list(pick_in.shape), BF16)
        a_exp = sb("a_exp", [P, KD, STATES])
        a_neg = sb("a_neg", [P, KD, STATES])
        xn = sb("xn", [P, CT, D])
        stats = sb("stats", [P, CT, 6])
        mean_var = sb("mean_var", [P, CT, 2])
        var_eps = sb("var_eps", [P, CT])
        rstd = sb("rstd", [P, CT])
        xnT = sb("xnT", [P, 2, KD, CH])
        low = sb("low", [RANK, CH])
        bc_rest = sb("bc_rest", [P, 2, CT, N2])
        bc_parts = sb("bc_parts", [P, CT, 3 * N2], BF16)
        bcT = sb("bcT", [3 * N2, 2, CH], BF16)
        z = sb("z", [P, KD, CH])
        z_abs = sb("z_abs", [P, KD, CH])
        z_exp = sb("z_exp", [P, KD, CH])
        z_log = sb("z_log", [P, KD, CH])
        delta = sb("delta", [P, 2, KD, CH])
        du = sb("du", [P, 2, KD, CH])
        decay = sb("decay", [P, 4, CH])
        drive = sb("drive", [P, 4, CH])
        h = sb("h", [P, 4, CH])
        state = sb("state", [P, SLOTS])
        c_bc = sb("c_bc", [P, 2, CH])
        hc = sb("hc", [P, 4, CH])
        y_out = sb("y_out", [P, KD, CH])

        b_ps = psum("b", [P, 2, CH])
        c_ps = psum("c", [P, CH])
        y_ps = psum("y", [P, KD, CH])
        misc = [psum(f"misc{i}", [P, CH]) for i in range(3)]

        s_pick = sem("pick_bc_here")
        once = sem("a_ready")
        s_stat = sem("stats_ready")
        s_mv = sem("mean_var_ready")
        s_var = sem("var_ready")
        s_rstd = sem("rstd_ready")
        s_xn = sem("xn_ready")
        s_fill = sem("misc_filled")
        s_act = sem("misc_used_by_act")
        s_dve = sem("misc_used_by_dve")
        chain = sem("part_steps")
        s_bcp = sem("bc_parts_ready")
        s_abs = sem("z_abs_ready")
        s_zexp = sem("z_exp_ready")
        s_log = sem("z_log_ready")
        s_delta = sem("delta_ready")
        s_du = sem("du_ready")
        s_b = sem("b_spread")
        s_c = sem("c_spread")
        s_ck = sem("c_kept")
        s_decay = sem("decay_ready")
        s_drive = sem("drive_ready")
        s_h = sem("h_ready")
        s_state = sem("state_kept")
        s_hc = sem("hc_ready")
        s_y = sem("y_added")
        s_yout = sem("y_out_ready")
        s_add = sem("chunk_added")

        TA, TB, LOW, BC, DT0, DT1, BCT, OUT0, OUT1 = range(9)
        ACT_USES = [TA, TB, LOW, BCT]
        DVE_USES = [BC, DT0, DT1, OUT0, OUT1]
        PREP = 7

        def bank(c, k):
            return misc[(k if c is None else PREP + k) % 3]

        def filled(c, k, last=False):
            if c is None:
                return k + 1
            return PREP + c * 9 + (k - PREP if last else k) + 1

        def used_act(c, k):
            return ACT_USES.index(k) + 1 + (0 if c is None else 4 * (c + 1))

        def used_dve(c, k, last=False):
            if c is None:
                return DVE_USES.index(k) + 1
            return 3 + 5 * c + DVE_USES.index(k) + 1 - (3 if last else 0)

        def chunk_of(c):
            return 0 if c is None else c + 1

        def tiles(c, t, n=1):
            return slice(c * CT + t, c * CT + t + n) if isinstance(c, int) else bass.ds(c * CT + t, n)

        block = ctx.enter_context(nc.Block())

        @block.sync
        def _(sp):
            sp.dma_start(pick_bc[:, :, :], pick_in).then_inc(s_pick, 16)

        @block.vector
        def _(dve):
            def norm_stats(c):
                for t in range(CT):
                    last = dve.bn_stats(stats[:, t, :], x[:, tiles(c, t), :].rearrange("p a d -> p (a d)"))
                last.then_inc(s_stat, 1)
                dve.wait_ge(s_stat, c + 1)
                dve.sem_inc(s_mv, 1)
                for t in range(CT):
                    last = dve.bn_aggr(mean_var[:, t, :], stats[:, t, :])
                last.then_inc(s_mv, 1)
                dve.wait_ge(s_mv, 2 * c + 2)
                dve.tensor_scalar(var_eps[:, :], mean_var[:, :, 1], EPS, None, ALU.add).then_inc(s_var, 1)

            def norm_apply(c):
                dve.wait_ge(s_rstd, c + 1)
                for t in range(CT):
                    last = dve.tensor_scalar(xn[:, t, :], x[:, tiles(c, t), :].rearrange("p a d -> p (a d)"),
                                             mean_var[:, t, 0:1], rstd[:, t:t + 1], ALU.subtract, ALU.mult)
                last.then_inc(s_xn, 1)

            def split_bc(beside):
                c = chunk_of(beside)
                dve.wait_ge(s_fill, filled(beside, BC))
                whole = bank(beside, BC)[:, 0:CT * N2].rearrange("p (t n) -> p t n", t=CT)
                base = c * 4
                dve.tensor_copy(bc_parts[:, :, 0:N2], whole).then_inc(chain, 1)
                dve.wait_ge(chain, base + 1)
                dve.tensor_tensor(bc_rest[:, 0, :, :], whole, bc_parts[:, :, 0:N2], ALU.subtract).then_inc(s_dve, 1)
                dve.wait_ge(s_dve, used_dve(beside, BC))
                dve.tensor_copy(bc_parts[:, :, N2:2 * N2], bc_rest[:, 0, :, :]).then_inc(chain, 1)
                dve.wait_ge(chain, base + 2)
                dve.tensor_tensor(bc_rest[:, 1, :, :], bc_rest[:, 0, :, :], bc_parts[:, :, N2:2 * N2], ALU.subtract).then_inc(chain, 1)
                dve.wait_ge(chain, base + 3)
                dve.tensor_copy(bc_parts[:, :, 2 * N2:3 * N2], bc_rest[:, 1, :, :]).then_inc(chain, 1)
                dve.wait_ge(chain, base + 4)
                dve.sem_inc(s_bcp, 1)

            def biased(beside, m):
                c = chunk_of(beside)
                dve.wait_ge(s_fill, filled(beside, DT0 + m))
                dve.tensor_scalar(z[:, m, :], bank(beside, DT0 + m)[:, :], w["dt_b"][:, m:m + 1], None, ALU.add).then_inc(s_dve, 1)
                dve.wait_ge(s_dve, used_dve(beside, DT0 + m))
                dve.scalar_tensor_tensor(out=z_abs[:, m, :], in0=z[:, m, :], scalar=-1.0, in1=z[:, m, :], op0=ALU.mult, op1=ALU.max).then_inc(s_abs, 1)

            def soft(c, par, m):
                dve.wait_ge(s_log, 2 * c + m + 1)
                dve.scalar_tensor_tensor(out=delta[:, par, m, :], in0=z[:, m, :], scalar=0.0, in1=z_log[:, m, :],
                                         op0=ALU.max, op1=ALU.add).then_inc(s_delta, 1)
                dve.wait_ge(s_delta, 2 * c + m + 1)
                dve.tensor_tensor(du[:, par, m, :], delta[:, par, m, :], xnT[:, par, m, :], ALU.mult).then_inc(s_du, 1)

            def drives(c, par, s):
                m = s % 2
                if s == 0:
                    dve.wait_ge(s_du, 2 * c + 2)
                if m == 0:
                    dve.wait_ge(s_b, c * STATES + s // 2 + 1)
                dve.tensor_tensor(drive[:, s % 4, :], du[:, par, m, :], b_ps[:, (s // 2) % 2, :], ALU.mult).then_inc(s_drive, 1)

            def slot(c, par, s, last=False):
                n, m = c * SLOTS + s, s % 2
                if s + 1 < SLOTS:
                    drives(c, par, s + 1)
                elif not last:
                    drives(c + 1, 1 - par, 0)
                dve.wait_ge(s_drive, n + 3)
                dve.wait_ge(s_decay, n + 1)
                dve.wait_ge(s_hc, n + 1)
                if par == 0:
                    first = 0.0
                else:
                    dve.wait_ge(s_state, (c - 1) * STATES + s + 1)
                    first = state[:, s:s + 1]
                dve.tensor_tensor_scan(h[:, s % 4, :], decay[:, s % 4, :], drive[:, s % 4, :], first,
                                       ALU.mult, ALU.add).then_inc(s_h, 1)

            def out(c, par):
                dve.wait_ge(s_y, c * SLOTS + SLOTS + 4)
                for m in range(KD):
                    last = dve.scalar_tensor_tensor(out=y_out[:, m, :], in0=xnT[:, par, m, :], scalar=w["D"][:, m:m + 1],
                                                    in1=y_ps[:, m, :], op0=ALU.mult, op1=ALU.add)
                last.then_inc(s_yout, 1)

            def add(c, last):
                for r in range(2):
                    dve.wait_ge(s_fill, filled(c, OUT0 + r, last))
                    here = x[:, tiles(c, 2 * r, 2), :]
                    b = bank(c, OUT0 + r if not last else r)
                    dve.tensor_tensor(here, b[:, :].rearrange("p (a d) -> p a d", a=2), here, ALU.add).then_inc(s_dve, 1)

            def chunk(c, par, last=False):
                for s in range(3, SLOTS):
                    slot(c, par, s, last)
                    if not last:
                        if s == 4:
                            norm_stats(c + 1)
                        if s == 6:
                            norm_apply(c + 1)
                        if s == 14:
                            split_bc(c)
                        if s in (17, 18):
                            biased(c, s - 17)
                        if s in (25, 26):
                            soft(c + 1, 1 - par, s - 25)
                if not last:
                    for s in range(3):
                        slot(c + 1, 1 - par, s)
                out(c, par)
                add(c, last)

            dve.sem_inc(s_drive, 2)
            dve.sem_inc(s_h, 4)
            dve.sem_inc(s_yout, 1)
            dve.wait_ge(once, 1)
            dve.tensor_scalar(a_neg[:, :, :], a_exp[:, :, :], -1.0, None, ALU.mult).then_inc(once, 1)
            norm_stats(0)
            norm_apply(0)
            split_bc(None)
            for m in range(KD):
                biased(None, m)
            for m in range(KD):
                soft(0, 0, m)
            drives(0, 0, 0)
            for s in range(3):
                slot(0, 0, s)
            with dve.Fori(0, CHUNKS // 2 - 1) as pair:
                c = pair * 2
                chunk(c, 0)
                chunk(c + 1, 1)
            chunk(CHUNKS - 2, 0)
            chunk(CHUNKS - 1, 1, last=True)

        @block.gpsimd
        def _(pool):
            def norm_pow(c):
                pool.wait_ge(s_var, c + 1)
                pool.tensor_tensor(rstd[:, :], var_eps[:, :], const["minus_half"][:, 0:CT], ALU.pow).then_inc(s_rstd, 1)

            def chunk(c, par, last=False):
                for s in range(SLOTS):
                    n = c * SLOTS + s
                    pool.wait_ge(s_h, n + 5)
                    if par == 0:
                        end = h[:, s % 4, CH - 1:CH]
                        pool.tensor_tensor(state[:, s:s + 1], end, const["one"][:, 0:1], ALU.mult).then_inc(s_state, 1)
                    if s % 2 == 0:
                        pool.wait_ge(s_ck, c * STATES + s // 2 + 2)
                    pool.wait_ge(s_y, n + 1)
                    pool.tensor_tensor(hc[:, s % 4, :], h[:, s % 4, :], c_bc[:, (s // 2) % 2, :], ALU.mult).then_inc(s_hc, 1)
                    if s == 4 and not last:
                        norm_pow(c + 1)

            pool.sem_inc(s_hc, 4)
            norm_pow(0)
            with pool.Fori(0, CHUNKS // 2 - 1) as pair:
                c = pair * 2
                chunk(c, 0)
                chunk(c + 1, 1)
            chunk(CHUNKS - 2, 0)
            chunk(CHUNKS - 1, 1, last=True)

        @block.scalar
        def _(act):
            def keep(beside, k, out):
                act.wait_ge(s_fill, filled(beside, k))
                src = bank(beside, k)
                if k == LOW:
                    src = src[0:RANK, :]
                elif k == BCT:
                    src = src[0:3 * N2, 0:CH // 2].bitcast(BF16)
                else:
                    src = src[:, :]
                act.activation(out, src, ACT.Copy).then_inc(s_act, 1)

            def logs(c, m):
                act.wait_ge(s_abs, 2 * c + m + 1)
                act.activation(z_exp[:, m, :], z_abs[:, m, :], ACT.Exp, scale=-1.0).then_inc(s_zexp, 1)
                act.wait_ge(s_zexp, 2 * c + m + 1)
                act.activation(z_log[:, m, :], z_exp[:, m, :], ACT.Ln, bias=const["one"][:, 0:1]).then_inc(s_log, 1)

            def slot(c, par, s):
                n, m = c * SLOTS + s, s % 2
                if m == 0:
                    i = c * STATES + s // 2
                    act.wait_ge(s_c, i + 1)
                    act.wait_ge(s_hc, 2 * i + 2)
                    act.activation(c_bc[:, (s // 2) % 2, :], c_ps[:, :], ACT.Copy).then_inc(s_ck, 1)
                act.wait_ge(s_h, n + 1)
                if s < 2:
                    act.wait_ge(s_delta, 2 * c + s + 1)
                act.activation(decay[:, s % 4, :], delta[:, par, m, :], ACT.Exp,
                               scale=a_neg[:, m, s // 2:s // 2 + 1]).then_inc(s_decay, 1)

            def chunk(c, par, last=False):
                for s in range(SLOTS):
                    slot(c, par, s)
                    if not last:
                        if s == 11:
                            keep(c, TA, xnT[:, 1 - par, 0, :])
                            keep(c, TB, xnT[:, 1 - par, 1, :])
                        if s == 14:
                            keep(c, LOW, low[:, :])
                        if s in (21, 22):
                            logs(c + 1, s - 21)
                        if s == 23:
                            keep(c, BCT, bcT[:, 1 - par, :])

            act.activation(a_exp[:, :, :], w["A_log"][:, :, :], ACT.Exp).then_inc(once, 1)
            act.sem_inc(s_ck, 1)
            keep(None, TA, xnT[:, 0, 0, :])
            keep(None, TB, xnT[:, 0, 1, :])
            keep(None, LOW, low[:, :])
            for m in range(KD):
                logs(0, m)
            keep(None, BCT, bcT[:, 0, :])
            act.wait_ge(once, 2)
            with act.Fori(0, CHUNKS // 2 - 1) as pair:
                c = pair * 2
                chunk(c, 0)
                chunk(c + 1, 1)
            chunk(CHUNKS - 2, 0)
            chunk(CHUNKS - 1, 1, last=True)

        @block.tensor
        def _(pe):
            def turn_halves(beside):
                pe.wait_ge(s_xn, chunk_of(beside) + 1)
                if beside is not None:
                    pe.wait_ge(s_act, 4 * (beside + 1))
                    pe.wait_ge(s_dve, 3 + 5 * beside)
                for k in range(KD):
                    for t in range(CT):
                        last = pe.transpose(bank(beside, TA + k)[:, t * P:(t + 1) * P], xn[:, t, k * P:(k + 1) * P], const["ident"][:, :])
                    last.then_inc(s_fill, 1)

            def project(beside, par):
                pe.wait_ge(s_act, used_act(beside, TB))
                for k in range(KD):
                    last = pe.matmul(bank(beside, LOW)[0:RANK, :], w["low"][:, k, :], xnT[:, par, k, :], start=(k == 0), stop=(k == KD - 1))
                last.then_inc(s_fill, 1)
                for t in range(CT):
                    for k in range(KD):
                        last = pe.matmul(bank(beside, BC)[:, t * N2:(t + 1) * N2], xnT[:, par, k, t * P:(t + 1) * P], w["bc"][:, k, :],
                                         start=(k == 0), stop=(k == KD - 1))
                last.then_inc(s_fill, 1)

            def steps(beside):
                pe.wait_ge(s_act, used_act(beside, LOW))
                for m in range(KD):
                    pe.matmul(bank(beside, DT0 + m)[:, :], w["dt_w"][:, m * P:(m + 1) * P], low[:, :], start=True, stop=True).then_inc(s_fill, 1)

            def turn_bc(beside):
                pe.wait_ge(s_bcp, chunk_of(beside) + 1)
                dst = bank(beside, BCT)[0:3 * N2, 0:CH // 2].bitcast(BF16)
                for t in range(CT):
                    last = pe.transpose(dst[:, t * P:(t + 1) * P], bc_parts[:, t, :], const["ident_bf"][:, :])
                last.then_inc(s_fill, 1)

            def spread(c, par, n):
                i = c * STATES + n
                if n == 0:
                    pe.wait_ge(s_act, 4 * (c + 1))
                pe.wait_ge(s_drive, 2 * i)
                pe.matmul(b_ps[:, n % 2, :], pick_bc[:, n, :], bcT[:, par, :], start=True, stop=True).then_inc(s_b, 1)
                pe.wait_ge(s_ck, i + 1)
                pe.matmul(c_ps[:, :], pick_bc[:, STATES + n, :], bcT[:, par, :], start=True, stop=True).then_inc(s_c, 1)

            def collect(c, par, s):
                n, m = c * SLOTS + s, s % 2
                if s == 0:
                    pe.wait_ge(s_yout, c + 1)
                pe.wait_ge(s_hc, n + 5)
                pe.matmul(y_ps[:, m, :], const["ident"][:, :], hc[:, s % 4, :], start=(s < 2), stop=(s >= SLOTS - 2)).then_inc(s_y, 1)

            def turn_out(c, last):
                pe.wait_ge(s_yout, c + 2)
                for r in range(2):
                    pe.wait_ge(s_dve, 3 + 5 * c + (3 if not last else 0))
                    b = bank(c, OUT0 + r if not last else r)
                    for a in range(2):
                        for m in range(KD):
                            t = 2 * r + a
                            mm = pe.transpose(b[:, a * D + m * P:a * D + (m + 1) * P], y_out[:, m, t * P:(t + 1) * P], const["ident"][:, :])
                    mm.then_inc(s_fill, 1)

            def chunk(c, par, last=False):
                for s in range(SLOTS):
                    if s % 2 == 0:
                        n = s // 2 + 2
                        if n < STATES:
                            spread(c, par, n)
                        elif not last:
                            spread(c + 1, 1 - par, n - STATES)
                    collect(c, par, s)
                    if not last:
                        if s == 7:
                            turn_halves(c)
                        if s == 9:
                            project(c, 1 - par)
                        if s == 13:
                            steps(c)
                        if s == 16:
                            turn_bc(c)
                turn_out(c, last)

            pe.sem_inc(s_y, 4)
            turn_halves(None)
            project(None, 0)
            steps(None)
            turn_bc(None)
            pe.wait_ge(s_pick, 16)
            spread(0, 0, 0)
            spread(0, 0, 1)
            with pe.Fori(0, CHUNKS // 2 - 1) as pair:
                c = pair * 2
                chunk(c, 0)
                chunk(c + 1, 1)
            chunk(CHUNKS - 2, 0)
            chunk(CHUNKS - 1, 1, last=True)


def build(nc, ins, out, stages):
    with ExitStack() as ctx:
        def keep(names, within=ctx):
            return {n: within.enter_context(nc.sbuf_tensor("w_" + n, list(ins[n].shape), ins[n].dtype)) for n in names}

        def load(sp, kept, here):
            for n, t in kept.items():
                sp.dma_start(t[tuple(slice(None) for _ in t.shape)], ins[n]).then_inc(here, 16)

        def weights(kept, prefix):
            return {n[len(prefix):]: t for n, t in kept.items() if n.startswith(prefix)}

        x = ctx.enter_context(nc.sbuf_tensor("x", [P, TILES, D], F32))
        x_tiles = ins["x"].rearrange("b (t p) d -> p (b t) d", p=P)
        first = ["ident", "ident_bf", "minus_half", "iota", "pick_gate", "f0_router"]
        by_unit = ["f0_gate", "f0_up", "f0_down"]
        late = [n for n in ins if n.startswith(("f1_", "sc_")) or n in ("pick_gate1", "cost")]
        by_stage = ["at_wq", "at_wk", "at_wv", "pick_bc"]
        early = keep([n for n in ins if n not in ["x"] + by_unit + late + by_stage and not n.startswith("at_")])
        first_layer = ctx.enter_context(ExitStack())
        to_split = ctx.enter_context(ExitStack())

        def by_units(within, kind, dt):
            return {n: within.enter_context(nc.sbuf_tensor(f"{n}_{kind}", list(ins[n].shape), dt, side="right")) for n in by_unit}

        high, low = (by_units(first_layer, half, R32) for half in ("hi", "lo"))
        raw0 = by_units(to_split, "raw", F32)
        f0 = {n[3:]: (high[n], low[n]) for n in by_unit}
        attention_only = ctx.enter_context(ExitStack())
        early.update(keep(["at_wo"], attention_only))
        qk_parts = nc.dram_tensor("qk_parts", (2, HEADS, PARTS * DH, TOKENS), BF16, kind="Internal").ap()
        v_rows = nc.dram_tensor("v_rows", (TOKENS, HEADS * 2 * DH), F32, kind="Internal").ap()
        s_first = ctx.enter_context(nc.semaphore("first_inputs_here"))
        s_x = ctx.enter_context(nc.semaphore("rest_of_x_here"))
        s_w = ctx.enter_context(nc.semaphore("rest_of_units_here"))
        s_early = ctx.enter_context(nc.semaphore("early_inputs_here"))
        s_late = ctx.enter_context(nc.semaphore("late_inputs_here"))
        s_out = ctx.enter_context(nc.semaphore("outputs_there"))

        def load_x(sp, c, here):
            sp.dma_start(x[:, c * CT:(c + 1) * CT, :], x_tiles[:, c * CT:(c + 1) * CT, :]).then_inc(here, 16)

        with nc.Block() as block:
            @block.sync
            def _(sp):
                load_x(sp, 0, s_first)
                load(sp, {n: early[n] for n in first}, s_first)
                for n in by_unit:
                    sp.dma_start(raw0[n][:, 0:FIRST_UNITS], ins[n][:, 0:FIRST_UNITS]).then_inc(s_first, 16)
                for c in range(1, FIRST_CHUNKS):
                    load_x(sp, c, s_first)
                sp.wait_ge(s_first, 16 * (FIRST_CHUNKS + len(first) + len(by_unit)))

        def load_early(sp):
            rest = {n: t for n, t in early.items() if n not in first}
            for n in by_unit:
                sp.dma_start(raw0[n][:, FIRST_UNITS:UNITS0], ins[n][:, FIRST_UNITS:UNITS0]).then_inc(s_w, 16)
            for c in range(FIRST_CHUNKS, CHUNKS):
                load_x(sp, c, s_x)
            load(sp, rest, s_early)
            sp.wait_ge(s_w, 16 * len(by_unit))
            sp.wait_ge(s_x, 16 * (CHUNKS - FIRST_CHUNKS))
            sp.wait_ge(s_early, 16 * len(rest))

        const = dict(early)
        f0["router"] = early["f0_router"]
        for n, s in enumerate(stages):
            if n == 0:
                ffn_moe(nc, f"a{n}", x, f0, const, load_early, x_rest=(s_x, 16 * (CHUNKS - FIRST_CHUNKS)),
                        raw=({n[3:]: t for n, t in raw0.items()}, (s_first, 1), (s_w, 16 * len(by_unit))))
                to_split.close()
            elif s == "ffn_moe":
                attention_only.close()
                second = keep([n for n in late if n not in ("f1_w1", "f1_w2")])
                split = ("f1_w1", "f1_w2")
                raw1 = keep(split, to_split)
                const.update(second)

                def load_late(sp):
                    load(sp, second, s_late)
                    load(sp, raw1, s_late)
                    sp.wait_ge(s_late, 16 * (len(second) + len(raw1)))

                ffn_moe(nc, f"a{n}", x, f0, const, load_late)
                first_layer.close()
                halves = {n: [ctx.enter_context(nc.sbuf_tensor(f"{n}_{half}", list(ins[n].shape), R32, side="right")) for half in ("hi", "lo")]
                          for n in split}
                for name, (high, low) in halves.items():
                    const.update({name + "_hi": high, name + "_lo": low})
                split_weights(nc, [(raw1[n], *halves[n]) for n in split])
                to_split.close()
            if s == "attention":
                attention_inputs(nc, f"a{n}i", x, {n[3:]: ins[n] for n in by_stage if n.startswith("at_")}, const, qk_parts, v_rows)
                attention(nc, f"a{n}", x, weights(early, "at_"), const, qk_parts, v_rows)
            if s == "scan_mixer":
                scan_mixer(nc, f"a{n}", x, weights(const, "sc_"), const, ins["pick_bc"])
            if s == "ffn_gelu":
                ffn_gelu(nc, f"a{n}", x, weights(const, "f1_"), const)
        with nc.Block() as block:
            @block.sync
            def _(sp):
                o_tiles = out.rearrange("b (t p) d -> p (b t) d", p=P)
                for c in range(CHUNKS):
                    sp.dma_start(o_tiles[:, c * CT:(c + 1) * CT, :], x[:, c * CT:(c + 1) * CT, :]).then_inc(s_out, 16)
                sp.wait_ge(s_out, 16 * CHUNKS)


STAGES = ["ffn_moe", "attention", "ffn_moe", "ffn_gelu", "scan_mixer", "ffn_gelu"]


def lay_out(inputs):
    a = {k: np.asarray(v) for k, v in inputs.items()}
    bf = mybir.dt.np(BF16)
    rows = lambda m: np.ascontiguousarray(m.reshape(m.shape[0] // P, P, *m.shape[1:]).swapaxes(0, 1))
    g = {"x": a["L0_attn_x"]}
    g["f0_router"] = rows(np.concatenate([a["L0_ffn_gate_w"], a["L0_ffn_se_gate_w"]], 0).T)
    for mine, routed, shared in (("f0_gate", "L0_ffn_w_gate", "L0_ffn_sh_gate"), ("f0_up", "L0_ffn_w_up", "L0_ffn_sh_up")):
        units = np.concatenate([a[routed], a[shared].reshape(2, P, D)], 0)
        g[mine] = np.ascontiguousarray(units.reshape(UNITS0, P, KD, P).transpose(3, 0, 2, 1))
    down = np.concatenate([a["L0_ffn_w_down"].transpose(0, 2, 1), a["L0_ffn_sh_down"].T.reshape(2, P, D)], 0)
    g["f0_down"] = np.ascontiguousarray(down.transpose(1, 0, 2))
    for n in "qkv":
        g["at_w" + n] = rows(a["L0_attn_W" + n])
    wo = np.zeros((HG, GH, 2 * DH, D), np.float32)
    wo[:, :, 0:DH] = a["L0_attn_Wo"].reshape(HG, GH, DH, D)
    g["at_wo"] = np.ascontiguousarray(wo.reshape(HG, P, D).transpose(1, 0, 2))
    cols = lambda v: np.ascontiguousarray(v.reshape(KD, P, *v.shape[1:]).swapaxes(0, 1))
    g["sc_A_log"], g["sc_dt_b"], g["sc_D"] = cols(a["L1_attn_A_log"]), cols(a["L1_attn_dt_proj_b"]), cols(a["L1_attn_D"])
    g["sc_low"] = rows(a["L1_attn_x_proj_w"][0:RANK].T)
    g["sc_bc"] = rows(a["L1_attn_x_proj_w"][RANK:].T)
    g["sc_dt_w"] = np.ascontiguousarray(a["L1_attn_dt_proj_w"].T)
    one = lambda v: np.ascontiguousarray(np.broadcast_to(v[None], (P, v.shape[0])))
    g["f1_router"] = rows(a["L1_ffn_router_w"])
    g["f1_router_b"] = one(a["L1_ffn_router_b"])
    g["f1_down_w"] = rows(a["L1_ffn_down_w"])
    g["f1_down_b"] = a["L1_ffn_down_b"].reshape(P, 1)
    w1 = [a[f"L1_ffn_e{e}_w1"] for e in range(E1)] + [a["L1_ffn_shared_w1"]]
    g["f1_w1"] = np.ascontiguousarray(np.concatenate(w1, 1).reshape(P, HT1 + 1, P))
    b1 = [a[f"L1_ffn_e{e}_b1"] for e in range(E1)] + [a["L1_ffn_shared_b1"]]
    g["f1_b1"] = np.ascontiguousarray(np.concatenate(b1).reshape(HT1 + 1, P).T)
    w2 = [a[f"L1_ffn_e{e}_w2"] for e in range(E1)] + [a["L1_ffn_shared_w2"]]
    g["f1_w2"] = rows(np.concatenate(w2, 0))
    b2 = [a[f"L1_ffn_e{e}_b2"] for e in range(E1)] + [a["L1_ffn_shared_b2"]]
    g["f1_b2"] = np.ascontiguousarray(np.stack(b2, 1))
    g["f1_up_w"], g["f1_core_w"] = a["L1_ffn_up_w"], rows(a["L1_ffn_core_w"])
    g["f1_up_b"], g["f1_core_b"] = one(a["L1_ffn_up_b"]), one(a["L1_ffn_core_b"])
    g["ident"] = np.eye(P, dtype=np.float32)
    g["ident_bf"] = np.eye(P, dtype=bf)
    g["iota"] = np.tile(np.arange(E0, dtype=np.float32), (P, 1))
    g["minus_half"] = np.full((P, 8), -0.5, np.float32)
    g["pick_gate"] = np.ascontiguousarray(
        np.broadcast_to(np.tile(np.eye(G0), (3, 1))[:, :, None], (3 * G0, G0, P)).astype(bf))
    query, key = np.arange(P)[:, None], np.arange(P)[None]
    g["hide_right"] = np.where(key > query, np.float32(HIDDEN), np.float32(0)).astype(bf)
    g["hide_below"] = np.ascontiguousarray(g["hide_right"].T)
    g["onward"] = np.ascontiguousarray((key >= query).astype(np.float32).T)
    floor = np.zeros((P, GH, BT), np.float32)
    floor[P - 1, :, BT - 1] = -3e38
    g["floor"] = floor.reshape(P, GH * BT)
    pick = np.zeros((P, GH), np.float32)
    pick[np.arange(GH) * 2 * DH + DH, np.arange(GH)] = 1
    g["pick_den"] = pick
    g["one"] = np.ones((P, 1), np.float32)
    g["pick_bc"] = np.ascontiguousarray(
        np.broadcast_to(np.tile(np.eye(2 * STATES), (3, 1))[:, :, None], (6 * STATES, 2 * STATES, P)).astype(bf))
    g["pick_gate1"] = np.ascontiguousarray(
        np.broadcast_to(np.tile(np.eye(E1), (3, 1))[:, :, None], (3 * E1, E1, P)).astype(bf))
    g["cost"] = np.tile(np.float32(1e-7) * np.array([2 * P * h for h in HID1], np.float32), (P, 1))
    return g


def kernel(**inputs):
    import concourse.bacc as _bacc
    from concourse.bass_utils import run_bass_kernel_spmd as _run

    nc = _bacc.Bacc("TRN2", target_bir_lowering=False, num_devices=1)
    arrays, ins = {}, {}
    for name, v in lay_out(inputs).items():
        arrays[f"in_{name}"] = v
        ins[name] = nc.dram_tensor(f"in_{name}", v.shape, mybir.dt.from_np(v.dtype), kind="ExternalInput").ap()
    out = nc.dram_tensor("out_0", (B, T, D), F32, kind="ExternalOutput").ap()
    build(nc, ins, out, STAGES)
    return _run(nc, [arrays], core_ids=[0]).results[0]["out_0"]
```
